# Optimizing a Trainium2 kernel written in Bass

```python
import numpy as np
import jax
import jax.numpy as jnp

def _softmax(x, axis=-1):
    return jax.nn.softmax(x, axis=axis)

def _gelu(x):
    return jax.nn.gelu(x, approximate=True)

def _silu(x):
    return jax.nn.silu(x)

def _sigmoid(x):
    return jax.nn.sigmoid(x)

def _layernorm(x, axis=-1, eps=1e-05):
    m = jnp.mean(x, axis=axis, keepdims=True)
    v = jnp.var(x, axis=axis, keepdims=True)
    return (x - m) / jnp.sqrt(v + eps)

def _scatter_add(tgt, idx, src, axis=0):
    return tgt.at[idx].add(src)

def _segment_sum(src, seg, n):
    return jax.ops.segment_sum(src, seg, n)
kernel_name = 'mk_seq_postln_d1_jaxref_r4_9dc92a'

def setup_inputs(seed: int=0):
    np.random.seed(seed)
    _w = jnp.asarray

    def _L0_attn_setup():
        import jax, jax.numpy as jnp
        import numpy as np
        D_MODEL = 256
        D_STATE = 64
        EXPAND = 2
        D_INNER = D_MODEL * EXPAND
        DT_RANK = 32
        B, L = (4, 1024)
        key = jax.random.key(seed)
        ks = jax.random.split(key, 8)
        s = lambda fan_in: 1.0 / np.sqrt(fan_in)
        return {'x': jax.random.normal(ks[0], (B, L, D_MODEL), dtype=jnp.float32), 'W_in': jax.random.uniform(ks[1], (2 * D_INNER, D_MODEL), minval=-s(D_MODEL), maxval=s(D_MODEL)), 'conv_w': jax.random.uniform(ks[2], (D_INNER, 1, 4), minval=-s(4), maxval=s(4)), 'conv_b': jax.random.uniform(ks[3], (D_INNER,), minval=-s(4), maxval=s(4)), 'W_x': jax.random.uniform(ks[4], (DT_RANK + 2 * D_STATE, D_INNER), minval=-s(D_INNER), maxval=s(D_INNER)), 'W_dt': jax.random.uniform(ks[5], (D_INNER, DT_RANK), minval=-s(DT_RANK), maxval=s(DT_RANK)), 'b_dt': jax.random.uniform(ks[6], (D_INNER,), minval=-s(DT_RANK), maxval=s(DT_RANK)), 'W_out': jax.random.uniform(ks[7], (D_MODEL, D_INNER), minval=-s(D_INNER), maxval=s(D_INNER))}
    _L0_attn_in = _L0_attn_setup()

    def _L0_ffn_setup():
        import jax, jax.numpy as jnp
        import numpy as np
        E = 16
        K = 4
        NG = 4
        TG = 2
        SCALE = 2.5
        NORM_TOPK = True
        H = 256
        I = 128
        SH_I = I * 2
        B, S = (2, 512)
        key = jax.random.key(seed)
        ks = jax.random.split(key, 9)

        def w(k, shape, fan_in):
            return jax.random.normal(k, shape, jnp.float32) * (1.0 / np.sqrt(fan_in))
        return {'hidden_states': jax.random.normal(ks[0], (B, S, H), jnp.float32), 'gate_w': w(ks[1], (E, H), H), 'gate_bias': jnp.zeros((E,), jnp.float32), 'Wg': w(ks[2], (E, I, H), H), 'Wu': w(ks[3], (E, I, H), H), 'Wd': w(ks[4], (E, H, I), I), 'Ws_g': w(ks[5], (SH_I, H), H), 'Ws_u': w(ks[6], (SH_I, H), H), 'Ws_d': w(ks[7], (H, SH_I), SH_I)}
    _L0_ffn_in = _L0_ffn_setup()
    _d = {'L0_attn_x': _L0_attn_in['x'], 'L0_attn_W_in': _L0_attn_in['W_in'], 'L0_attn_conv_w': _L0_attn_in['conv_w'], 'L0_attn_conv_b': _L0_attn_in['conv_b'], 'L0_attn_W_x': _L0_attn_in['W_x'], 'L0_attn_W_dt': _L0_attn_in['W_dt'], 'L0_attn_b_dt': _L0_attn_in['b_dt'], 'L0_attn_W_out': _L0_attn_in['W_out'], 'L0_ffn_gate_w': _L0_ffn_in['gate_w'], 'L0_ffn_gate_bias': _L0_ffn_in['gate_bias'], 'L0_ffn_Wg': _L0_ffn_in['Wg'], 'L0_ffn_Wu': _L0_ffn_in['Wu'], 'L0_ffn_Wd': _L0_ffn_in['Wd'], 'L0_ffn_Ws_g': _L0_ffn_in['Ws_g'], 'L0_ffn_Ws_u': _L0_ffn_in['Ws_u'], 'L0_ffn_Ws_d': _L0_ffn_in['Ws_d']}
    _x0 = _d['L0_attn_x']
    _d['L0_attn_x'] = jax.random.normal(jax.random.fold_in(jax.random.key(seed), 1), (2, 2048, 256), dtype=_x0.dtype)
    del _x0
    return _d

def reference(L0_attn_x, L0_attn_W_in, L0_attn_conv_w, L0_attn_conv_b, L0_attn_W_x, L0_attn_W_dt, L0_attn_b_dt, L0_attn_W_out, L0_ffn_gate_w, L0_ffn_gate_bias, L0_ffn_Wg, L0_ffn_Wu, L0_ffn_Wd, L0_ffn_Ws_g, L0_ffn_Ws_u, L0_ffn_Ws_d):

    def _L0_attn_ref(x, W_in, conv_w, conv_b, W_x, W_dt, b_dt, W_out):
        import jax, jax.numpy as jnp
        import numpy as np
        D_MODEL = 256
        D_STATE = 64
        EXPAND = 2
        D_INNER = D_MODEL * EXPAND
        DT_RANK = 32
        B, L = (4, 1024)
        Bsz, Lseq, _ = x.shape
        d_inner = W_in.shape[0] // 2
        shortcut = x
        xz = jnp.einsum('bld,ed->ble', x, W_in)
        xs, z = (xz[..., :d_inner], xz[..., d_inner:])
        xc = jax.lax.conv_general_dilated(xs.transpose(0, 2, 1), conv_w, (1,), [(3, 0)], dimension_numbers=('NCH', 'OIH', 'NCH'), feature_group_count=d_inner)
        xc = jax.nn.silu(xc + conv_b[None, :, None]).transpose(0, 2, 1)
        xp = jnp.einsum('ble,fe->blf', xc, W_x)
        dt = xp[..., :DT_RANK]
        a = jax.nn.softplus(jnp.einsum('blr,er->ble', dt, W_dt) + b_dt)
        y = xc * a
        out = jnp.einsum('ble,de->bld', y * jax.nn.silu(z), W_out)
        return out + shortcut

    def _L0_ffn_ref(hidden_states, gate_w, gate_bias, Wg, Wu, Wd, Ws_g, Ws_u, Ws_d):
        import jax, jax.numpy as jnp
        import numpy as np
        E = 16
        K = 4
        NG = 4
        TG = 2
        SCALE = 2.5
        NORM_TOPK = True
        H = 256
        I = 128
        SH_I = I * 2
        B, S = (2, 512)
        x = hidden_states
        b, s, h = x.shape
        n = b * s
        xf = x.reshape(n, h)
        logits = xf @ gate_w.T
        scores = jax.nn.sigmoid(logits)
        sfc = scores + gate_bias
        epg = E // NG
        grp = sfc.reshape(n, NG, epg)
        g_scores = jax.lax.top_k(grp, 2)[0].sum(-1)
        _, gidx = jax.lax.top_k(g_scores, TG)
        gmask = jax.nn.one_hot(gidx, NG, dtype=sfc.dtype).sum(1)
        emask = jnp.repeat(gmask, epg, axis=1)
        masked = jnp.where(emask > 0, sfc, -jnp.inf)
        _, topk_idx = jax.lax.top_k(masked, K)
        topk_w = jnp.take_along_axis(scores, topk_idx, axis=1)
        if K > 1 and NORM_TOPK:
            topk_w = topk_w / (topk_w.sum(-1, keepdims=True) + 1e-20)
        topk_w = topk_w * SCALE
        cw = (jax.nn.one_hot(topk_idx, E, dtype=topk_w.dtype) * topk_w[..., None]).sum(1)
        hg = jnp.einsum('nh,eih->nei', xf, Wg)
        hu = jnp.einsum('nh,eih->nei', xf, Wu)
        act = jax.nn.silu(hg) * hu
        y = jnp.einsum('nei,ne,ehi->nh', act, cw, Wd)
        shared = jax.nn.silu(xf @ Ws_g.T) * (xf @ Ws_u.T) @ Ws_d.T
        y = y + shared
        return (x + y.reshape(b, s, h)).astype(hidden_states.dtype)
    x = L0_attn_x
    x = _layernorm(x + _L0_attn_ref(x, L0_attn_W_in, L0_attn_conv_w, L0_attn_conv_b, L0_attn_W_x, L0_attn_W_dt, L0_attn_b_dt, L0_attn_W_out), axis=-1)
    x = _layernorm(x + _L0_ffn_ref(x, L0_ffn_gate_w, L0_ffn_gate_bias, L0_ffn_Wg, L0_ffn_Wu, L0_ffn_Wd, L0_ffn_Ws_g, L0_ffn_Ws_u, L0_ffn_Ws_d), axis=-1)
    return x

_drawn_inputs = setup_inputs


def setup_inputs(seed=0):
    import zlib

    import numpy as np

    out = dict(_drawn_inputs(seed))
    spreads = {'L0_ffn_gate_bias': (0.0, 0.1)}
    factors = {'L0_attn_W_x': 6.592, 'L0_attn_W_dt': 6.322, 'L0_attn_b_dt': 5.03}
    for name, (base, spread) in spreads.items():
        noise = np.random.default_rng([zlib.crc32(name.encode()), seed]).standard_normal(out[name].shape)
        drawn = base * np.exp(spread * noise) if base else spread * noise
        out[name] = jnp.asarray(drawn.astype(out[name].dtype))
    for name, factor in factors.items():
        out[name] = (out[name] * factor).astype(out[name].dtype)
    return out
```

```python
import concourse.bass as bass
from concourse import mybir
from contextlib import ExitStack

P = 128
F32 = mybir.dt.float32
F32R = mybir.dt.float32r
BF16 = mybir.dt.bfloat16
I32 = mybir.dt.int32
ALU = mybir.AluOpType
ACT = mybir.ActivationFunctionType
AX_X = mybir.AxisListType.X

EPS = 1e-5
SCALE = 2.5
TOP = 4
GROUPS_KEPT = 2
LOWEST = 3e38
EXP_MAX = 2.0 ** 60


def mamba_moe(nc, x_tok, x_T, w_in_T, conv_w, conv_b, w_x_T, w_dt_T, b_dt, w_out_T,
              gate_w_T, gate_bias, wg_T, wu_T, wd_T, ws_g_T, ws_u_T, ws_d_T, out, seq_len):
    N, D = x_tok.shape
    DI = w_in_T.shape[1] // 2
    R = w_dt_T.shape[0]
    TAPS = conv_w.shape[2]
    E, _, I = wg_T.shape
    SH = ws_d_T.shape[0]
    T = 512
    NT = N // T
    SUB = T // P
    KD, KI, KS = D // P, DI // P, SH // P
    NG = 4
    EG = E // NG
    ROW = D + 2 * E
    CAP = N + P
    IDLE = E * CAP
    NTILES = -(-(N * TOP // P + E) // SUB) * SUB
    HALO = TAPS - 1

    x_buf = nc.dram_tensor("x_buf", (IDLE + P, ROW), F32).ap()
    y_buf = nc.dram_tensor("y_buf", (TOP * N, D), F32).ap()

    with ExitStack() as ctx:
        def sb(name, shape, dt=F32, scope=ctx):
            return scope.enter_context(nc.sbuf_tensor(name, shape, dt))

        def sem(name):
            return ctx.enter_context(nc.semaphore(name))

        psum = ctx.enter_context(nc.psum_tensor("psum", [P, 8, T], F32))

        res = sb("res", [P, N // P, D])
        ident = sb("ident", [P, P])
        counts = sb("counts", [P, E])
        pad_row = sb("pad_row", [P, ROW])
        TC = -(-NTILES // P)
        region = sb("region", [P, E])
        ntile_i = sb("ntile_i", [P, E], I32)
        ntile, row_step = sb("ntile", [P, E]), sb("row_step", [P, E])
        ends = [sb(f"ends{i}", [P, 8 + E]) for i in range(3)]
        tile_no = sb("tile_no", [P, TC])
        is_past, past_step = sb("is_past", [P, TC, E]), sb("past_step", [P, TC, E])
        tile_ef, tile_row = sb("tile_ef", [P, TC]), sb("tile_row", [P, TC])
        tile_e = sb("tile_e", [1, NTILES], I32)
        tile_at = sb("tile_at", [1, NTILES], I32)
        pad_at = sb("pad_at", [1, E], I32)

        p0 = ExitStack()
        raw_gu = sb("raw_gu", [P, E, KD, 2 * I], F32, p0)
        raw_d = sb("raw_d", [P, E, D], F32, p0)
        p1sb = lambda name, shape, dt=F32: sb(name, shape, dt, p0)
        win_hi, win_lo = (p1sb(n, [P, KD, 2 * DI], F32R) for n in ("win_hi", "win_lo"))
        wx = p1sb("wx", [P, KI, 2 * R])
        wdt_hi = p1sb("wdt_hi", [2 * R, DI], F32R)
        wdt_lo = p1sb("wdt_lo", [R, DI], F32R)
        wout = p1sb("wout", [P, KI, D])
        gw = p1sb("gw", [P, KD, E])
        gw_hi, gw_lo = (p1sb(n, [P, KD, E], F32R) for n in ("gw_hi", "gw_lo"))
        wsgu_hi, wsgu_lo = (p1sb(n, [P, KD, 2 * SH], F32R) for n in ("wsgu_hi", "wsgu_lo"))
        wsd = p1sb("wsd", [P, KS, D])
        cw_taps = p1sb("cw_taps", [P, KI, TAPS])
        cbias = p1sb("cbias", [P, KI])
        dtbias = p1sb("dtbias", [P, KI])
        gbias = p1sb("gbias", [P, E])
        keep = p1sb("keep", [P, NT])
        tri = p1sb("tri", [P, P], BF16)
        ones = p1sb("ones", [P, P], BF16)
        before = p1sb("before", [P, NG, NG])
        tok_row = p1sb("tok_row", [P, SUB])

        xT = p1sb("xT", [P, KD, T])
        x_hi, x_lo = (p1sb(n, [P, KD, T], F32R) for n in ("x_hi", "x_lo"))
        xtok = p1sb("xtok", [P, SUB, D])
        xs = p1sb("xs", [P, KI, HALO + T])
        xc = p1sb("xc", [P, KI, T])
        zs = p1sb("zs", [P, KI, T])
        m = p1sb("m", [P, KI, T])
        sp = p1sb("sp", [P, KI, T])
        dt = p1sb("dt", [2 * R, T], F32R)
        x1 = p1sb("x1", [P, SUB, D])
        x1T_hi, x1T_lo = (p1sb(n, [P, KD, T], F32R) for n in ("x1T_hi", "x1T_lo"))
        sg = p1sb("sg", [P, KS, T])
        sh = p1sb("sh", [P, KS, T])
        stats = p1sb("stats", [P, SUB, 6])
        mv = p1sb("mv", [P, SUB, 2])
        var = p1sb("var", [P, SUB])
        rstd = p1sb("rstd", [P, SUB])
        nt = p1sb("nt", [P, SUB])
        S3 = [P, SUB, E]
        score, sfc, picked = p1sb("score", S3), p1sb("sfc", S3), p1sb("picked", S3)
        above, sel, wsel, posn = p1sb("above", S3), p1sb("sel", S3), p1sb("wsel", S3), p1sb("posn", S3)
        sel16 = p1sb("sel16", S3, BF16)
        pmx, pmn = p1sb("pmx", [P, SUB, NG, 2]), p1sb("pmn", [P, SUB, NG, 2])
        g1, g2, g3, gsc = (p1sb(n, [P, SUB * NG]) for n in ("g1", "g2", "g3", "gsc"))
        cmp_a, cmp_b = p1sb("cmp_a", [P, SUB, NG, NG]), p1sb("cmp_b", [P, SUB, NG, NG])
        gkeep, gpen = p1sb("gkeep", [P, SUB * NG]), p1sb("gpen", [P, SUB * NG])
        top8, pos8 = p1sb("top8", [P, SUB, 8]), p1sb("pos8", [P, SUB, 8])
        nabove, wsum = p1sb("nabove", [P, SUB]), p1sb("wsum", [P, SUB])
        pre = [p1sb(f"pre{i}", [P, SUB, 8 + E]) for i in range(3)]

        row = p1sb("row", [P, SUB, ROW])
        row_id = p1sb("row_id", [P, SUB, TOP], I32)
        p0.close()

        p2 = ctx.enter_context(ExitStack())
        p2sb = lambda name, shape, dt=F32: sb(name, shape, dt, p2)
        RING = 4
        t_hi, t_lo = ([p2sb(f"{n}{i}", [P, KD, T], F32R) for i in range(2)] for n in ("t_hi", "t_lo"))
        g_act = p2sb("g_act", [P, SUB, I])
        e_act = p2sb("e_act", [P, SUB, I])
        a_hi, a_lo = p2sb("a_hi", [P, T], F32R), p2sb("a_lo", [P, T], F32R)
        in_raw = 4 * KD * T + 2 * SUB * I + 2 * T
        behind_raw = p2sb("behind_raw", [P, E * (KD * 2 * I + D) - in_raw])
        ew_gu_hi, ew_gu_lo = (p2sb(n, [P, E, KD, 2 * I], F32R) for n in ("ew_gu_hi", "ew_gu_lo"))
        ew_d_hi, ew_d_lo = (p2sb(n, [P, E, D], F32R) for n in ("ew_d_hi", "ew_d_lo"))
        y_out = [p2sb(f"y_out{i}", [P, SUB, D]) for i in range(2)]
        y_id = [p2sb(f"y_id{i}", [P, SUB], I32) for i in range(RING)]
        tiles_in = p2sb("tiles_in", [P, RING, SUB, ROW])
        p2.close()
        p3 = ctx.enter_context(ExitStack())
        YR = 2 * SUB
        y_in = [sb(f"y_in{i}", [P, TOP, D], F32, p3) for i in range(YR)]
        o_stats, o_nt = sb("o_stats", [P, SUB, 6], F32, p3), sb("o_nt", [P, SUB], F32, p3)
        o_mv = [sb(f"o_mv{i}", [P, SUB, 2], F32, p3) for i in range(2)]
        o_var = [sb(f"o_var{i}", [P, SUB], F32, p3) for i in range(2)]
        o_rstd = [sb(f"o_rstd{i}", [P, SUB], F32, p3) for i in range(2)]
        o_shift = [sb(f"o_shift{i}", [P, SUB], F32, p3) for i in range(2)]

        win_f = sp[:, :, :].rearrange("p a b -> p (a b)").rearrange("p (k n) -> p k n", k=KD)
        wsgu_f = sh[:, :, :]
        wdt_f = sg[0:2 * R, 0, :]

        names = """w_in_in w_x_in w_dt_in w_out_in gate_in w_sgu_in w_sd_in consts_in
            win_h win_l wdt_h wdt_l gw_h gw_l wsgu_h wsgu_l
            ones_ready keep_one keep_ready pre_zero id_zero id_ready tri_one tri_ready before_one before_ready const_ready
            xT_in xtok_in x_hi_done x_lo_done s1_mm s1_evac halo_done conv_step xc_done m_done
            wx_mm dt_hi dt_lo wdt_mm exp_done exp_clamped ln_done sp_done y_done
            wout_mm ln_in bn bn_mv var_done rstd_ln rstd_exp norm_step x1_done xt_mm x1T_h x1T_l
            gate_mm gate_exp route_step sel_done rank_mm routed row_x sent
            sgu_mm ssilu h_done sd_mm res_done
            raw_in table_step table_mm table_done pad_ready pads_out ew_hi ew_lo
            tile_in0 tile_in1 tile_in2 tile_in3 t_mm t_h t_l gu_mm g_silu e_mul at_mm a_h a_l y_mm
            y_half0 y_half1 y_id_done y_sent0 y_sent1
            y_in0 y_in1 y_in2 y_in3 y_in4 y_in5 y_in6 y_in7 y_paired
            y_used0 y_used1 y_used2 y_used3 y_used4 y_used5 y_used6 y_used7 y_summed
            o_bn o_agg o_var_done o_rstd_ln o_rstd_exp o_norm o_ready o_done stored""".split()
        s = {n: sem(n) for n in names}

        def at_least_alone(eng, name, n):
            if isinstance(n, int):
                return at_least(eng, name, n)
            n = eng.to_reg(n)
            eng.wait_ge(s["ones_ready"], 1)
            eng.wait_ge(s[name], n)

        def at_least(eng, name, n):
            if isinstance(n, int) and n <= 0:
                return
            eng.wait_ge(s[name], n)

        TABLE_STEPS = 16
        NQ = NTILES // SUB

        def quad(j, u):
            return RING * j + u, u % RING, j + u // RING, u % 2

        def table_values(eng, table, q, most):
            return nc.values_load_multi_w_load_instructions(
                table[0:1, bass.ds(SUB * q, SUB)], engines=(eng.engine,), min_val=0, max_val=most,
                skip_runtime_bounds_check_because="the table is clamped to these bounds")[1]

        def quads_left(j):
            return RING if isinstance(j, int) and j == NQ // RING - 1 else 2 * RING

        def is_first(j, u):
            return isinstance(j, int) and j == 0 and u == 0

        def each_quad(eng, iteration):
            def body(j):
                for u in range(RING):
                    iteration(j, u)
            body(0)
            with eng.Fori(1, NQ // RING - 1) as j:
                body(j)
            body(NQ // RING - 1)

        block = ctx.enter_context(nc.Block())
        taps = cw_taps

        @block.sync
        def _(sp_):
            sp_.dma_start(win_f, w_in_T.rearrange("(k p) n -> p k n", p=P)).then_inc(s["w_in_in"], 16)

            def load_x(t):
                at_least(sp_, "x_hi_done", t)
                at_least(sp_, "x_lo_done", t)
                sp_.dma_start(xT[:, :, :], x_T.rearrange("(k p) n -> p k n", p=P)[:, :, bass.ds(t * T, T)]) \
                   .then_inc(s["xT_in"], 16)

            def load_tok(t):
                at_least(sp_, "ln_in", 2 * t)
                sp_.dma_start(xtok[:, :, :], x_tok.rearrange("(n p) d -> p n d", p=P)[:, bass.ds(t * SUB, SUB), :]) \
                   .then_inc(s["xtok_in"], 16)

            load_x(0)
            sp_.dma_start(cw_taps[:, :, :], conv_w).then_inc(s["consts_in"], 16)
            sp_.dma_start(cbias[:, :], conv_b).then_inc(s["consts_in"], 16)
            sp_.dma_start(dtbias[:, :], b_dt).then_inc(s["consts_in"], 16)
            sp_.dma_start(gbias[:, :], gate_bias.to_broadcast([P, E])).then_inc(s["consts_in"], 16)
            for i in range(2):
                sp_.dma_start(wx[:, :, i * R:(i + 1) * R],
                              w_x_T.rearrange("(k p) n -> p k n", p=P)[:, :, 0:R]).then_inc(s["w_x_in"], 16)
                sp_.dma_start(wdt_f[i * R:(i + 1) * R, :], w_dt_T).then_inc(s["w_dt_in"], 16)
            sp_.dma_start(wout[:, :, :], w_out_T.rearrange("(k p) n -> p k n", p=P)).then_inc(s["w_out_in"], 16)
            load_tok(0)
            sp_.dma_start(gw[:, :, :], gate_w_T.rearrange("(k p) n -> p k n", p=P)).then_inc(s["gate_in"], 16)
            for i, w in enumerate((ws_g_T, ws_u_T)):
                sp_.dma_start(wsgu_f[:, :, i * SH:(i + 1) * SH],
                              w.rearrange("(k p) n -> p k n", p=P)).then_inc(s["w_sgu_in"], 16)
            sp_.dma_start(wsd[:, :, :], ws_d_T.rearrange("(k p) n -> p k n", p=P)).then_inc(s["w_sd_in"], 16)
            load_x(1)
            for e in range(E):
                for i, w in enumerate((wg_T, wu_T)):
                    sp_.dma_start(raw_gu[:, e, :, i * I:(i + 1) * I],
                                  w[e, :, :].rearrange("(k p) i -> p k i", p=P)).then_inc(s["raw_in"], 16)
                sp_.dma_start(raw_d[:, e, :], wd_T[e, :, :]).then_inc(s["raw_in"], 16)
            with sp_.Fori(1, NT - 1) as t:
                load_x(t + 1)
                load_tok(t)
            load_tok(NT - 1)

            at_least(sp_, "pad_ready", 1)
            sp_.dma_start(x_buf[IDLE:IDLE + P, :], pad_row[:, :]).then_inc(s["pads_out"], 16)
            at_least(sp_, "table_done", 3)
            for e in range(E):
                first = sp_.value_load(pad_at[0:1, e:e + 1], min_val=0, max_val=IDLE)
                sp_.dma_start(x_buf[bass.ds(first, P), :], pad_row[:, :]).then_inc(s["pads_out"], 16)
            at_least(sp_, "pads_out", 16 * (E + 1))
            at_least(sp_, "sent", 16 * SUB * TOP * NT)

            def load_tiles(j, u):
                q, slot, turn, _ = quad(j, u)
                at_least(sp_, "y_id_done", SUB * (q - RING + 1))
                for i, first in enumerate(table_values(sp_, tile_at, q, IDLE)):
                    sp_.dma_start(tiles_in[:, slot, i, :], x_buf[bass.ds(first, P), :]) \
                       .then_inc(s[f"tile_in{slot}"], 16)
            each_quad(sp_, load_tiles)

            for i in range(2):
                at_least(sp_, f"y_sent{i}", 16 * SUB * NQ // 2)

            def load_results(j):
                for u in range(YR):
                    at_least(sp_, f"y_used{u}", j)
                    sp_.dma_start(y_in[u][:, :, :], y_buf.rearrange("(k n p) d -> p n k d", k=TOP, p=P)
                                  [:, bass.ds(YR * j + u, 1), :, :].squeeze(1)).then_inc(s[f"y_in{u}"], 16)

            load_results(0)
            with sp_.Fori(1, N // P // YR) as j:
                load_results(j)
            at_least(sp_, "stored", 16 * N // P // SUB)

        @block.gpsimd
        def _(pool):
            nc.gpsimd.memset(ident[:, :], 0.0).then_inc(s["id_zero"], 1)
            pool.wait_ge(s["id_zero"], 1)
            nc.gpsimd.affine_select(out=ident[:, :], in_=ident[:, :], compare_op=ALU.not_equal, fill=1.0,
                                    base=0, pattern=[[-1, P]], channel_multiplier=1).then_inc(s["id_ready"], 1)
            nc.gpsimd.memset(tri[:, :], 1.0).then_inc(s["tri_one"], 1)
            pool.wait_ge(s["tri_one"], 1)
            nc.gpsimd.affine_select(out=tri[:, :], in_=tri[:, :], compare_op=ALU.is_gt, fill=0.0,
                                    base=0, pattern=[[1, P]], channel_multiplier=-1).then_inc(s["tri_ready"], 1)
            nc.gpsimd.memset(ones[:, :], 1.0).then_inc(s["ones_ready"], 1)
            nc.gpsimd.memset(before[:, :, :], 1.0).then_inc(s["before_one"], 1)
            pool.wait_ge(s["before_one"], 1)
            nc.gpsimd.affine_select(out=before[:, :, :], in_=before[:, :, :], compare_op=ALU.is_gt, fill=0.0,
                                    base=0, pattern=[[1, NG], [-1, NG]], channel_multiplier=0) \
                     .then_inc(s["before_ready"], 1)
            nc.gpsimd.iota(tok_row[:, :], pattern=[[P, SUB]], base=-N, channel_multiplier=1,
                           allow_small_or_imprecise_dtypes=True).then_inc(s["const_ready"], 1)
            for v in (counts, region):
                nc.gpsimd.iota(v[:, :], pattern=[[CAP, E]], base=0, channel_multiplier=0,
                               allow_small_or_imprecise_dtypes=True).then_inc(s["const_ready"], 1)
            nc.gpsimd.iota(tile_no[:, :], pattern=[[P, TC]], base=0, channel_multiplier=1,
                           allow_small_or_imprecise_dtypes=True).then_inc(s["const_ready"], 1)
            nc.gpsimd.memset(pad_row[:, 0:D + E], 0.0)
            nc.gpsimd.memset(pad_row[:, D + E:ROW], float(TOP * N)).then_inc(s["pad_ready"], 1)

            def gate_product(t):
                for c in range(KI):
                    at_least(pool, "xc_done", KI * t + c + 1)
                    at_least(pool, "s1_evac", 2 * KI * t + KI + c + 1)
                    if c == 0:
                        at_least(pool, "wout_mm", 2 * t)
                    nc.gpsimd.tensor_tensor(m[:, c, :], xc[:, c, :], zs[:, c, :], ALU.mult).then_inc(s["m_done"], 1)

            def clamp(t):
                for c in range(KI):
                    at_least_alone(pool, "exp_done", KI * t + c + 1)
                    nc.gpsimd.tensor_scalar(sp[:, c, :], sp[:, c, :], EXP_MAX, None, ALU.min) \
                             .then_inc(s["exp_clamped"], 1)

            def send(t):
                at_least_alone(pool, "routed", t + 1)
                at_least_alone(pool, "row_x", t + 1)
                for b in range(SUB):
                    for k in range(TOP):
                        nc.gpsimd.indirect_dma_start(
                            out=x_buf, out_offset=bass.IndirectOffsetOnAxis(ap=row_id[:, b, k:k + 1], axis=0),
                            in_=row[:, b, :], in_offset=None).then_inc(s["sent"], 16)

            gate_product(0)
            clamp(0)
            gate_product(1)
            with pool.Fori(1, NT - 1) as t:
                clamp(t)
                send(t - 1)
                gate_product(t + 1)
            clamp(NT - 1)
            send(NT - 2)
            send(NT - 1)

            def send_results(j, u):
                q, slot, turn, par = quad(j, u)
                at_least_alone(pool, "y_half0", q + 1)
                at_least_alone(pool, "y_half1", q + 1)
                at_least_alone(pool, "y_id_done", SUB * (q + 1))
                for i in range(SUB):
                    nc.gpsimd.indirect_dma_start(
                        out=y_buf, out_offset=bass.IndirectOffsetOnAxis(ap=y_id[slot][:, i:i + 1], axis=0),
                        in_=y_out[par][:, i, :], in_offset=None, bounds_check=TOP * N - 1, oob_is_err=False) \
                      .then_inc(s[f"y_sent{par}"], 16)
            each_quad(pool, send_results)

            with pool.Fori(0, N // P // YR) as j:
                for u in range(YR):
                    at_least(pool, f"y_in{u}", 16 * (j + 1))
                    nc.gpsimd.tensor_tensor(y_in[u][:, 0:2, :], y_in[u][:, 0:2, :], y_in[u][:, 2:4, :], ALU.add) \
                             .then_inc(s["y_paired"], 1)

        def split_mm(pe, o, w_hi, w_lo, v_hi, v_lo, start, stop):
            pe.matmul(o, w_hi, v_hi, start=start, stop=False)
            pe.matmul(o, w_hi, v_lo, start=False, stop=False)
            return pe.matmul(o, w_lo, v_hi, start=False, stop=stop)

        @block.tensor
        def _(pe):
            def in_proj(t, chunks):
                for j in chunks:
                    if j == 0:
                        at_least(pe, "x_hi_done", t + 1)
                        at_least(pe, "x_lo_done", t + 1)
                    at_least(pe, "s1_evac", 2 * KI * t + j - 1)
                    for k in range(KD):
                        mm = split_mm(pe, psum[:, j % 2, :], win_hi[:, k, j * P:(j + 1) * P],
                                      win_lo[:, k, j * P:(j + 1) * P], x_hi[:, k, :], x_lo[:, k, :],
                                      k == 0, k == KD - 1)
                    mm.then_inc(s["s1_mm"], 1)

            def dt_in(t):
                at_least(pe, "dt_lo", t)
                for c in range(KI):
                    at_least(pe, "xc_done", KI * t + c + 1)
                    mm = pe.matmul(psum[0:2 * R, 2, :], wx[:, c, :], xc[:, c, :], start=c == 0, stop=c == KI - 1)
                mm.then_inc(s["wx_mm"], 1)

            def dt_out(t, chunks):
                at_least(pe, "dt_lo", t + 1)
                at_least(pe, "x1T_h", t)
                at_least(pe, "x1T_l", t)
                for c in chunks:
                    if c >= 2:
                        at_least(pe, "sp_done", KI * t + c - 1)
                    pe.matmul(psum[:, 4 + c % 2, :], wdt_hi[:, c * P:(c + 1) * P], dt[:, :], start=True, stop=False)
                    pe.matmul(psum[:, 4 + c % 2, :], wdt_lo[:, c * P:(c + 1) * P], dt[0:R, :],
                              start=False, stop=True).then_inc(s["wdt_mm"], 1)

            def out_proj(t):
                at_least(pe, "y_done", KI * (t + 1))
                for b in range(SUB):
                    o = psum[:, 4 + b // 2, (b % 2) * D:(b % 2 + 1) * D]
                    for c in range(KI):
                        mm = pe.matmul(o, m[:, c, b * P:(b + 1) * P], wout[:, c, :], start=c == 0, stop=c == KI - 1)
                    if b % 2:
                        mm.then_inc(s["wout_mm"], 1)

            def transposes(t):
                for b in range(SUB):
                    at_least(pe, "x1_done", SUB * t + b + 1)
                    for k in range(KD):
                        mm = pe.transpose(psum[:, 4 + k, b * P:(b + 1) * P], x1[:, b, k * P:(k + 1) * P], ident[:, :])
                mm.then_inc(s["xt_mm"], 1)

            def gate(t):
                at_least(pe, "x1T_h", t + 1)
                at_least(pe, "x1T_l", t + 1)
                at_least(pe, "routed", t)
                for b in range(SUB):
                    r = slice(b * P, (b + 1) * P)
                    for k in range(KD):
                        o = psum[:, 3, b * E:(b + 1) * E]
                        pe.matmul(o, x1T_hi[:, k, r], gw_hi[:, k, :], start=k == 0, stop=False)
                        pe.matmul(o, x1T_hi[:, k, r], gw_lo[:, k, :], start=False, stop=False)
                        mm = pe.matmul(o, x1T_lo[:, k, r], gw_hi[:, k, :], start=False, stop=k == KD - 1)
                mm.then_inc(s["gate_mm"], 1)

            def shared_up(t):
                for i in range(KS):
                    at_least(pe, "res_done", 2 * t)
                    at_least(pe, "h_done", KS * t + i)
                    for j in range(2):
                        c = slice(j * SH + i * P, j * SH + (i + 1) * P)
                        for k in range(KD):
                            mm = split_mm(pe, psum[:, 6 + j, :], wsgu_hi[:, k, c], wsgu_lo[:, k, c],
                                          x1T_hi[:, k, :], x1T_lo[:, k, :], k == 0, k == KD - 1)
                    mm.then_inc(s["sgu_mm"], 1)

            def ranks(t):
                at_least(pe, "sel_done", t + 1)
                for b in range(SUB):
                    o = psum[:, 3, (SUB + b) * E:(SUB + b + 1) * E]
                    pe.matmul(o, tri[:, :], sel16[:, b, :], start=True, stop=b == 0)
                    for q in range(b):
                        pe.matmul(o, ones[:, :], sel16[:, q, :], start=False, stop=q == b - 1)
                for b in range(SUB):
                    mm = pe.matmul(psum[:, 3, 2 * SUB * E:(2 * SUB + 1) * E], ones[:, :], sel16[:, b, :],
                                   start=b == 0, stop=b == SUB - 1)
                mm.then_inc(s["rank_mm"], 1)

            def shared_down(t):
                at_least(pe, "h_done", KS * (t + 1))
                for b in range(SUB):
                    o = psum[:, 6 + b // 2, (b % 2) * D:(b % 2 + 1) * D]
                    for c in range(KS):
                        mm = pe.matmul(o, sh[:, c, b * P:(b + 1) * P], wsd[:, c, :], start=c == 0, stop=c == KS - 1)
                    if b % 2:
                        mm.then_inc(s["sd_mm"], 1)

            def tile(t, first=False, last=False):
                dt_out(t, range(0, 2))
                if not last:
                    in_proj(t + 1, range(0, KI))
                dt_out(t, range(2, KI))
                if not last:
                    in_proj(t + 1, range(KI, 2 * KI))
                if not first:
                    ranks(t - 1)
                    shared_up(t - 1)
                    shared_down(t - 1)
                out_proj(t)
                if not last:
                    dt_in(t + 1)
                transposes(t)
                gate(t)

            pe.wait_ge(s["win_h"], 1)
            pe.wait_ge(s["win_l"], 1)
            in_proj(0, range(2 * KI))
            pe.wait_ge(s["w_x_in"], 32)
            dt_in(0)
            pe.wait_ge(s["wdt_h"], 1)
            pe.wait_ge(s["wdt_l"], 1)
            pe.wait_ge(s["w_out_in"], 16)
            pe.wait_ge(s["id_ready"], 1)
            pe.wait_ge(s["gw_h"], 1)
            pe.wait_ge(s["gw_l"], 1)
            tile(0, first=True)
            pe.wait_ge(s["tri_ready"], 1)
            pe.wait_ge(s["ones_ready"], 1)
            pe.wait_ge(s["wsgu_h"], 1)
            pe.wait_ge(s["wsgu_l"], 1)
            pe.wait_ge(s["w_sd_in"], 16)
            tile(1)
            with pe.Fori(2, NT - 1) as t:
                tile(t)
            tile(NT - 1, last=True)
            ranks(NT - 1)
            shared_up(NT - 1)
            at_least(pe, "table_step", TABLE_STEPS)
            for i, v in enumerate((tile_ef, tile_row)):
                for c in range(TC):
                    n = min(P, NTILES - c * P)
                    mm = pe.matmul(psum[0:1, 3, i * NTILES + c * P:i * NTILES + c * P + n], v[:, c:c + 1],
                                   ident[:, 0:n], start=True, stop=True)
            mm.then_inc(s["table_mm"], 1)
            shared_down(NT - 1)

            def tile_experts(q):
                return table_values(pe, tile_e, q, E - 1)

            def turn_x(j, u):
                q, slot, turn, par = quad(j, u)
                at_least(pe, f"tile_in{slot}", 16 * SUB * (turn + 1))
                for k in range(KD):
                    at_least(pe, "t_l", KD * (q - 1) + k + 1)
                    for i in range(SUB):
                        mm = pe.transpose(psum[:, 2 + k, i * P:(i + 1) * P],
                                          tiles_in[:, slot, i, k * P:(k + 1) * P], ident[:, :])
                    mm.then_inc(s["t_mm"], 1)

            def gate_up(j, u, experts):
                q, slot, turn, par = quad(j, u)
                at_least(pe, "t_l", KD * (q + 1))
                at_least(pe, "e_mul", SUB * q)
                for i, e in enumerate(experts):
                    o = psum[:, i // 2, (i % 2) * 2 * I:(i % 2 + 1) * 2 * I]
                    r = slice(i * P, (i + 1) * P)
                    for k in range(KD):
                        w_hi, w_lo = (w[:, bass.ds(e, 1), k, :].squeeze(1) for w in (ew_gu_hi, ew_gu_lo))
                        pe.matmul(o, t_hi[par][:, k, r], w_hi, start=k == 0, stop=False)
                        pe.matmul(o, t_hi[par][:, k, r], w_lo, start=False, stop=False)
                        mm = pe.matmul(o, t_lo[par][:, k, r], w_hi, start=False, stop=k == KD - 1)
                mm.then_inc(s["gu_mm"], 1)

            def turn_act(j, u):
                q, slot, turn, par = quad(j, u)
                at_least(pe, "e_mul", SUB * (q + 1))
                at_least(pe, "a_l", q)
                for i in range(SUB):
                    mm = pe.transpose(psum[:, 4, i * P:(i + 1) * P], e_act[:, i, :], ident[:, :])
                mm.then_inc(s["at_mm"], 1)

            def down(j, u, experts):
                q, slot, turn, par = quad(j, u)
                at_least(pe, "a_l", q + 1)
                at_least(pe, "y_half0", q)
                at_least(pe, "y_half1", q)
                for i, e in enumerate(experts):
                    o = psum[:, 6 + i // 2, (i % 2) * D:(i % 2 + 1) * D]
                    r = slice(i * P, (i + 1) * P)
                    w_hi, w_lo = (w[:, bass.ds(e, 1), :].squeeze(1) for w in (ew_d_hi, ew_d_lo))
                    pe.matmul(o, a_hi[:, r], w_hi, start=True, stop=False)
                    pe.matmul(o, a_hi[:, r], w_lo, start=False, stop=False)
                    mm = pe.matmul(o, a_lo[:, r], w_hi, start=False, stop=True)
                    if i % 2:
                        mm.then_inc(s["y_mm"], 1)

            def iteration(j, u):
                q, left = RING * j + u, quads_left(j)
                if u + 2 < left:
                    turn_x(j, u + 2)
                if not is_first(j, u):
                    down(j, u - 1, tile_experts(q - 1))
                if u + 1 < left:
                    experts = tile_experts(q + 1)
                turn_act(j, u)
                if u + 1 < left:
                    gate_up(j, u + 1, experts)

            at_least(pe, "table_done", 3)
            at_least(pe, "res_done", 2 * NT)
            turn_x(0, 0)
            turn_x(0, 1)
            at_least(pe, "ew_lo", 3)
            gate_up(0, 0, tile_experts(0))
            each_quad(pe, iteration)
            down(NQ // RING - 1, RING - 1, tile_experts(NQ - 1))

        @block.scalar
        def _(act):
            A = nc.scalar.activation

            def split_x(t):
                at_least(act, "xT_in", 16 * (t + 1))
                at_least(act, "s1_mm", 2 * KI * t)
                A(x_hi[:, :, :], xT[:, :, :], ACT.Copy).then_inc(s["x_hi_done"], 1)

            def conv_in(t, chunks):
                for c in chunks:
                    at_least(act, "s1_mm", 2 * KI * t + c + 1)
                    at_least(act, "halo_done", t + 1)
                    at_least(act, "m_done", KI * t)
                    at_least(act, "wx_mm", t)
                    A(xs[:, c, HALO:HALO + T], psum[:, c % 2, :], ACT.Copy)
                    A(xc[:, c, :], psum[:, c % 2, :], ACT.Identity, bias=cbias[:, c:c + 1],
                      scale=taps[:, c, HALO:HALO + 1]).then_inc(s["s1_evac"], 1)

            def silu_z(t):
                for c in range(KI):
                    at_least(act, "s1_mm", 2 * KI * t + KI + c + 1)
                    at_least(act, "m_done", KI * t)
                    A(zs[:, c, :], psum[:, c % 2, :], ACT.Silu).then_inc(s["s1_evac"], 1)

            def silu_xc(t):
                for c in range(KI):
                    at_least(act, "conv_step", KI * HALO * t + HALO * (c + 1))
                    A(xc[:, c, :], xc[:, c, :], ACT.Silu).then_inc(s["xc_done"], 1)

            def dt_high(t):
                at_least(act, "wx_mm", t + 1)
                at_least(act, "wdt_mm", KI * t)
                A(dt[:, :], psum[0:2 * R, 2, :], ACT.Copy).then_inc(s["dt_hi"], 1)

            def exps(t, chunks):
                for c in chunks:
                    at_least(act, "wdt_mm", KI * t + c + 1)
                    at_least(act, "y_done", KI * t)
                    A(sp[:, c, :], psum[:, 4 + c % 2, :], ACT.Exp, bias=dtbias[:, c:c + 1]).then_inc(s["exp_done"], 1)

            def logs(t, chunks):
                for c in chunks:
                    at_least(act, "exp_clamped", KI * t + c + 1)
                    A(sp[:, c, :], sp[:, c, :], ACT.Ln, bias=1.0).then_inc(s["ln_done"], 1)

            def rstd_guess(t):
                at_least(act, "var_done", t + 1)
                A(rstd[:, :], var[:, :], ACT.Ln).then_inc(s["rstd_ln"], 1)
                act.wait_ge(s["rstd_ln"], t + 1)
                A(rstd[:, :], rstd[:, :], ACT.Exp, scale=-0.5).then_inc(s["rstd_exp"], 1)

            def x1T_high(t):
                at_least(act, "xt_mm", t + 1)
                at_least(act, "sgu_mm", KS * t)
                A(x1T_hi[:, :, :], psum[:, 4:4 + KD, :], ACT.Copy).then_inc(s["x1T_h"], 1)

            def gate_exp(t):
                at_least(act, "gate_mm", t + 1)
                A(score[:, :, :], psum[:, 3, 0:SUB * E].rearrange("p (b e) -> p b e", e=E), ACT.Exp,
                  scale=-1.0).then_inc(s["gate_exp"], 1)

            def shared_silu(t):
                for i in range(KS):
                    at_least(act, "sgu_mm", KS * t + i + 1)
                    A(sg[:, i, :], psum[:, 6, :], ACT.Silu).then_inc(s["ssilu"], 1)

            def copy_row(t):
                at_least(act, "x1_done", SUB * (t + 1))
                at_least(act, "sent", 16 * SUB * TOP * t)
                A(row[:, :, 0:D], x1[:, :, :], ACT.Copy).then_inc(s["row_x"], 1)

            def tile(t, first=False, last=False, more=True):
                nc.scalar.preload_act_table_set("natural_log_exp_and_others")
                exps(t, range(0, 2))
                if not last:
                    conv_in(t + 1, range(0, 2))
                logs(t, range(0, 2))
                if not last:
                    conv_in(t + 1, range(2, KI))
                exps(t, range(2, KI))
                logs(t, range(2, KI))
                if not last:
                    silu_z(t + 1)
                    silu_xc(t + 1)
                if not first:
                    shared_silu(t - 1)
                    copy_row(t - 1)
                if more:
                    split_x(t + 2)
                nc.scalar.preload_act_table_set("natural_log_exp_and_others")
                if not last:
                    dt_high(t + 1)
                rstd_guess(t)
                x1T_high(t)
                gate_exp(t)

            act.wait_ge(s["w_in_in"], 16)
            A(win_hi[:, :, :], win_f, ACT.Copy).then_inc(s["win_h"], 1)
            split_x(0)
            act.wait_ge(s["consts_in"], 64)
            conv_in(0, range(KI))
            silu_z(0)
            silu_xc(0)
            act.wait_ge(s["w_dt_in"], 32)
            A(wdt_hi[:, :], wdt_f, ACT.Copy).then_inc(s["wdt_h"], 1)
            dt_high(0)
            act.wait_ge(s["gate_in"], 16)
            A(gw_hi[:, :, :], gw[:, :, :], ACT.Copy).then_inc(s["gw_h"], 1)
            act.wait_ge(s["w_sgu_in"], 32)
            A(wsgu_hi[:, :, :], wsgu_f, ACT.Copy).then_inc(s["wsgu_h"], 1)
            act.wait_ge(s["win_l"], 1)
            act.wait_ge(s["wdt_l"], 1)
            split_x(1)
            tile(0, first=True)
            tile(1)
            with act.Fori(2, NT - 2) as t:
                tile(t)
            tile(NT - 2, more=False)
            tile(NT - 1, last=True, more=False)
            shared_silu(NT - 1)
            copy_row(NT - 1)

            at_least(act, "raw_in", 16 * 3 * E)
            at_least(act, "res_done", 2 * NT)
            at_least(act, "m_done", KI * NT)
            for h in range(2):
                r = slice(h * E // 2, (h + 1) * E // 2)
                A(ew_gu_hi[:, r, :, :], raw_gu[:, r, :, :], ACT.Copy).then_inc(s["ew_hi"], 1)
            A(ew_d_hi[:, :, :], raw_d[:, :, :], ACT.Copy).then_inc(s["ew_hi"], 1)

            def x_high(j, u, k):
                q, slot, turn, par = quad(j, u)
                at_least(act, "t_mm", KD * q + k + 1)
                at_least(act, "gu_mm", q - 1)
                A(t_hi[par][:, k, :], psum[:, 2 + k, :], ACT.Copy).then_inc(s["t_h"], 1)

            def gate_silu(j, u):
                q, slot, turn, par = quad(j, u)
                at_least(act, "gu_mm", q + 1)
                at_least(act, "e_mul", SUB * q)
                A(g_act[:, :, :], psum[:, 0:2, :].rearrange("p a (b i) -> p (a b) i", i=2 * I)[:, :, 0:I],
                  ACT.Silu).then_inc(s["g_silu"], 1)

            def act_high(j, u):
                q, slot, turn, par = quad(j, u)
                at_least(act, "at_mm", q + 1)
                at_least(act, "y_mm", 2 * q)
                A(a_hi[:, :], psum[:, 4, :], ACT.Copy).then_inc(s["a_h"], 1)

            def result(j, u):
                q, slot, turn, par = quad(j, u)
                at_least(act, "y_mm", 2 * q + 1)
                at_least(act, f"y_sent{par}", 16 * SUB * ((RING // 2) * j + u // 2))
                A(y_out[par][:, 0:2, :], psum[:, 6, :].rearrange("p (b d) -> p b d", d=D), ACT.Copy) \
                    .then_inc(s["y_half0"], 1)

            def iteration(j, u):
                gate_silu(j, u)
                if u + 2 < quads_left(j):
                    for k in range(KD):
                        x_high(j, u + 2, k)
                if not is_first(j, u):
                    result(j, u - 1)
                act_high(j, u)

            at_least(act, "ew_lo", 3)
            for u in range(2):
                for k in range(KD):
                    x_high(0, u, k)
            each_quad(act, iteration)
            result(NQ // RING - 1, RING - 1)

            nc.scalar.preload_act_table_set("natural_log_exp_and_others")

            def out_guess(j, h):
                g = 2 * j + h
                at_least(act, "o_var_done", g + 1)
                A(o_rstd[h][:, :], o_var[h][:, :], ACT.Ln).then_inc(s["o_rstd_ln"], 1)
                act.wait_ge(s["o_rstd_ln"], g + 1)
                A(o_rstd[h][:, :], o_rstd[h][:, :], ACT.Exp, scale=-0.5).then_inc(s["o_rstd_exp"], 1)

            def out_norm(j, h):
                at_least(act, "o_ready", 2 * j + h + 1)
                for i in range(SUB):
                    x2 = res[:, bass.ds(SUB * (2 * j + h) + i, 1), :].squeeze(1)
                    A(x2, x2, ACT.Identity, bias=o_shift[h][:, i:i + 1], scale=o_rstd[h][:, i:i + 1]) \
                        .then_inc(s["o_done"], 1)
                at_least(act, "o_done", SUB * (2 * j + h + 1))
                r = bass.ds(SUB * (2 * j + h), SUB)
                act.dma_start(out.rearrange("(n p) d -> p n d", p=P)[:, r, :], res[:, r, :]).then_inc(s["stored"], 16)

            out_guess(0, 0)
            with act.Fori(0, N // P // YR - 1) as j:
                out_norm(j, 0)
                out_guess(j, 1)
                out_norm(j, 1)
                out_guess(j + 1, 0)
            j = N // P // YR - 1
            out_norm(j, 0)
            out_guess(j, 1)
            out_norm(j, 1)

        @block.vector
        def _(dve):
            V = nc.vector

            def f32(ap):
                return ap.bitcast(F32)

            def split_x(t):
                at_least(dve, "x_hi_done", t + 1)
                V.tensor_tensor(x_lo[:, :, :], xT[:, :, :], f32(x_hi[:, :, :]), ALU.subtract).then_inc(s["x_lo_done"], 1)

            def halo(t):
                at_least(dve, "conv_step", KI * HALO * t)
                at_least(dve, "s1_evac", 2 * KI * (t - 1) + KI)
                V.tensor_scalar(xs[:, :, 0:HALO], xs[:, :, T:T + HALO], keep[:, bass.ds(t, 1)], None, ALU.mult) \
                 .then_inc(s["halo_done"], 1)

            def conv(t, chunks):
                for c in chunks:
                    for k in range(HALO):
                        n = KI * HALO * t + HALO * c + k
                        if k == 0:
                            at_least(dve, "s1_evac", 2 * KI * t + c + 1)
                            at_least(dve, "halo_done", t + 1)
                        else:
                            at_least(dve, "conv_step", n)
                        V.scalar_tensor_tensor(xc[:, c, :], xs[:, c, k:k + T], taps[:, c, k:k + 1], xc[:, c, :],
                                               ALU.mult, ALU.add).then_inc(s["conv_step"], 1)

            def dt_low(t):
                at_least(dve, "dt_hi", t + 1)
                V.tensor_tensor(dt[R:2 * R, :], psum[R:2 * R, 2, :], f32(dt[R:2 * R, :]), ALU.subtract) \
                 .then_inc(s["dt_lo"], 1)

            def softplus(t, chunks):
                for c in chunks:
                    at_least(dve, "ln_done", KI * t + c + 1)
                    V.scalar_tensor_tensor(sp[:, c, :], psum[:, 4 + c % 2, :], dtbias[:, c:c + 1], sp[:, c, :],
                                           ALU.add, ALU.max).then_inc(s["sp_done"], 1)
                for c in chunks:
                    at_least(dve, "sp_done", KI * t + c + 1)
                    at_least(dve, "m_done", KI * t + c + 1)
                    V.tensor_tensor(m[:, c, :], m[:, c, :], sp[:, c, :], ALU.mult).then_inc(s["y_done"], 1)

            def layer_norm(t):
                at_least(dve, "xtok_in", 16 * (t + 1))
                at_least(dve, "row_x", t)
                at_least(dve, "res_done", 2 * t)
                for h in range(2):
                    at_least(dve, "wout_mm", 2 * t + h + 1)
                    V.scalar_tensor_tensor(x1[:, 2 * h:2 * h + 2, :], xtok[:, 2 * h:2 * h + 2, :], 2.0,
                                           psum[:, 4 + h, :].rearrange("p (b d) -> p b d", d=D),
                                           ALU.mult, ALU.add).then_inc(s["ln_in"], 1)
                for b in range(SUB):
                    at_least(dve, "ln_in", 2 * t + b // 2 + 1)
                    V.bn_stats(stats[:, b, :], x1[:, b, :]).then_inc(s["bn"], 1)
                for b in range(SUB):
                    at_least_alone(dve, "bn", SUB * t + b + 1)
                    V.bn_aggr(mv[:, b, :], stats[:, b, :]).then_inc(s["bn_mv"], 1)
                dve.wait_ge(s["bn_mv"], SUB * (t + 1))
                V.tensor_scalar(var[:, :], mv[:, :, 1], EPS, None, ALU.add).then_inc(s["var_done"], 1)
                dve.wait_ge(s["rstd_exp"], t + 1)
                V.tensor_tensor(nt[:, :], rstd[:, :], rstd[:, :], ALU.mult).then_inc(s["norm_step"], 1)
                dve.wait_ge(s["norm_step"], 4 * t + 1)
                V.tensor_tensor(nt[:, :], nt[:, :], var[:, :], ALU.mult).then_inc(s["norm_step"], 1)
                dve.wait_ge(s["norm_step"], 4 * t + 2)
                V.tensor_scalar(nt[:, :], nt[:, :], -0.5, 1.5, ALU.mult, ALU.add).then_inc(s["norm_step"], 1)
                dve.wait_ge(s["norm_step"], 4 * t + 3)
                V.tensor_tensor(rstd[:, :], rstd[:, :], nt[:, :], ALU.mult).then_inc(s["norm_step"], 1)
                dve.wait_ge(s["norm_step"], 4 * t + 4)
                for b in range(SUB):
                    V.tensor_scalar(x1[:, b, :], x1[:, b, :], mv[:, b, 0:1], rstd[:, b:b + 1],
                                    ALU.subtract, ALU.mult).then_inc(s["x1_done"], 1)

            def x1T_low(t):
                at_least(dve, "x1T_h", t + 1)
                V.tensor_tensor(x1T_lo[:, :, :], psum[:, 4:4 + KD, :], f32(x1T_hi[:, :, :]), ALU.subtract) \
                 .then_inc(s["x1T_l"], 1)

            def shared_act(t):
                for i in range(KS):
                    at_least(dve, "ssilu", KS * t + i + 1)
                    at_least(dve, "sd_mm", 2 * t)
                    V.tensor_tensor(sh[:, i, :], sg[:, i, :], psum[:, 7, :], ALU.mult).then_inc(s["h_done"], 1)

            def residual(t):
                for h in range(2):
                    at_least(dve, "sd_mm", 2 * t + h + 1)
                    V.scalar_tensor_tensor(res[:, bass.ds(t * SUB + 2 * h, 2), :], x1[:, 2 * h:2 * h + 2, :], 2.0,
                                           psum[:, 6 + h, :].rearrange("p (b d) -> p b d", d=D), ALU.mult, ALU.add) \
                     .then_inc(s["res_done"], 1)

            done = [0]
            STEPS = 51

            def step(ins, t, wait=True, alone=False):
                done[0] += 1
                ins.then_inc(s["route_step"], 1)
                if wait:
                    (at_least_alone if alone else at_least)(dve, "route_step", STEPS * t + done[0])

            def flat(ap):
                return ap.rearrange("p b e -> p (b e)")

            def prefix_sum(t):
                for i, d in enumerate((1, 2, 4, 8)):
                    a, b = pre[(0, 1, 2, 1)[i]], pre[(1, 2, 1, 2)[i]]
                    step(V.tensor_tensor(b[:, :, 8:8 + E], a[:, :, 8:8 + E], a[:, :, 8 - d:8 - d + E], ALU.add), t)

            def route(t):
                done[0] = 0
                dve.wait_ge(s["gate_exp"], t + 1)
                step(V.tensor_scalar(flat(sfc[:, :, :]), flat(score[:, :, :]), 1.0, None, ALU.add), t)
                step(V.reciprocal(flat(score[:, :, :]), flat(sfc[:, :, :])), t)
                step(V.tensor_tensor(sfc[:, :, :], score[:, :, :],
                                     gbias[:, :].unsqueeze(1).to_broadcast([P, SUB, E]), ALU.add), t)
                grp = flat(sfc[:, :, :]).rearrange("p (g j k) -> p g j k", j=2, k=2)
                mx, mn = (v[:, :, :, :].rearrange("p b g k -> p (b g) k") for v in (pmx, pmn))
                step(V.tensor_tensor(mx, grp[:, :, 0, :], grp[:, :, 1, :], ALU.max), t, False)
                step(V.tensor_tensor(mn, grp[:, :, 0, :], grp[:, :, 1, :], ALU.min), t)
                step(V.tensor_tensor(g1[:, :], mx[:, :, 0], mx[:, :, 1], ALU.max), t, False)
                step(V.tensor_tensor(g2[:, :], mx[:, :, 0], mx[:, :, 1], ALU.min), t, False)
                step(V.tensor_tensor(g3[:, :], mn[:, :, 0], mn[:, :, 1], ALU.max), t)
                step(V.tensor_tensor(g2[:, :], g2[:, :], g3[:, :], ALU.max), t)
                step(V.tensor_tensor(gsc[:, :], g1[:, :], g2[:, :], ALU.add), t)
                gs = gsc[:, :].rearrange("p (b g) -> p b g", g=NG)
                one, other = (gs.unsqueeze(a).to_broadcast([P, SUB, NG, NG]) for a in (3, 2))
                ca, cb = (v[:, :, :, :] for v in (cmp_a, cmp_b))
                step(V.tensor_tensor(ca, other, one, ALU.is_gt), t, False)
                step(V.tensor_tensor(cb, other, one, ALU.is_equal), t)
                step(V.tensor_tensor(cb, cb, before[:, :, :].unsqueeze(1).to_broadcast([P, SUB, NG, NG]), ALU.mult), t)
                step(V.tensor_tensor(ca, ca, cb, ALU.add), t)
                step(V.tensor_reduce(g1[:, :], ca.rearrange("p b g k -> p (b g) k"), axis=AX_X, op=ALU.add), t)
                step(V.tensor_scalar(gkeep[:, :], g1[:, :], float(GROUPS_KEPT), None, ALU.is_lt), t)
                step(V.tensor_scalar(gpen[:, :], gkeep[:, :], 1.0, LOWEST, ALU.subtract, ALU.mult), t, False)
                pk = picked[:, :, :].rearrange("p b (g j) -> p (b g) j", j=EG)
                sf = sfc[:, :, :].rearrange("p b (g j) -> p (b g) j", j=EG)
                step(V.tensor_tensor(pk, sf, gkeep[:, :].unsqueeze(2).to_broadcast([P, SUB * NG, EG]), ALU.mult), t)
                step(V.tensor_tensor(pk, pk, gpen[:, :].unsqueeze(2).to_broadcast([P, SUB * NG, EG]), ALU.add),
                     t, alone=True)
                for b in range(SUB):
                    step(V.max(top8[:, b, :], picked[:, b, :]), t, b == SUB - 1)
                fourth = top8[:, :, TOP - 1:TOP].to_broadcast([P, SUB, E])
                step(V.tensor_tensor(above[:, :, :], picked[:, :, :], fourth, ALU.is_gt), t, False)
                step(V.tensor_tensor(pre[0][:, :, 8:8 + E], picked[:, :, :], fourth, ALU.is_equal), t)
                step(V.tensor_reduce(nabove[:, :], above[:, :, :], axis=AX_X, op=ALU.add), t, False)
                prefix_sum(t)
                step(V.tensor_tensor(posn[:, :, :], pre[2][:, :, 8:8 + E],
                                     nabove[:, :].unsqueeze(2).to_broadcast([P, SUB, E]), ALU.add), t)
                step(V.scalar_tensor_tensor(posn[:, :, :], posn[:, :, :], float(TOP), pre[0][:, :, 8:8 + E],
                                            ALU.is_le, ALU.mult), t)
                step(V.tensor_tensor(pre[0][:, :, 8:8 + E], posn[:, :, :], above[:, :, :], ALU.add), t)
                V.tensor_copy(sel16[:, :, :], pre[0][:, :, 8:8 + E]).then_inc(s["sel_done"], 1)
                sl = pre[0][:, :, 8:8 + E]
                step(V.tensor_tensor(wsel[:, :, :], score[:, :, :], sl, ALU.mult), t)
                step(V.tensor_reduce(wsum[:, :], wsel[:, :, :], axis=AX_X, op=ALU.add), t)
                step(V.tensor_scalar(wsum[:, :], wsum[:, :], 1e-20, None, ALU.add), t)
                step(V.reciprocal(nabove[:, :], wsum[:, :]), t)
                at_least(dve, "sent", 16 * SUB * TOP * t)
                step(V.scalar_tensor_tensor(row[:, :, D:D + E], wsel[:, :, :], SCALE,
                                            nabove[:, :].unsqueeze(2).to_broadcast([P, SUB, E]),
                                            ALU.mult, ALU.mult), t, False)
                prefix_sum(t)
                step(V.scalar_tensor_tensor(row[:, :, D + E:ROW], pre[2][:, :, 8:8 + E], float(N),
                                            tok_row[:, :].unsqueeze(2).to_broadcast([P, SUB, E]),
                                            ALU.mult, ALU.add), t)
                step(V.tensor_scalar(tok_row[:, :], tok_row[:, :], float(T), None, ALU.add), t)

            def place(t):
                dve.wait_ge(s["rank_mm"], t + 1)
                rank = psum[:, 3, SUB * E:2 * SUB * E].rearrange("p (b e) -> p b e", e=E)
                step(V.tensor_tensor(posn[:, :, :], rank, counts[:, :].unsqueeze(1).to_broadcast([P, SUB, E]),
                                     ALU.add), t)
                step(V.tensor_tensor(counts[:, :], counts[:, :], psum[:, 3, 2 * SUB * E:(2 * SUB + 1) * E],
                                     ALU.add), t)
                step(V.scalar_tensor_tensor(posn[:, :, :], posn[:, :, :], 1.0, pre[0][:, :, 8:8 + E],
                                            ALU.add, ALU.mult), t, alone=True)
                for b in range(SUB):
                    step(V.max(pos8[:, b, :], posn[:, b, :]), t, b == SUB - 1)
                V.tensor_scalar(row_id[:, :, :], pos8[:, :, 0:TOP], 1.0, None, ALU.subtract).then_inc(s["routed"], 1)
                assert done[0] == STEPS, done[0]

            def table():
                n = [0]

                def then(ins):
                    n[0] += 1
                    ins.then_inc(s["table_step"], 1)
                    dve.wait_ge(s["table_step"], n[0])
                V.tensor_copy(pad_at[:, :], counts[0:1, :]).then_inc(s["table_done"], 1)
                then(V.tensor_tensor(ntile[:, :], counts[:, :], region[:, :], ALU.subtract))
                then(V.tensor_scalar(ntile_i[:, :], ntile[:, :], float(P - 1), None, ALU.add))
                then(V.tensor_scalar(ntile_i[:, :], ntile_i[:, :], P.bit_length() - 1, None, ALU.arith_shift_right))
                then(V.tensor_copy(ends[0][:, 8:8 + E], ntile_i[:, :]))
                then(V.tensor_scalar(row_step[:, :], ends[0][:, 8:8 + E], -float(P), float(CAP), ALU.mult, ALU.add))
                for i, d in enumerate((1, 2, 4, 8)):
                    a, b = ends[(0, 1, 2, 1)[i]], ends[(1, 2, 1, 2)[i]]
                    then(V.tensor_tensor(b[:, 8:8 + E], a[:, 8:8 + E], a[:, 8 - d:8 - d + E], ALU.add))
                S2 = [P, TC, E]
                then(V.tensor_tensor(is_past[:, :, :], tile_no[:, :].unsqueeze(2).to_broadcast(S2),
                                     ends[2][:, 8:8 + E].unsqueeze(1).to_broadcast(S2), ALU.is_ge))
                then(V.tensor_tensor(past_step[:, :, :], is_past[:, :, :],
                                     row_step[:, :].unsqueeze(1).to_broadcast(S2), ALU.mult))
                then(V.tensor_reduce(tile_ef[:, :], is_past[:, :, :], axis=AX_X, op=ALU.add))
                then(V.tensor_scalar(tile_ef[:, :], tile_ef[:, :], float(E - 1), None, ALU.min))
                then(V.tensor_reduce(tile_row[:, :], past_step[:, :, :], axis=AX_X, op=ALU.add))
                then(V.scalar_tensor_tensor(tile_row[:, :], tile_no[:, :], float(P), tile_row[:, :], ALU.mult, ALU.add))
                then(V.tensor_scalar(tile_row[:, :], tile_row[:, :], float(IDLE), None, ALU.min))
                assert n[0] == TABLE_STEPS, n[0]

            def tile(t, first=False, last=False, more=True):
                if not last:
                    halo(t + 1)
                if not first:
                    route(t - 1)
                softplus(t, range(0, 2))
                if not last:
                    conv(t + 1, range(0, 1))
                softplus(t, range(2, KI))
                if not last:
                    conv(t + 1, range(1, KI))
                if not first:
                    place(t - 1)
                    shared_act(t - 1)
                    residual(t - 1)
                if more:
                    split_x(t + 2)
                layer_norm(t)
                if not last:
                    dt_low(t + 1)
                x1T_low(t)

            dve.wait_ge(s["win_h"], 1)
            V.tensor_tensor(win_lo[:, :, :], win_f, f32(win_hi[:, :, :]), ALU.subtract).then_inc(s["win_l"], 1)
            split_x(0)
            V.memset(keep[:, :], 1.0).then_inc(s["keep_one"], 1)
            V.memset(xs[:, :, T:T + HALO], 0.0).then_inc(s["keep_one"], 1)
            dve.wait_ge(s["keep_one"], 2)
            for t in range(0, NT, seq_len // T):
                V.memset(keep[:, t:t + 1], 0.0).then_inc(s["keep_ready"], 1)
            for v in pre:
                V.memset(v[:, :, 0:8], 0.0).then_inc(s["pre_zero"], 1)
            for v in ends:
                V.memset(v[:, 0:8], 0.0).then_inc(s["pre_zero"], 1)
            dve.wait_ge(s["keep_ready"], N // seq_len)
            dve.wait_ge(s["consts_in"], 64)
            halo(0)
            conv(0, range(KI))
            dve.wait_ge(s["wdt_h"], 1)
            V.tensor_tensor(wdt_lo[:, :], wdt_f[0:R, :], f32(wdt_hi[0:R, :]), ALU.subtract).then_inc(s["wdt_l"], 1)
            dt_low(0)
            dve.wait_ge(s["gw_h"], 1)
            V.tensor_tensor(gw_lo[:, :, :], gw[:, :, :], f32(gw_hi[:, :, :]), ALU.subtract).then_inc(s["gw_l"], 1)
            dve.wait_ge(s["wsgu_h"], 1)
            V.tensor_tensor(wsgu_lo[:, :, :], wsgu_f, f32(wsgu_hi[:, :, :]), ALU.subtract).then_inc(s["wsgu_l"], 1)
            split_x(1)
            dve.wait_ge(s["before_ready"], 1)
            dve.wait_ge(s["const_ready"], 4)
            dve.wait_ge(s["pre_zero"], len(pre) + len(ends))
            tile(0, first=True)
            tile(1)
            with dve.Fori(2, NT - 2) as t:
                tile(t)
            tile(NT - 2, more=False)
            tile(NT - 1, last=True, more=False)
            route(NT - 1)
            place(NT - 1)
            table()
            shared_act(NT - 1)
            residual(NT - 1)
            at_least(dve, "table_mm", 1)
            V.tensor_copy(tile_e[:, :], psum[0:1, 3, 0:NTILES]).then_inc(s["table_done"], 1)
            V.tensor_copy(tile_at[:, :], psum[0:1, 3, NTILES:2 * NTILES]).then_inc(s["table_done"], 1)
            for h in range(2):
                r = slice(h * E // 2, (h + 1) * E // 2)
                at_least(dve, "ew_hi", h + 1)
                V.tensor_tensor(ew_gu_lo[:, r, :, :], raw_gu[:, r, :, :], f32(ew_gu_hi[:, r, :, :]), ALU.subtract) \
                 .then_inc(s["ew_lo"], 1)
            at_least(dve, "ew_hi", 3)
            V.tensor_tensor(ew_d_lo[:, :, :], raw_d[:, :, :], f32(ew_d_hi[:, :, :]), ALU.subtract) \
             .then_inc(s["ew_lo"], 1)

            def tile_experts(q):
                return table_values(dve, tile_e, q, E - 1)

            def x_low(j, u, k):
                q, slot, turn, par = quad(j, u)
                at_least(dve, "t_h", KD * q + k + 1)
                V.tensor_tensor(t_lo[par][:, k, :], psum[:, 2 + k, :], f32(t_hi[par][:, k, :]), ALU.subtract) \
                 .then_inc(s["t_l"], 1)

            def weigh(j, u):
                q, slot, turn, par = quad(j, u)
                up = psum[:, 0:2, :].rearrange("p a (b i) -> p (a b) i", i=2 * I)
                experts = tile_experts(q)
                at_least(dve, "g_silu", q + 1)
                at_least(dve, "at_mm", q)
                for i, e in enumerate(experts):
                    V.scalar_tensor_tensor(e_act[:, i, :], g_act[:, i, :], tiles_in[:, slot, i, bass.ds(D + e, 1)],
                                           up[:, i, I:2 * I], ALU.mult, ALU.mult).then_inc(s["e_mul"], 1)
                return experts

            def result_rows(j, u, experts):
                q, slot, turn, par = quad(j, u)
                at_least(dve, f"y_sent{par}", 16 * SUB * (RING // 2 * (turn - 1) + slot // 2 + 1))
                for i, e in enumerate(experts):
                    V.tensor_copy(y_id[slot][:, i:i + 1], tiles_in[:, slot, i, bass.ds(D + E + e, 1)]) \
                     .then_inc(s["y_id_done"], 1)

            def act_low(j, u):
                q, slot, turn, par = quad(j, u)
                at_least(dve, "a_h", q + 1)
                V.tensor_tensor(a_lo[:, :], psum[:, 4, :], f32(a_hi[:, :]), ALU.subtract).then_inc(s["a_l"], 1)

            def result(j, u):
                q, slot, turn, par = quad(j, u)
                at_least(dve, f"y_sent{par}", 16 * SUB * ((RING // 2) * j + u // 2))
                at_least(dve, "y_mm", 2 * q + 2)
                V.tensor_copy(y_out[par][:, 2:4, :], psum[:, 7, :].rearrange("p (b d) -> p b d", d=D)) \
                 .then_inc(s["y_half1"], 1)

            def iteration(j, u):
                experts = weigh(j, u)
                if u + 2 < quads_left(j):
                    for k in range(KD):
                        x_low(j, u + 2, k)
                if not is_first(j, u):
                    result(j, u - 1)
                act_low(j, u)
                result_rows(j, u, experts)

            for u in range(2):
                for k in range(KD):
                    x_low(0, u, k)
            each_quad(dve, iteration)
            result(NQ // RING - 1, RING - 1)

            def sums(j, h):
                g = 2 * j + h
                x2 = [res[:, bass.ds(SUB * g + i, 1), :].squeeze(1) for i in range(SUB)]
                for i in range(SUB):
                    y = y_in[h * SUB + i]
                    at_least(dve, "y_paired", SUB * g + i + 1)
                    V.tensor_tensor(y[:, 0, :], y[:, 0, :], y[:, 1, :], ALU.add).then_inc(s["y_summed"], 1)
                for i in range(SUB):
                    at_least(dve, "y_summed", SUB * g + i + 1)
                    V.tensor_tensor(x2[i], x2[i], y_in[h * SUB + i][:, 0, :], ALU.add) \
                     .then_inc(s[f"y_used{h * SUB + i}"], 1)
                for i in range(SUB):
                    at_least_alone(dve, f"y_used{h * SUB + i}", j + 1)
                    V.bn_stats(o_stats[:, i, :], x2[i]).then_inc(s["o_bn"], 1)
                for i in range(SUB):
                    at_least_alone(dve, "o_bn", SUB * g + i + 1)
                    V.bn_aggr(o_mv[h][:, i, :], o_stats[:, i, :]).then_inc(s["o_agg"], 1)
                at_least(dve, "o_agg", SUB * (g + 1))
                V.tensor_scalar(o_var[h][:, :], o_mv[h][:, :, 1], EPS, None, ALU.add).then_inc(s["o_var_done"], 1)

            def norm(j, h):
                g = 2 * j + h
                rs, nt_ = o_rstd[h][:, :], o_nt[:, :]
                at_least(dve, "o_rstd_exp", g + 1)
                V.tensor_tensor(nt_, rs, rs, ALU.mult).then_inc(s["o_norm"], 1)
                at_least(dve, "o_norm", 4 * g + 1)
                V.tensor_tensor(nt_, nt_, o_var[h][:, :], ALU.mult).then_inc(s["o_norm"], 1)
                at_least(dve, "o_norm", 4 * g + 2)
                V.tensor_scalar(nt_, nt_, -0.5, 1.5, ALU.mult, ALU.add).then_inc(s["o_norm"], 1)
                at_least(dve, "o_norm", 4 * g + 3)
                V.tensor_tensor(rs, rs, nt_, ALU.mult).then_inc(s["o_norm"], 1)
                at_least(dve, "o_norm", 4 * g + 4)
                V.scalar_tensor_tensor(o_shift[h][:, :], o_mv[h][:, :, 0], -1.0, rs, ALU.mult, ALU.mult) \
                 .then_inc(s["o_ready"], 1)

            def body(j):
                sums(j, 1)
                norm(j, 0)
                sums(j + 1, 0)
                norm(j, 1)

            sums(0, 0)
            body(0)
            with dve.Fori(1, N // P // YR - 1) as j:
                body(j)
            j = N // P // YR - 1
            sums(j, 1)
            norm(j, 0)
            norm(j, 1)


_ORDER = ("x_tok x_T w_in_T conv_w conv_b w_x_T w_dt_T b_dt w_out_T gate_w_T gate_bias "
          "wg_T wu_T wd_T ws_g_T ws_u_T ws_d_T").split()


def kernel(L0_attn_x, L0_attn_W_in, L0_attn_conv_w, L0_attn_conv_b, L0_attn_W_x, L0_attn_W_dt, L0_attn_b_dt,
           L0_attn_W_out, L0_ffn_gate_w, L0_ffn_gate_bias, L0_ffn_Wg, L0_ffn_Wu, L0_ffn_Wd, L0_ffn_Ws_g,
           L0_ffn_Ws_u, L0_ffn_Ws_d):
    import numpy as np
    import concourse.bacc as bacc
    from concourse import mybir as mb
    from concourse.bass_utils import run_bass_kernel_spmd

    x = np.asarray(L0_attn_x)
    batch, seq, d = x.shape
    x = x.reshape(batch * seq, d)
    per_channel = lambda v: np.asarray(v).reshape(-1, 128).T
    laid = {
        "x_tok": x, "x_T": x.T,
        "w_in_T": np.asarray(L0_attn_W_in).T,
        "conv_w": np.asarray(L0_attn_conv_w).reshape(-1, 128, 4).transpose(1, 0, 2),
        "conv_b": per_channel(L0_attn_conv_b),
        "w_x_T": np.asarray(L0_attn_W_x).T,
        "w_dt_T": np.asarray(L0_attn_W_dt).T,
        "b_dt": per_channel(L0_attn_b_dt),
        "w_out_T": np.asarray(L0_attn_W_out).T,
        "gate_w_T": np.asarray(L0_ffn_gate_w).T,
        "gate_bias": np.asarray(L0_ffn_gate_bias).reshape(1, -1),
        "wg_T": np.asarray(L0_ffn_Wg).transpose(0, 2, 1),
        "wu_T": np.asarray(L0_ffn_Wu).transpose(0, 2, 1),
        "wd_T": np.asarray(L0_ffn_Wd).transpose(0, 2, 1),
        "ws_g_T": np.asarray(L0_ffn_Ws_g).T,
        "ws_u_T": np.asarray(L0_ffn_Ws_u).T,
        "ws_d_T": np.asarray(L0_ffn_Ws_d).T,
    }
    nc = bacc.Bacc("TRN2", target_bir_lowering=False, num_devices=1)
    arrays, args = {}, []
    for name in _ORDER:
        a = np.ascontiguousarray(laid[name])
        arrays[f"in_{name}"] = a
        args.append(nc.dram_tensor(f"in_{name}", a.shape, mb.dt.from_np(a.dtype), kind="ExternalInput").ap())
    out = nc.dram_tensor("out_dram", x.shape, mb.dt.from_np(x.dtype), kind="ExternalOutput").ap()
    mamba_moe(nc, *args, out, seq)
    got = run_bass_kernel_spmd(nc, [arrays], core_ids=[0]).results[0]["out_dram"]
    return got.reshape(batch, seq, d)
```

```python
import concourse.bass as bass
from concourse import mybir
from contextlib import ExitStack

P = 128
F32 = mybir.dt.float32
F32R = mybir.dt.float32r
BF16 = mybir.dt.bfloat16
I32 = mybir.dt.int32
ALU = mybir.AluOpType
ACT = mybir.ActivationFunctionType
AX_X = mybir.AxisListType.X

EPS = 1e-5
SCALE = 2.5
TOP = 4
GROUPS_KEPT = 2
LOWEST = 3e38
RSQRT_MAGIC = float(0x5F3759DF)
NEWTON = 3
EXP_MAX = 2.0 ** 60


def mamba_moe(nc, x_tok, x_T, w_in_T, conv_w, conv_b, w_x_T, w_dt_T, b_dt, w_out_T,
              gate_w_T, gate_bias, wg_T, wu_T, wd_T, ws_g_T, ws_u_T, ws_d_T, out, seq_len):
    N, D = x_tok.shape
    DI = w_in_T.shape[1] // 2
    R = w_dt_T.shape[0]
    TAPS = conv_w.shape[2]
    E, _, I = wg_T.shape
    SH = ws_d_T.shape[0]
    T = 512
    NT = N // T
    SUB = T // P
    KD, KI, KS = D // P, DI // P, SH // P
    NG = 4
    EG = E // NG
    ROW = D + 2 * E
    CAP = N + P
    IDLE = E * CAP
    NTILES = -(-(N * TOP // P + E) // SUB) * SUB
    HALO = TAPS - 1

    x_buf = nc.dram_tensor("x_buf", (IDLE + P, ROW), F32).ap()
    y_buf = nc.dram_tensor("y_buf", (TOP * N, D), F32).ap()

    with ExitStack() as ctx:
        def sb(name, shape, dt=F32, scope=ctx):
            return scope.enter_context(nc.sbuf_tensor(name, shape, dt))

        def sem(name):
            return ctx.enter_context(nc.semaphore(name))

        psum = ctx.enter_context(nc.psum_tensor("psum", [P, 8, T], F32))

        res = sb("res", [P, N // P, D])
        ident = sb("ident", [P, P])
        counts = sb("counts", [P, E])
        pad_row = sb("pad_row", [P, ROW])
        TC = -(-NTILES // P)
        region = sb("region", [P, E])
        ntile_i = sb("ntile_i", [P, E], I32)
        ntile, row_step = sb("ntile", [P, E]), sb("row_step", [P, E])
        ends = [sb(f"ends{i}", [P, 8 + E]) for i in range(3)]
        tile_no = sb("tile_no", [P, TC])
        is_past, past_step = sb("is_past", [P, TC, E]), sb("past_step", [P, TC, E])
        tile_ef, tile_row = sb("tile_ef", [P, TC]), sb("tile_row", [P, TC])
        tile_e = sb("tile_e", [1, NTILES], I32)
        tile_at = sb("tile_at", [1, NTILES], I32)
        pad_at = sb("pad_at", [1, E], I32)

        p0 = ExitStack()
        raw_gu = sb("raw_gu", [P, E, KD, 2 * I], F32, p0)
        raw_d = sb("raw_d", [P, E, D], F32, p0)
        p1sb = lambda name, shape, dt=F32: sb(name, shape, dt, p0)
        win_hi, win_lo = (p1sb(n, [P, KD, 2 * DI], F32R) for n in ("win_hi", "win_lo"))
        xT = p1sb("xT", [P, KD, T])
        x_hi, x_lo = (p1sb(n, [P, KD, T], F32R) for n in ("x_hi", "x_lo"))
        xs = p1sb("xs", [P, KI, HALO + T])
        xc = p1sb("xc", [P, KI, T])
        zs = p1sb("zs", [P, KI, T])
        m = p1sb("m", [P, KI, T])
        sp = p1sb("sp", [P, KI, T])
        wx = p1sb("wx", [P, KI, 2 * R])
        wdt_hi = p1sb("wdt_hi", [2 * R, DI], F32R)
        wdt_lo = p1sb("wdt_lo", [R, DI], F32R)
        wout = p1sb("wout", [P, KI, D])
        gw = p1sb("gw", [P, KD, E])
        gw_hi, gw_lo = (p1sb(n, [P, KD, E], F32R) for n in ("gw_hi", "gw_lo"))
        wsgu_hi, wsgu_lo = (p1sb(n, [P, KD, 2 * SH], F32R) for n in ("wsgu_hi", "wsgu_lo"))
        wsd = p1sb("wsd", [P, KS, D])
        cw_taps = p1sb("cw_taps", [P, KI, TAPS])
        cbias = p1sb("cbias", [P, KI])
        dtbias = p1sb("dtbias", [P, KI])
        gbias = p1sb("gbias", [P, E])
        keep = p1sb("keep", [P, NT])
        tri = p1sb("tri", [P, P], BF16)
        ones = p1sb("ones", [P, P], BF16)
        before = p1sb("before", [P, NG, NG])
        tok_row = p1sb("tok_row", [P, SUB])

        dt = p1sb("dt", [2 * R, T], F32R)
        x1 = p1sb("x1", [P, SUB, D])
        x1T_hi, x1T_lo = (p1sb(n, [P, KD, T], F32R) for n in ("x1T_hi", "x1T_lo"))
        sg = p1sb("sg", [P, KS, T])
        sh = p1sb("sh", [P, KS, T])
        stats = p1sb("stats", [P, SUB, 6])
        mv = p1sb("mv", [P, SUB, 2])
        var, neg_half, rstd, newton = (p1sb(n, [P, SUB]) for n in ("var", "neg_half", "rstd", "newton"))
        half_bits = p1sb("half_bits", [P, SUB], I32)
        S3 = [P, SUB, E]
        score, sfc, picked = p1sb("score", S3), p1sb("sfc", S3), p1sb("picked", S3)
        above, equal, sel, wsel, posn = (p1sb(n, S3) for n in ("above", "equal", "sel", "wsel", "posn"))
        sel16 = p1sb("sel16", S3, BF16)
        pmx, pmn = p1sb("pmx", [P, SUB, NG, 2]), p1sb("pmn", [P, SUB, NG, 2])
        g1, g2, g3, gsc = (p1sb(n, [P, SUB * NG]) for n in ("g1", "g2", "g3", "gsc"))
        cmp_a, cmp_b = p1sb("cmp_a", [P, SUB, NG, NG]), p1sb("cmp_b", [P, SUB, NG, NG])
        gkeep, gpen = p1sb("gkeep", [P, SUB * NG]), p1sb("gpen", [P, SUB * NG])
        top8, pos8 = p1sb("top8", [P, SUB, 8]), p1sb("pos8", [P, SUB, 8])
        nabove, wsum = p1sb("nabove", [P, SUB]), p1sb("wsum", [P, SUB])
        slots, ones_f = p1sb("slots", S3), p1sb("ones_f", S3)
        block_start = p1sb("block_start", S3)

        row, row_end = p1sb("row", [P, SUB, ROW]), p1sb("row_end", [P, SUB, ROW])
        xtok = row_end[:, :, 0:D]
        row_id, row_id_end = (p1sb(n, [P, SUB, TOP], I32) for n in ("row_id", "row_id_end"))
        p0.close()

        p2 = ctx.enter_context(ExitStack())
        p2sb = lambda name, shape, dt=F32: sb(name, shape, dt, p2)
        RING = 4
        t_hi, t_lo = ([p2sb(f"{n}{i}", [P, KD, T], F32R) for i in range(2)] for n in ("t_hi", "t_lo"))
        g_act = p2sb("g_act", [P, SUB, I])
        e_act = p2sb("e_act", [P, SUB, I])
        a_hi, a_lo = p2sb("a_hi", [P, T], F32R), p2sb("a_lo", [P, T], F32R)
        in_raw = 4 * KD * T + 2 * SUB * I + 2 * T
        behind_raw = p2sb("behind_raw", [P, E * (KD * 2 * I + D) - in_raw])
        ew_gu_hi, ew_gu_lo = (p2sb(n, [P, E, KD, 2 * I], F32R) for n in ("ew_gu_hi", "ew_gu_lo"))
        ew_d_hi, ew_d_lo = (p2sb(n, [P, E, D], F32R) for n in ("ew_d_hi", "ew_d_lo"))
        y_out = [p2sb(f"y_out{i}", [P, SUB, D]) for i in range(2)]
        y_id = [p2sb(f"y_id{i}", [P, SUB], I32) for i in range(RING)]
        tiles_in = p2sb("tiles_in", [P, RING, SUB, ROW])
        p2.close()
        p3 = ctx.enter_context(ExitStack())
        YR = 2 * SUB
        y_in = [sb(f"y_in{i}", [P, TOP, D], F32, p3) for i in range(YR)]
        o_stats = sb("o_stats", [P, SUB, 6], F32, p3)
        o_neg_half, o_newton = sb("o_neg_half", [P, SUB], F32, p3), sb("o_newton", [P, SUB], F32, p3)
        o_half_bits = sb("o_half_bits", [P, SUB], I32, p3)
        o_mv, o_var = sb("o_mv", [P, SUB, 2], F32, p3), sb("o_var", [P, SUB], F32, p3)
        o_rstd = [sb(f"o_rstd{i}", [P, SUB], F32, p3) for i in range(2)]
        o_shift = [sb(f"o_shift{i}", [P, SUB], F32, p3) for i in range(2)]

        win_f = sp[:, :, :].rearrange("p a b -> p (a b)").rearrange("p (k n) -> p k n", k=KD)
        wsgu_f = sh[:, :, :]
        wdt_f = sg[0:2 * R, 0, :]

        names = """w_in_in w_x_in w_dt_in w_out_in gate_in w_sgu_in w_sd_in consts_in
            win_h win_l wdt_h wdt_l gw_h gw_l wsgu_h wsgu_l
            ones_ready keep_one keep_ready pre_zero id_zero id_ready tri_one tri_ready before_one before_ready const_ready
            xT_in xtok_in x_hi_done x_lo_done s1_mm s1_evac halo_done conv_step tap_done conv_step_pool xc_done m_done
            wx_mm dt_hi dt_lo wdt_mm exp_done exp_clamped ln_done sp_done y_done
            wout_mm ln_in bn bn_mv norm_step x1_done x1_twice xt_mm x1T_h x1T_l
            gate_mm gate_exp route_step sel_done rank_mm routed row_x sent
            sgu_mm ssilu h_done sd_mm res_done
            raw_in table_step table_mm table_done pad_at_done pad_ready pads_out ew_hi ew_lo ew_lo_pool
            tile_in0 tile_in1 tile_in2 tile_in3 t_mm t_h t_l gu_mm g_silu e_mul at_mm a_h a_l y_mm
            y_half0 y_half1 y_id_done y_sent0 y_sent1
            y_in0 y_in1 y_in2 y_in3 y_in4 y_in5 y_in6 y_in7 y_paired
            y_used0 y_used1 y_used2 y_used3 y_used4 y_used5 y_used6 y_used7 y_summed
            o_bn o_agg o_norm o_ready o_done stored""".split()
        s = {n: sem(n) for n in names}

        def at_least_alone(eng, name, n):
            if isinstance(n, int):
                return at_least(eng, name, n)
            n = eng.to_reg(n)
            eng.wait_ge(s["ones_ready"], 1)
            eng.wait_ge(s[name], n)

        def at_least(eng, name, n):
            if isinstance(n, int) and n <= 0:
                return
            eng.wait_ge(s[name], n)

        TABLE_STEPS = 16
        NORM_STEPS = 4 + 3 * NEWTON
        NQ = NTILES // SUB

        def quad(j, u):
            return RING * j + u, u % RING, j + u // RING, u % 2

        def table_values(eng, table, q, most):
            return nc.values_load_multi_w_load_instructions(
                table[0:1, bass.ds(SUB * q, SUB)], engines=(eng.engine,), min_val=0, max_val=most,
                skip_runtime_bounds_check_because="the table is clamped to these bounds")[1]

        def quads_left(j):
            return RING if isinstance(j, int) and j == NQ // RING - 1 else 2 * RING

        def is_first(j, u):
            return isinstance(j, int) and j == 0 and u == 0

        def each_quad(eng, iteration):
            def body(j):
                for u in range(RING):
                    iteration(j, u)
            body(0)
            with eng.Fori(1, NQ // RING - 1) as j:
                body(j)
            body(NQ // RING - 1)

        PART = E // 4
        gu_parts = [slice(i * PART, (i + 1) * PART) for i in range(4)]
        d_parts = [slice(0, E // 2), slice(E // 2, E)]
        GU_POOL = 2
        CONV_DVE = KI // 2
        STEPS_DVE, STEPS_POOL = HALO * CONV_DVE, HALO * (KI - CONV_DVE)
        tap_out = [sg[:, 0, :], sg[:, 1, :], sh[:, 0, :], sh[:, 1, :], zs[:, 2, :], zs[:, 3, :]]
        assert len(tap_out) == STEPS_POOL

        def tap_added(eng, t, n):
            if isinstance(t, int) and not 0 < t < NT:
                return
            at_least(eng, "conv_step_pool", STEPS_POOL * t + n)

        block = ctx.enter_context(nc.Block())
        taps = cw_taps

        @block.sync
        def _(sp_):
            sp_.dma_start(win_f, w_in_T.rearrange("(k p) n -> p k n", p=P)).then_inc(s["w_in_in"], 16)

            def load_x(t):
                at_least(sp_, "x_hi_done", t)
                at_least(sp_, "x_lo_done", t)
                sp_.dma_start(xT[:, :, :], x_T.rearrange("(k p) n -> p k n", p=P)[:, :, bass.ds(t * T, T)]) \
                   .then_inc(s["xT_in"], 16)

            def load_tok(t):
                at_least(sp_, "ln_in", 2 * t)
                sp_.dma_start(xtok, x_tok.rearrange("(n p) d -> p n d", p=P)[:, bass.ds(t * SUB, SUB), :]) \
                   .then_inc(s["xtok_in"], 16)

            load_x(0)
            sp_.dma_start(cw_taps[:, :, :], conv_w).then_inc(s["consts_in"], 16)
            sp_.dma_start(cbias[:, :], conv_b).then_inc(s["consts_in"], 16)
            sp_.dma_start(dtbias[:, :], b_dt).then_inc(s["consts_in"], 16)
            sp_.dma_start(gbias[:, :], gate_bias.to_broadcast([P, E])).then_inc(s["consts_in"], 16)
            for i in range(2):
                sp_.dma_start(wx[:, :, i * R:(i + 1) * R],
                              w_x_T.rearrange("(k p) n -> p k n", p=P)[:, :, 0:R]).then_inc(s["w_x_in"], 16)
                sp_.dma_start(wdt_f[i * R:(i + 1) * R, :], w_dt_T).then_inc(s["w_dt_in"], 16)
            sp_.dma_start(wout[:, :, :], w_out_T.rearrange("(k p) n -> p k n", p=P)).then_inc(s["w_out_in"], 16)
            load_tok(0)
            sp_.dma_start(gw[:, :, :], gate_w_T.rearrange("(k p) n -> p k n", p=P)).then_inc(s["gate_in"], 16)
            for i, w in enumerate((ws_g_T, ws_u_T)):
                sp_.dma_start(wsgu_f[:, :, i * SH:(i + 1) * SH],
                              w.rearrange("(k p) n -> p k n", p=P)).then_inc(s["w_sgu_in"], 16)
            sp_.dma_start(wsd[:, :, :], ws_d_T.rearrange("(k p) n -> p k n", p=P)).then_inc(s["w_sd_in"], 16)
            load_x(1)
            for e in range(E):
                for i, w in enumerate((wg_T, wu_T)):
                    sp_.dma_start(raw_gu[:, e, :, i * I:(i + 1) * I],
                                  w[e, :, :].rearrange("(k p) i -> p k i", p=P)).then_inc(s["raw_in"], 16)
                sp_.dma_start(raw_d[:, e, :], wd_T[e, :, :]).then_inc(s["raw_in"], 16)
            with sp_.Fori(1, NT - 1) as t:
                load_x(t + 1)
                load_tok(t)
            load_tok(NT - 1)

            at_least(sp_, "pad_ready", 1)
            sp_.dma_start(x_buf[IDLE:IDLE + P, :], pad_row[:, :]).then_inc(s["pads_out"], 16)
            at_least(sp_, "pad_at_done", 1)
            for g in range(NG):
                firsts = table_values(sp_, pad_at, g, IDLE)
                for first in firsts:
                    sp_.dma_start(x_buf[bass.ds(first, P), :], pad_row[:, :]).then_inc(s["pads_out"], 16)
            at_least(sp_, "pads_out", 16 * (E + 1))
            at_least(sp_, "sent", 16 * SUB * TOP * NT)
            at_least(sp_, "table_done", 2)

            def load_tiles(j, u):
                q, slot, turn, _ = quad(j, u)
                at_least(sp_, "y_id_done", SUB * (q - RING + 1))
                for i, first in enumerate(table_values(sp_, tile_at, q, IDLE)):
                    sp_.dma_start(tiles_in[:, slot, i, :], x_buf[bass.ds(first, P), :]) \
                       .then_inc(s[f"tile_in{slot}"], 16)
            each_quad(sp_, load_tiles)

            for i in range(2):
                at_least(sp_, f"y_sent{i}", 16 * SUB * NQ // 2)

            def load_results(j):
                for u in range(YR):
                    at_least(sp_, f"y_used{u}", j)
                    sp_.dma_start(y_in[u][:, :, :], y_buf.rearrange("(k n p) d -> p n k d", k=TOP, p=P)
                                  [:, bass.ds(YR * j + u, 1), :, :].squeeze(1)).then_inc(s[f"y_in{u}"], 16)

            load_results(0)
            with sp_.Fori(1, N // P // YR) as j:
                load_results(j)
            at_least(sp_, "stored", 16 * N // P // SUB)

        @block.gpsimd
        def _(pool):
            nc.gpsimd.memset(ident[:, :], 0.0).then_inc(s["id_zero"], 1)
            pool.wait_ge(s["id_zero"], 1)
            nc.gpsimd.affine_select(out=ident[:, :], in_=ident[:, :], compare_op=ALU.not_equal, fill=1.0,
                                    base=0, pattern=[[-1, P]], channel_multiplier=1).then_inc(s["id_ready"], 1)
            nc.gpsimd.memset(tri[:, :], 1.0).then_inc(s["tri_one"], 1)
            pool.wait_ge(s["tri_one"], 1)
            nc.gpsimd.affine_select(out=tri[:, :], in_=tri[:, :], compare_op=ALU.is_gt, fill=0.0,
                                    base=0, pattern=[[1, P]], channel_multiplier=-1).then_inc(s["tri_ready"], 1)
            nc.gpsimd.memset(ones[:, :], 1.0).then_inc(s["ones_ready"], 1)
            nc.gpsimd.memset(before[:, :, :], 1.0).then_inc(s["before_one"], 1)
            pool.wait_ge(s["before_one"], 1)
            nc.gpsimd.affine_select(out=before[:, :, :], in_=before[:, :, :], compare_op=ALU.is_gt, fill=0.0,
                                    base=0, pattern=[[1, NG], [-1, NG]], channel_multiplier=0) \
                     .then_inc(s["before_ready"], 1)
            nc.gpsimd.iota(tok_row[:, :], pattern=[[P - TOP * N, SUB]], base=-N, channel_multiplier=1,
                           allow_small_or_imprecise_dtypes=True).then_inc(s["const_ready"], 1)
            for v in (counts, region):
                nc.gpsimd.iota(v[:, :], pattern=[[CAP, E]], base=0, channel_multiplier=0,
                               allow_small_or_imprecise_dtypes=True).then_inc(s["const_ready"], 1)
            nc.gpsimd.iota(tile_no[:, :], pattern=[[P, TC]], base=0, channel_multiplier=1,
                           allow_small_or_imprecise_dtypes=True).then_inc(s["const_ready"], 1)
            nc.gpsimd.memset(pad_row[:, 0:D + E], 0.0)
            nc.gpsimd.memset(pad_row[:, D + E:ROW], float(TOP * N)).then_inc(s["pad_ready"], 1)

            def conv(t):
                for n in range(STEPS_POOL):
                    c = CONV_DVE + n // HALO
                    at_least(pool, "tap_done", STEPS_POOL * (t - 1) + n + 1)
                    if n % HALO:
                        tap_added(pool, t, n)
                    nc.gpsimd.tensor_tensor(xc[:, c, :], xc[:, c, :], tap_out[n], ALU.add) \
                             .then_inc(s["conv_step_pool"], 1)

            def gate_product(t):
                for c in range(KI):
                    at_least(pool, "xc_done", KI * t + c + 1)
                    at_least(pool, "s1_evac", 2 * KI * t + KI + c + 1)
                    if c == 0:
                        at_least(pool, "wout_mm", 2 * t)
                    nc.gpsimd.tensor_tensor(m[:, c, :], xc[:, c, :], zs[:, c, :], ALU.mult).then_inc(s["m_done"], 1)

            def x_low(t):
                at_least(pool, "x_hi_done", t + 1)
                at_least(pool, "s1_mm", 2 * KI * t)
                nc.gpsimd.tensor_tensor(x_lo[:, :, :], xT[:, :, :], x_hi[:, :, :].bitcast(F32), ALU.subtract) \
                         .then_inc(s["x_lo_done"], 1)

            def send(t, row=row, row_id=row_id):
                at_least_alone(pool, "routed", t + 1)
                at_least_alone(pool, "row_x", t + 1)
                for b in range(SUB):
                    for k in range(TOP):
                        nc.gpsimd.indirect_dma_start(
                            out=x_buf, out_offset=bass.IndirectOffsetOnAxis(ap=row_id[:, b, k:k + 1], axis=0),
                            in_=row[:, b, :], in_offset=None).then_inc(s["sent"], 16)

            x_low(0)
            gate_product(0)
            x_low(1)

            def tile(t, first=False, more=True):
                conv(t + 1)
                gate_product(t + 1)
                if more:
                    x_low(t + 2)
                if not first:
                    send(t - 1)
            tile(0, first=True)
            with pool.Fori(1, NT - 2) as t:
                tile(t)
            tile(NT - 2, more=False)
            for i in range(GU_POOL):
                r = gu_parts[i]
                at_least(pool, "ew_hi", i + 1)
                nc.gpsimd.tensor_tensor(ew_gu_lo[:, r, :, :], raw_gu[:, r, :, :], ew_gu_hi[:, r, :, :].bitcast(F32),
                                        ALU.subtract).then_inc(s["ew_lo_pool"], 1)
            send(NT - 2)
            send(NT - 1, row_end, row_id_end)

            def send_results(j, u):
                q, slot, turn, par = quad(j, u)
                at_least_alone(pool, "y_half0", q + 1)
                at_least_alone(pool, "y_half1", q + 1)
                at_least_alone(pool, "y_id_done", SUB * (q + 1))
                for i in range(SUB):
                    nc.gpsimd.indirect_dma_start(
                        out=y_buf, out_offset=bass.IndirectOffsetOnAxis(ap=y_id[slot][:, i:i + 1], axis=0),
                        in_=y_out[par][:, i, :], in_offset=None, bounds_check=TOP * N - 1, oob_is_err=False) \
                      .then_inc(s[f"y_sent{par}"], 16)
            each_quad(pool, send_results)

            with pool.Fori(0, N // P // YR) as j:
                for u in range(YR):
                    at_least(pool, f"y_in{u}", 16 * (j + 1))
                    nc.gpsimd.tensor_tensor(y_in[u][:, 0:2, :], y_in[u][:, 0:2, :], y_in[u][:, 2:4, :], ALU.add) \
                             .then_inc(s["y_paired"], 1)

        def split_mm(pe, o, w_hi, w_lo, v_hi, v_lo, start, stop):
            pe.matmul(o, w_hi, v_hi, start=start, stop=False)
            pe.matmul(o, w_hi, v_lo, start=False, stop=False)
            return pe.matmul(o, w_lo, v_hi, start=False, stop=stop)

        @block.tensor
        def _(pe):
            def in_proj(t, chunks):
                for j in chunks:
                    if j == 0:
                        at_least(pe, "x_hi_done", t + 1)
                        at_least(pe, "x_lo_done", t + 1)
                    at_least(pe, "s1_evac", 2 * KI * t + j - 1)
                    for k in range(KD):
                        mm = split_mm(pe, psum[:, j % 2, :], win_hi[:, k, j * P:(j + 1) * P],
                                      win_lo[:, k, j * P:(j + 1) * P], x_hi[:, k, :], x_lo[:, k, :],
                                      k == 0, k == KD - 1)
                    mm.then_inc(s["s1_mm"], 1)

            def dt_in(t):
                at_least(pe, "dt_lo", t)
                for c in range(KI):
                    at_least(pe, "xc_done", KI * t + c + 1)
                    mm = pe.matmul(psum[0:2 * R, 2, :], wx[:, c, :], xc[:, c, :], start=c == 0, stop=c == KI - 1)
                mm.then_inc(s["wx_mm"], 1)

            def dt_out(t, chunks):
                at_least(pe, "dt_lo", t + 1)
                at_least(pe, "x1T_h", t)
                at_least(pe, "x1T_l", t)
                for c in chunks:
                    if c >= 2:
                        at_least(pe, "sp_done", KI * t + c - 1)
                    pe.matmul(psum[:, 4 + c % 2, :], wdt_hi[:, c * P:(c + 1) * P], dt[:, :], start=True, stop=False)
                    pe.matmul(psum[:, 4 + c % 2, :], wdt_lo[:, c * P:(c + 1) * P], dt[0:R, :],
                              start=False, stop=True).then_inc(s["wdt_mm"], 1)

            def out_proj(t):
                at_least(pe, "y_done", KI * (t + 1))
                for b in range(SUB):
                    o = psum[:, 4 + b // 2, (b % 2) * D:(b % 2 + 1) * D]
                    for c in range(KI):
                        mm = pe.matmul(o, m[:, c, b * P:(b + 1) * P], wout[:, c, :], start=c == 0, stop=c == KI - 1)
                    if b % 2:
                        mm.then_inc(s["wout_mm"], 1)

            def transposes(t):
                for b in range(SUB):
                    at_least(pe, "x1_done", SUB * t + b + 1)
                    for k in range(KD):
                        mm = pe.transpose(psum[:, 4 + k, b * P:(b + 1) * P], x1[:, b, k * P:(k + 1) * P], ident[:, :])
                mm.then_inc(s["xt_mm"], 1)

            def gate(t):
                at_least(pe, "x1T_h", t + 1)
                at_least(pe, "x1T_l", t + 1)
                at_least(pe, "gate_exp", t)
                for b in range(SUB):
                    r = slice(b * P, (b + 1) * P)
                    for k in range(KD):
                        o = psum[:, 3, b * E:(b + 1) * E]
                        pe.matmul(o, x1T_hi[:, k, r], gw_hi[:, k, :], start=k == 0, stop=False)
                        pe.matmul(o, x1T_hi[:, k, r], gw_lo[:, k, :], start=False, stop=False)
                        mm = pe.matmul(o, x1T_lo[:, k, r], gw_hi[:, k, :], start=False, stop=k == KD - 1)
                mm.then_inc(s["gate_mm"], 1)

            def shared_up(t, i):
                at_least(pe, "res_done", 2 * t)
                at_least(pe, "h_done", KS * t + i)
                for j in range(2):
                    c = slice(j * SH + i * P, j * SH + (i + 1) * P)
                    for k in range(KD):
                        mm = split_mm(pe, psum[:, 6 + j, :], wsgu_hi[:, k, c], wsgu_lo[:, k, c],
                                      x1T_hi[:, k, :], x1T_lo[:, k, :], k == 0, k == KD - 1)
                mm.then_inc(s["sgu_mm"], 1)

            def ranks(t):
                at_least(pe, "sel_done", t + 1)
                at_least(pe, "routed", t)
                for b in range(SUB):
                    o = psum[:, 3, (SUB + b) * E:(SUB + b + 1) * E]
                    pe.matmul(o, tri[:, :], sel16[:, b, :], start=True, stop=b == 0)
                    for q in range(b):
                        pe.matmul(o, ones[:, :], sel16[:, q, :], start=False, stop=q == b - 1)
                for b in range(SUB):
                    mm = pe.matmul(psum[:, 3, 2 * SUB * E:(2 * SUB + 1) * E], ones[:, :], sel16[:, b, :],
                                   start=b == 0, stop=b == SUB - 1)
                mm.then_inc(s["rank_mm"], 1)

            def shared_down(t):
                at_least(pe, "h_done", KS * (t + 1))
                for b in range(SUB):
                    o = psum[:, 6 + b // 2, (b % 2) * D:(b % 2 + 1) * D]
                    for c in range(KS):
                        mm = pe.matmul(o, sh[:, c, b * P:(b + 1) * P], wsd[:, c, :], start=c == 0, stop=c == KS - 1)
                    if b % 2:
                        mm.then_inc(s["sd_mm"], 1)

            def tile(t, first=False, last=False):
                dt_out(t, range(0, 2))
                if not last:
                    in_proj(t + 1, range(0, KI))
                dt_out(t, range(2, KI))
                if not first:
                    shared_up(t - 1, 0)
                if not last:
                    in_proj(t + 1, range(KI, KI + 2))
                out_proj(t)
                if not last:
                    in_proj(t + 1, range(KI + 2, 2 * KI))
                if not first:
                    shared_up(t - 1, 1)
                if not first and not last:
                    ranks(t - 1)
                if not last:
                    dt_in(t + 1)
                transposes(t)
                if last:
                    ranks(t - 1)
                if not first:
                    shared_down(t - 1)
                gate(t)

            pe.wait_ge(s["win_h"], 1)
            pe.wait_ge(s["win_l"], 1)
            in_proj(0, range(2 * KI))
            pe.wait_ge(s["w_x_in"], 32)
            dt_in(0)
            pe.wait_ge(s["wdt_h"], 1)
            pe.wait_ge(s["wdt_l"], 1)
            pe.wait_ge(s["w_out_in"], 16)
            pe.wait_ge(s["id_ready"], 1)
            pe.wait_ge(s["gw_h"], 1)
            pe.wait_ge(s["gw_l"], 1)
            tile(0, first=True)
            pe.wait_ge(s["tri_ready"], 1)
            pe.wait_ge(s["ones_ready"], 1)
            pe.wait_ge(s["wsgu_h"], 1)
            pe.wait_ge(s["wsgu_l"], 1)
            pe.wait_ge(s["w_sd_in"], 16)
            tile(1)
            with pe.Fori(2, NT - 1) as t:
                tile(t)
            tile(NT - 1, last=True)
            shared_up(NT - 1, 0)
            ranks(NT - 1)
            shared_up(NT - 1, 1)
            at_least(pe, "table_step", TABLE_STEPS)
            for i, v in enumerate((tile_ef, tile_row)):
                for c in range(TC):
                    n = min(P, NTILES - c * P)
                    mm = pe.matmul(psum[0:1, 3, i * NTILES + c * P:i * NTILES + c * P + n], v[:, c:c + 1],
                                   ident[:, 0:n], start=True, stop=True)
            mm.then_inc(s["table_mm"], 1)
            shared_down(NT - 1)

            def tile_experts(q):
                return table_values(pe, tile_e, q, E - 1)

            def turn_x(j, u):
                q, slot, turn, par = quad(j, u)
                at_least(pe, f"tile_in{slot}", 16 * SUB * (turn + 1))
                for k in range(KD):
                    at_least(pe, "t_l", KD * (q - 1) + k + 1)
                    for i in range(SUB):
                        mm = pe.transpose(psum[:, 2 + k, i * P:(i + 1) * P],
                                          tiles_in[:, slot, i, k * P:(k + 1) * P], ident[:, :])
                    mm.then_inc(s["t_mm"], 1)

            def gate_up(j, u, experts):
                q, slot, turn, par = quad(j, u)
                at_least(pe, "t_l", KD * (q + 1))
                at_least(pe, "e_mul", SUB * q)
                for i, e in enumerate(experts):
                    o = psum[:, i // 2, (i % 2) * 2 * I:(i % 2 + 1) * 2 * I]
                    r = slice(i * P, (i + 1) * P)
                    for k in range(KD):
                        w_hi, w_lo = (w[:, bass.ds(e, 1), k, :].squeeze(1) for w in (ew_gu_hi, ew_gu_lo))
                        pe.matmul(o, t_hi[par][:, k, r], w_hi, start=k == 0, stop=False)
                        pe.matmul(o, t_hi[par][:, k, r], w_lo, start=False, stop=False)
                        mm = pe.matmul(o, t_lo[par][:, k, r], w_hi, start=False, stop=k == KD - 1)
                mm.then_inc(s["gu_mm"], 1)

            def turn_act(j, u):
                q, slot, turn, par = quad(j, u)
                at_least(pe, "e_mul", SUB * (q + 1))
                at_least(pe, "a_l", q)
                for i in range(SUB):
                    mm = pe.transpose(psum[:, 4, i * P:(i + 1) * P], e_act[:, i, :], ident[:, :])
                mm.then_inc(s["at_mm"], 1)

            def down(j, u, experts):
                q, slot, turn, par = quad(j, u)
                if isinstance(q, int):
                    at_least(pe, "ew_lo", len(gu_parts) - GU_POOL + len(d_parts))
                at_least(pe, "a_l", q + 1)
                at_least(pe, "y_half0", q)
                at_least(pe, "y_half1", q)
                for i, e in enumerate(experts):
                    o = psum[:, 6 + i // 2, (i % 2) * D:(i % 2 + 1) * D]
                    r = slice(i * P, (i + 1) * P)
                    w_hi, w_lo = (w[:, bass.ds(e, 1), :].squeeze(1) for w in (ew_d_hi, ew_d_lo))
                    pe.matmul(o, a_hi[:, r], w_hi, start=True, stop=False)
                    pe.matmul(o, a_hi[:, r], w_lo, start=False, stop=False)
                    mm = pe.matmul(o, a_lo[:, r], w_hi, start=False, stop=True)
                    if i % 2:
                        mm.then_inc(s["y_mm"], 1)

            def iteration(j, u):
                q, left = RING * j + u, quads_left(j)
                if u + 2 < left:
                    turn_x(j, u + 2)
                if not is_first(j, u):
                    down(j, u - 1, tile_experts(q - 1))
                if u + 1 < left:
                    experts = tile_experts(q + 1)
                turn_act(j, u)
                if u + 1 < left:
                    gate_up(j, u + 1, experts)

            at_least(pe, "table_done", 2)
            at_least(pe, "res_done", 2 * NT)
            turn_x(0, 0)
            turn_x(0, 1)
            at_least(pe, "ew_lo", len(gu_parts) - GU_POOL)
            at_least(pe, "ew_lo_pool", GU_POOL)
            gate_up(0, 0, tile_experts(0))
            each_quad(pe, iteration)
            down(NQ // RING - 1, RING - 1, tile_experts(NQ - 1))

        @block.scalar
        def _(act):
            A = nc.scalar.activation

            def split_x(t):
                at_least(act, "xT_in", 16 * (t + 1))
                at_least(act, "s1_mm", 2 * KI * t)
                A(x_hi[:, :, :], xT[:, :, :], ACT.Copy).then_inc(s["x_hi_done"], 1)

            def conv_in(t, chunks):
                for c in chunks:
                    at_least(act, "s1_mm", 2 * KI * t + c + 1)
                    at_least(act, "halo_done", t + 1)
                    at_least(act, "m_done", KI * t)
                    at_least(act, "wx_mm", t)
                    A(xs[:, c, HALO:HALO + T], psum[:, c % 2, :], ACT.Copy)
                    A(xc[:, c, :], psum[:, c % 2, :], ACT.Identity, bias=cbias[:, c:c + 1],
                      scale=taps[:, c, HALO:HALO + 1]).then_inc(s["s1_evac"], 1)

            def taps_out(t, steps):
                for n in steps:
                    c, k = CONV_DVE + n // HALO, n % HALO
                    at_least(act, "s1_evac", 2 * KI * t + c + 1)
                    at_least(act, "m_done", KI * t)
                    at_least(act, "h_done", KS * (t - 2))
                    at_least(act, "sd_mm", 2 * (t - 2))
                    A(tap_out[n], xs[:, c, k:k + T], ACT.Copy, scale=taps[:, c, k:k + 1]).then_inc(s["tap_done"], 1)

            def silu_z(t, chunks):
                for c in chunks:
                    if c >= 2:
                        tap_added(act, t, len(tap_out) - KI + c + 1)
                    at_least(act, "s1_mm", 2 * KI * t + KI + c + 1)
                    at_least(act, "m_done", KI * t)
                    A(zs[:, c, :], psum[:, c % 2, :], ACT.Silu).then_inc(s["s1_evac"], 1)

            def silu_xc(t):
                for c in range(KI):
                    if c < CONV_DVE:
                        at_least(act, "conv_step", STEPS_DVE * t + HALO * (c + 1))
                    else:
                        at_least(act, "conv_step_pool", STEPS_POOL * t + HALO * (c - CONV_DVE + 1))
                    A(xc[:, c, :], xc[:, c, :], ACT.Silu).then_inc(s["xc_done"], 1)

            def dt_high(t):
                at_least(act, "wx_mm", t + 1)
                at_least(act, "wdt_mm", KI * t)
                A(dt[:, :], psum[0:2 * R, 2, :], ACT.Copy).then_inc(s["dt_hi"], 1)

            def exps(t, chunks):
                for c in chunks:
                    at_least(act, "wdt_mm", KI * t + c + 1)
                    at_least(act, "y_done", KI * t)
                    A(sp[:, c, :], psum[:, 4 + c % 2, :], ACT.Exp, bias=dtbias[:, c:c + 1]).then_inc(s["exp_done"], 1)

            def logs(t, chunks):
                for c in chunks:
                    at_least(act, "exp_clamped", KI * t + c + 1)
                    A(sp[:, c, :], sp[:, c, :], ACT.Ln, bias=1.0).then_inc(s["ln_done"], 1)

            def x1T_high(t):
                at_least(act, "xt_mm", t + 1)
                at_least(act, "sgu_mm", KS * t)
                A(x1T_hi[:, :, :], psum[:, 4:4 + KD, :], ACT.Copy).then_inc(s["x1T_h"], 1)

            def gate_exp(t):
                at_least(act, "gate_mm", t + 1)
                A(score[:, :, :], psum[:, 3, 0:SUB * E].rearrange("p (b e) -> p b e", e=E), ACT.Exp,
                  scale=-1.0).then_inc(s["gate_exp"], 1)

            def shared_silu(t, i):
                at_least(act, "sgu_mm", KS * t + i + 1)
                tap_added(act, t + 2, i + 1)
                A(sg[:, i, :], psum[:, 6, :], ACT.Silu).then_inc(s["ssilu"], 1)

            def copy_row(t, row=row):
                at_least(act, "x1_done", SUB * (t + 1))
                if row is not row_end:
                    at_least(act, "sent", 16 * SUB * TOP * t)
                A(row[:, :, 0:D], x1[:, :, :], ACT.Copy).then_inc(s["row_x"], 1)
                A(res[:, bass.ds(t * SUB, SUB), :], x1[:, :, :], ACT.Copy, scale=2.0).then_inc(s["x1_twice"], 1)

            def weights_high(i):
                at_least(act, "raw_in", 16 * 3 * E)
                at_least(act, "s1_mm", 2 * KI * NT)
                at_least(act, "m_done", KI * NT)
                at_least(act, "wx_mm", NT)
                A(ew_gu_hi[:, gu_parts[i], :, :], raw_gu[:, gu_parts[i], :, :], ACT.Copy).then_inc(s["ew_hi"], 1)

            def tile(t, first=False, last=False, more=True):
                exps(t, range(0, 2))
                if not last:
                    conv_in(t + 1, range(0, 1))
                logs(t, range(0, 2))
                if not last:
                    conv_in(t + 1, range(1, KI))
                exps(t, range(2, KI))
                if not last:
                    taps_out(t + 1, range(0, 1))
                logs(t, range(2, KI))
                if not last:
                    taps_out(t + 1, range(1, STEPS_POOL))
                if last:
                    weights_high(0)
                if not first:
                    shared_silu(t - 1, 0)
                if last:
                    weights_high(1)
                if not last:
                    silu_z(t + 1, range(0, 2))
                if not first:
                    copy_row(t - 1)
                if last:
                    weights_high(2)
                if not last:
                    silu_xc(t + 1)
                    silu_z(t + 1, range(2, KI))
                if not first:
                    shared_silu(t - 1, 1)
                if last:
                    weights_high(3)
                if more:
                    split_x(t + 2)
                if not last:
                    dt_high(t + 1)
                nc.scalar.preload_act_table_set("natural_log_exp_and_others")
                x1T_high(t)
                gate_exp(t)

            act.wait_ge(s["w_in_in"], 16)
            A(win_hi[:, :, :], win_f, ACT.Copy).then_inc(s["win_h"], 1)
            split_x(0)
            act.wait_ge(s["consts_in"], 64)
            conv_in(0, range(KI))
            silu_z(0, range(KI))
            silu_xc(0)
            act.wait_ge(s["w_dt_in"], 32)
            A(wdt_hi[:, :], wdt_f, ACT.Copy).then_inc(s["wdt_h"], 1)
            dt_high(0)
            act.wait_ge(s["gate_in"], 16)
            A(gw_hi[:, :, :], gw[:, :, :], ACT.Copy).then_inc(s["gw_h"], 1)
            act.wait_ge(s["w_sgu_in"], 32)
            A(wsgu_hi[:, :, :], wsgu_f, ACT.Copy).then_inc(s["wsgu_h"], 1)
            act.wait_ge(s["win_l"], 1)
            act.wait_ge(s["wdt_l"], 1)
            act.wait_ge(s["wsgu_l"], 1)
            split_x(1)
            nc.scalar.preload_act_table_set("natural_log_exp_and_others")
            tile(0, first=True)
            tile(1)
            with act.Fori(2, NT - 2) as t:
                tile(t)
            tile(NT - 2, more=False)
            tile(NT - 1, last=True, more=False)
            shared_silu(NT - 1, 0)
            copy_row(NT - 1, row_end)
            shared_silu(NT - 1, 1)

            at_least(act, "res_done", 2 * NT)
            for r in d_parts:
                A(ew_d_hi[:, r, :], raw_d[:, r, :], ACT.Copy).then_inc(s["ew_hi"], 1)

            def x_high(j, u, k):
                q, slot, turn, par = quad(j, u)
                at_least(act, "t_mm", KD * q + k + 1)
                at_least(act, "gu_mm", q - 1)
                A(t_hi[par][:, k, :], psum[:, 2 + k, :], ACT.Copy).then_inc(s["t_h"], 1)

            def gate_silu(j, u):
                q, slot, turn, par = quad(j, u)
                at_least(act, "gu_mm", q + 1)
                at_least(act, "e_mul", SUB * q)
                A(g_act[:, :, :], psum[:, 0:2, :].rearrange("p a (b i) -> p (a b) i", i=2 * I)[:, :, 0:I],
                  ACT.Silu).then_inc(s["g_silu"], 1)

            def act_high(j, u):
                q, slot, turn, par = quad(j, u)
                at_least(act, "at_mm", q + 1)
                at_least(act, "y_mm", 2 * q)
                A(a_hi[:, :], psum[:, 4, :], ACT.Copy).then_inc(s["a_h"], 1)

            def result(j, u):
                q, slot, turn, par = quad(j, u)
                at_least(act, "y_mm", 2 * q + 1)
                at_least(act, f"y_sent{par}", 16 * SUB * ((RING // 2) * j + u // 2))
                A(y_out[par][:, 0:2, :], psum[:, 6, :].rearrange("p (b d) -> p b d", d=D), ACT.Copy) \
                    .then_inc(s["y_half0"], 1)

            def iteration(j, u):
                gate_silu(j, u)
                if u + 2 < quads_left(j):
                    for k in range(KD):
                        x_high(j, u + 2, k)
                if not is_first(j, u):
                    result(j, u - 1)
                act_high(j, u)

            at_least(act, "ew_lo", len(gu_parts) - GU_POOL)
            at_least(act, "ew_lo_pool", GU_POOL)
            for u in range(2):
                for k in range(KD):
                    x_high(0, u, k)
            each_quad(act, iteration)
            result(NQ // RING - 1, RING - 1)

            def out_norm(j, h):
                at_least(act, "o_ready", 2 * j + h + 1)
                for i in range(SUB):
                    x2 = res[:, bass.ds(SUB * (2 * j + h) + i, 1), :].squeeze(1)
                    A(x2, x2, ACT.Identity, bias=o_shift[h][:, i:i + 1], scale=o_rstd[h][:, i:i + 1]) \
                        .then_inc(s["o_done"], 1)
                at_least(act, "o_done", SUB * (2 * j + h + 1))
                r = bass.ds(SUB * (2 * j + h), SUB)
                act.dma_start(out.rearrange("(n p) d -> p n d", p=P)[:, r, :], res[:, r, :]).then_inc(s["stored"], 16)

            with act.Fori(0, N // P // YR) as j:
                for h in range(2):
                    out_norm(j, h)

        @block.vector
        def _(dve):
            V = nc.vector

            def f32(ap):
                return ap.bitcast(F32)

            def inverse_root(v, neg_half, half_bits, y, h, name, n):
                def then(ins):
                    nonlocal n
                    n = n + 1
                    ins.then_inc(s[name], 1)
                    dve.wait_ge(s[name], n)
                V.tensor_scalar(neg_half, v, -0.5, None, ALU.mult).then_inc(s[name], 1)
                n = n + 1
                then(V.tensor_scalar(half_bits, v.bitcast(I32), 1, None, ALU.arith_shift_right))
                then(V.tensor_scalar(y.bitcast(I32), half_bits, -1.0, RSQRT_MAGIC, ALU.mult, ALU.add))
                for i in range(NEWTON):
                    then(V.tensor_tensor(h, y, y, ALU.mult))
                    then(V.tensor_tensor(h, h, neg_half, ALU.mult))
                    then(V.scalar_tensor_tensor(y, h, 1.5, y, ALU.add, ALU.mult))
                return n

            def halo(t):
                at_least(dve, "conv_step", STEPS_DVE * t)
                at_least(dve, "conv_step_pool", STEPS_POOL * t)
                at_least(dve, "s1_evac", 2 * KI * (t - 1) + KI)
                V.tensor_scalar(xs[:, :, 0:HALO], xs[:, :, T:T + HALO], keep[:, bass.ds(t, 1)], None, ALU.mult) \
                 .then_inc(s["halo_done"], 1)

            def conv(t, chunks):
                for c in chunks:
                    for k in range(HALO):
                        n = STEPS_DVE * t + HALO * c + k
                        if k == 0:
                            at_least(dve, "s1_evac", 2 * KI * t + c + 1)
                            at_least(dve, "halo_done", t + 1)
                        elif c < CONV_DVE:
                            at_least(dve, "conv_step", n)
                        else:
                            at_least(dve, "conv_step_pool", n - STEPS_DVE)
                        V.scalar_tensor_tensor(xc[:, c, :], xs[:, c, k:k + T], taps[:, c, k:k + 1], xc[:, c, :],
                                               ALU.mult, ALU.add).then_inc(s["conv_step"] if c < CONV_DVE else s["conv_step_pool"], 1)

            def dt_low(t):
                at_least(dve, "dt_hi", t + 1)
                V.tensor_tensor(dt[R:2 * R, :], psum[R:2 * R, 2, :], f32(dt[R:2 * R, :]), ALU.subtract) \
                 .then_inc(s["dt_lo"], 1)

            def clamp(t, chunks):
                for c in chunks:
                    at_least(dve, "exp_done", KI * t + c + 1)
                    V.tensor_scalar(sp[:, c, :], sp[:, c, :], EXP_MAX, None, ALU.min).then_inc(s["exp_clamped"], 1)

            def softplus(t, chunks):
                for c in chunks:
                    at_least(dve, "ln_done", KI * t + c + 1)
                    V.scalar_tensor_tensor(sp[:, c, :], psum[:, 4 + c % 2, :], dtbias[:, c:c + 1], sp[:, c, :],
                                           ALU.add, ALU.max).then_inc(s["sp_done"], 1)
                for c in chunks:
                    at_least(dve, "sp_done", KI * t + c + 1)
                    at_least(dve, "m_done", KI * t + c + 1)
                    V.tensor_tensor(m[:, c, :], m[:, c, :], sp[:, c, :], ALU.mult).then_inc(s["y_done"], 1)

            def layer_norm(t):
                at_least(dve, "xtok_in", 16 * (t + 1))
                at_least(dve, "row_x", t)
                at_least(dve, "x1_twice", t)
                for h in range(2):
                    at_least(dve, "wout_mm", 2 * t + h + 1)
                    V.scalar_tensor_tensor(x1[:, 2 * h:2 * h + 2, :], xtok[:, 2 * h:2 * h + 2, :], 2.0,
                                           psum[:, 4 + h, :].rearrange("p (b d) -> p b d", d=D),
                                           ALU.mult, ALU.add).then_inc(s["ln_in"], 1)
                for b in range(SUB):
                    at_least(dve, "ln_in", 2 * t + b // 2 + 1)
                    V.bn_stats(stats[:, b, :], x1[:, b, :]).then_inc(s["bn"], 1)
                for b in range(SUB):
                    at_least_alone(dve, "bn", SUB * t + b + 1)
                    V.bn_aggr(mv[:, b, :], stats[:, b, :]).then_inc(s["bn_mv"], 1)
                dve.wait_ge(s["bn_mv"], SUB * (t + 1))
                n = NORM_STEPS * t
                V.tensor_scalar(var[:, :], mv[:, :, 1], EPS, None, ALU.add).then_inc(s["norm_step"], 1)
                dve.wait_ge(s["norm_step"], n + 1)
                inverse_root(var[:, :], neg_half[:, :], half_bits[:, :], rstd[:, :], newton[:, :], "norm_step", n + 1)
                for b in range(SUB):
                    V.tensor_scalar(x1[:, b, :], x1[:, b, :], mv[:, b, 0:1], rstd[:, b:b + 1],
                                    ALU.subtract, ALU.mult).then_inc(s["x1_done"], 1)

            def x1T_low(t):
                at_least(dve, "x1T_h", t + 1)
                V.tensor_tensor(x1T_lo[:, :, :], psum[:, 4:4 + KD, :], f32(x1T_hi[:, :, :]), ALU.subtract) \
                 .then_inc(s["x1T_l"], 1)

            def shared_act(t, i):
                at_least(dve, "ssilu", KS * t + i + 1)
                tap_added(dve, t + 2, KS + i + 1)
                at_least(dve, "sd_mm", 2 * t)
                V.tensor_tensor(sh[:, i, :], sg[:, i, :], psum[:, 7, :], ALU.mult).then_inc(s["h_done"], 1)

            def residual(t):
                for h in range(2):
                    at_least(dve, "sd_mm", 2 * t + h + 1)
                    at_least(dve, "x1_twice", t + 1)
                    r = res[:, bass.ds(t * SUB + 2 * h, 2), :]
                    V.tensor_tensor(r, r, psum[:, 6 + h, :].rearrange("p (b d) -> p b d", d=D), ALU.add) \
                     .then_inc(s["res_done"], 1)

            done = [0]
            STEPS = 45

            def step(ins, t, wait=True, alone=False):
                done[0] += 1
                ins.then_inc(s["route_step"], 1)
                if wait:
                    (at_least_alone if alone else at_least)(dve, "route_step", STEPS * t + done[0])

            def flat(ap):
                return ap.rearrange("p b e -> p (b e)")

            def route(t):
                done[0] = 0
                dve.wait_ge(s["gate_exp"], t + 1)
                step(V.tensor_scalar(flat(sfc[:, :, :]), flat(score[:, :, :]), 1.0, None, ALU.add), t)
                step(V.reciprocal(flat(score[:, :, :]), flat(sfc[:, :, :])), t)
                step(V.tensor_tensor(sfc[:, :, :], score[:, :, :],
                                     gbias[:, :].unsqueeze(1).to_broadcast([P, SUB, E]), ALU.add), t)
                grp = flat(sfc[:, :, :]).rearrange("p (g j k) -> p g j k", j=2, k=2)
                mx, mn = (v[:, :, :, :].rearrange("p b g k -> p (b g) k") for v in (pmx, pmn))
                step(V.tensor_tensor(mx, grp[:, :, 0, :], grp[:, :, 1, :], ALU.max), t, False)
                step(V.tensor_tensor(mn, grp[:, :, 0, :], grp[:, :, 1, :], ALU.min), t)
                step(V.tensor_tensor(g1[:, :], mx[:, :, 0], mx[:, :, 1], ALU.max), t, False)
                step(V.tensor_tensor(g2[:, :], mx[:, :, 0], mx[:, :, 1], ALU.min), t, False)
                step(V.tensor_tensor(g3[:, :], mn[:, :, 0], mn[:, :, 1], ALU.max), t)
                step(V.tensor_tensor(g2[:, :], g2[:, :], g3[:, :], ALU.max), t)
                step(V.tensor_tensor(gsc[:, :], g1[:, :], g2[:, :], ALU.add), t)

            def pick(t):
                gs = gsc[:, :].rearrange("p (b g) -> p b g", g=NG)
                one, other = (gs.unsqueeze(a).to_broadcast([P, SUB, NG, NG]) for a in (3, 2))
                ca, cb = (v[:, :, :, :] for v in (cmp_a, cmp_b))
                step(V.tensor_tensor(ca, other, one, ALU.is_gt), t, False)
                step(V.tensor_tensor(cb, other, one, ALU.is_equal), t)
                step(V.tensor_tensor(cb, cb, before[:, :, :].unsqueeze(1).to_broadcast([P, SUB, NG, NG]), ALU.mult), t)
                step(V.tensor_tensor(ca, ca, cb, ALU.add), t)
                step(V.tensor_reduce(g1[:, :], ca.rearrange("p b g k -> p (b g) k"), axis=AX_X, op=ALU.add), t)
                step(V.tensor_scalar(gkeep[:, :], g1[:, :], float(GROUPS_KEPT), None, ALU.is_lt), t)
                step(V.tensor_scalar(gpen[:, :], gkeep[:, :], 1.0, LOWEST, ALU.subtract, ALU.mult), t, False)
                pk = picked[:, :, :].rearrange("p b (g j) -> p (b g) j", j=EG)
                sf = sfc[:, :, :].rearrange("p b (g j) -> p (b g) j", j=EG)
                step(V.tensor_tensor(pk, sf, gkeep[:, :].unsqueeze(2).to_broadcast([P, SUB * NG, EG]), ALU.mult), t)
                step(V.tensor_tensor(pk, pk, gpen[:, :].unsqueeze(2).to_broadcast([P, SUB * NG, EG]), ALU.add),
                     t, alone=True)
                for b in range(SUB):
                    step(V.max(top8[:, b, :], picked[:, b, :]), t, b == SUB - 1)

            def choose(t, row=row):
                fourth = top8[:, :, TOP - 1:TOP].to_broadcast([P, SUB, E])
                step(V.tensor_tensor(above[:, :, :], picked[:, :, :], fourth, ALU.is_gt), t, False)
                step(V.tensor_tensor(equal[:, :, :], picked[:, :, :], fourth, ALU.is_equal), t)
                step(V.tensor_reduce(nabove[:, :], above[:, :, :], axis=AX_X, op=ALU.add), t, False)
                step(V.tensor_tensor_scan(flat(posn[:, :, :]), flat(block_start[:, :, :]), flat(equal[:, :, :]), 0.0,
                                          ALU.mult, ALU.add), t)
                step(V.tensor_tensor(posn[:, :, :], posn[:, :, :],
                                     nabove[:, :].unsqueeze(2).to_broadcast([P, SUB, E]), ALU.add), t)
                step(V.scalar_tensor_tensor(posn[:, :, :], posn[:, :, :], float(TOP), equal[:, :, :],
                                            ALU.is_le, ALU.mult), t)
                step(V.tensor_tensor(sel[:, :, :], posn[:, :, :], above[:, :, :], ALU.add), t)
                V.tensor_copy(sel16[:, :, :], sel[:, :, :]).then_inc(s["sel_done"], 1)
                step(V.tensor_tensor(wsel[:, :, :], score[:, :, :], sel[:, :, :], ALU.mult), t, False)
                step(V.tensor_tensor_scan(flat(slots[:, :, :]), flat(ones_f[:, :, :]), flat(sel[:, :, :]), 0.0,
                                          ALU.mult, ALU.add), t)
                step(V.tensor_reduce(wsum[:, :], wsel[:, :, :], axis=AX_X, op=ALU.add), t)
                step(V.tensor_scalar(wsum[:, :], wsum[:, :], 1e-20, None, ALU.add), t)
                step(V.reciprocal(nabove[:, :], wsum[:, :]), t)
                if row is not row_end:
                    at_least(dve, "sent", 16 * SUB * TOP * t)
                step(V.scalar_tensor_tensor(row[:, :, D:D + E], wsel[:, :, :], SCALE,
                                            nabove[:, :].unsqueeze(2).to_broadcast([P, SUB, E]),
                                            ALU.mult, ALU.mult), t, False)
                step(V.scalar_tensor_tensor(row[:, :, D + E:ROW], slots[:, :, :], float(N),
                                            tok_row[:, :].unsqueeze(2).to_broadcast([P, SUB, E]),
                                            ALU.mult, ALU.add), t)
                step(V.tensor_scalar(tok_row[:, :], tok_row[:, :], float(T), None, ALU.add), t)

            def place(t, row_id=row_id):
                dve.wait_ge(s["rank_mm"], t + 1)
                rank = psum[:, 3, SUB * E:2 * SUB * E].rearrange("p (b e) -> p b e", e=E)
                step(V.tensor_tensor(posn[:, :, :], rank, counts[:, :].unsqueeze(1).to_broadcast([P, SUB, E]),
                                     ALU.add), t)
                step(V.tensor_tensor(counts[:, :], counts[:, :], psum[:, 3, 2 * SUB * E:(2 * SUB + 1) * E],
                                     ALU.add), t)
                step(V.scalar_tensor_tensor(posn[:, :, :], posn[:, :, :], 1.0, sel[:, :, :],
                                            ALU.add, ALU.mult), t, alone=True)
                for b in range(SUB):
                    step(V.max(pos8[:, b, :], posn[:, b, :]), t, b == SUB - 1)
                V.tensor_scalar(row_id[:, :, :], pos8[:, :, 0:TOP], 1.0, None, ALU.subtract).then_inc(s["routed"], 1)
                assert done[0] == STEPS, done[0]

            def table():
                n = [0]

                def then(ins):
                    n[0] += 1
                    ins.then_inc(s["table_step"], 1)
                    dve.wait_ge(s["table_step"], n[0])
                V.tensor_copy(pad_at[:, :], counts[0:1, :]).then_inc(s["pad_at_done"], 1)
                then(V.tensor_tensor(ntile[:, :], counts[:, :], region[:, :], ALU.subtract))
                then(V.tensor_scalar(ntile_i[:, :], ntile[:, :], float(P - 1), None, ALU.add))
                then(V.tensor_scalar(ntile_i[:, :], ntile_i[:, :], P.bit_length() - 1, None, ALU.arith_shift_right))
                then(V.tensor_copy(ends[0][:, 8:8 + E], ntile_i[:, :]))
                then(V.tensor_scalar(row_step[:, :], ends[0][:, 8:8 + E], -float(P), float(CAP), ALU.mult, ALU.add))
                for i, d in enumerate((1, 2, 4, 8)):
                    a, b = ends[(0, 1, 2, 1)[i]], ends[(1, 2, 1, 2)[i]]
                    then(V.tensor_tensor(b[:, 8:8 + E], a[:, 8:8 + E], a[:, 8 - d:8 - d + E], ALU.add))
                S2 = [P, TC, E]
                then(V.tensor_tensor(is_past[:, :, :], tile_no[:, :].unsqueeze(2).to_broadcast(S2),
                                     ends[2][:, 8:8 + E].unsqueeze(1).to_broadcast(S2), ALU.is_ge))
                then(V.tensor_tensor(past_step[:, :, :], is_past[:, :, :],
                                     row_step[:, :].unsqueeze(1).to_broadcast(S2), ALU.mult))
                then(V.tensor_reduce(tile_ef[:, :], is_past[:, :, :], axis=AX_X, op=ALU.add))
                then(V.tensor_scalar(tile_ef[:, :], tile_ef[:, :], float(E - 1), None, ALU.min))
                then(V.tensor_reduce(tile_row[:, :], past_step[:, :, :], axis=AX_X, op=ALU.add))
                then(V.scalar_tensor_tensor(tile_row[:, :], tile_no[:, :], float(P), tile_row[:, :], ALU.mult, ALU.add))
                then(V.tensor_scalar(tile_row[:, :], tile_row[:, :], float(IDLE), None, ALU.min))
                assert n[0] == TABLE_STEPS, n[0]

            def weights_low(i):
                at_least(dve, "ew_hi", i + 1)
                at_least(dve, "wout_mm", 2 * NT)
                r = gu_parts[i]
                V.tensor_tensor(ew_gu_lo[:, r, :, :], raw_gu[:, r, :, :], f32(ew_gu_hi[:, r, :, :]), ALU.subtract) \
                 .then_inc(s["ew_lo"], 1)

            def tile(t, first=False, last=False, more=True):
                if not last:
                    halo(t + 1)
                if not first:
                    route(t - 1)
                clamp(t, range(0, 2))
                if not first:
                    pick(t - 1)
                softplus(t, range(0, 2))
                if not last:
                    conv(t + 1, range(0, 1))
                clamp(t, range(2, KI))
                softplus(t, range(2, KI))
                if not last:
                    conv(t + 1, range(1, 2))
                if not first:
                    shared_act(t - 1, 0)
                    if not last:
                        choose(t - 1)
                layer_norm(t)
                if not first:
                    shared_act(t - 1, 1)
                    if last:
                        choose(t - 1)
                    place(t - 1)
                if not last:
                    dt_low(t + 1)
                x1T_low(t)
                if not first:
                    residual(t - 1)

            dve.wait_ge(s["win_h"], 1)
            V.tensor_tensor(win_lo[:, :, :], win_f, f32(win_hi[:, :, :]), ALU.subtract).then_inc(s["win_l"], 1)
            V.memset(keep[:, :], 1.0).then_inc(s["keep_one"], 1)
            V.memset(xs[:, :, T:T + HALO], 0.0).then_inc(s["keep_one"], 1)
            dve.wait_ge(s["keep_one"], 2)
            for t in range(0, NT, seq_len // T):
                V.memset(keep[:, t:t + 1], 0.0).then_inc(s["keep_ready"], 1)
            V.memset(ones_f[:, :, :], 1.0).then_inc(s["pre_zero"], 1)
            V.memset(block_start[:, :, 1:E], 1.0).then_inc(s["pre_zero"], 1)
            V.memset(block_start[:, :, 0:1], 0.0).then_inc(s["pre_zero"], 1)
            for v in ends:
                V.memset(v[:, 0:8], 0.0).then_inc(s["pre_zero"], 1)
            dve.wait_ge(s["keep_ready"], N // seq_len)
            dve.wait_ge(s["consts_in"], 64)
            halo(0)
            conv(0, range(KI))
            dve.wait_ge(s["wdt_h"], 1)
            V.tensor_tensor(wdt_lo[:, :], wdt_f[0:R, :], f32(wdt_hi[0:R, :]), ALU.subtract).then_inc(s["wdt_l"], 1)
            dt_low(0)
            dve.wait_ge(s["gw_h"], 1)
            V.tensor_tensor(gw_lo[:, :, :], gw[:, :, :], f32(gw_hi[:, :, :]), ALU.subtract).then_inc(s["gw_l"], 1)
            dve.wait_ge(s["wsgu_h"], 1)
            V.tensor_tensor(wsgu_lo[:, :, :], wsgu_f, f32(wsgu_hi[:, :, :]), ALU.subtract).then_inc(s["wsgu_l"], 1)
            dve.wait_ge(s["before_ready"], 1)
            dve.wait_ge(s["const_ready"], 4)
            dve.wait_ge(s["pre_zero"], 3 + len(ends))
            tile(0, first=True)
            tile(1)
            with dve.Fori(2, NT - 2) as t:
                tile(t)
            tile(NT - 2, more=False)
            tile(NT - 1, last=True, more=False)
            route(NT - 1)
            pick(NT - 1)
            choose(NT - 1, row_end)
            place(NT - 1, row_id_end)
            table()
            shared_act(NT - 1, 0)
            for i in range(GU_POOL, len(gu_parts)):
                weights_low(i)
            shared_act(NT - 1, 1)
            residual(NT - 1)
            at_least(dve, "table_mm", 1)
            V.tensor_copy(tile_e[:, :], psum[0:1, 3, 0:NTILES]).then_inc(s["table_done"], 1)
            V.tensor_copy(tile_at[:, :], psum[0:1, 3, NTILES:2 * NTILES]).then_inc(s["table_done"], 1)
            for i, r in enumerate(d_parts):
                at_least(dve, "ew_hi", len(gu_parts) + i + 1)
                V.tensor_tensor(ew_d_lo[:, r, :], raw_d[:, r, :], f32(ew_d_hi[:, r, :]), ALU.subtract) \
                 .then_inc(s["ew_lo"], 1)

            def tile_experts(q):
                return table_values(dve, tile_e, q, E - 1)

            def x_low(j, u, k):
                q, slot, turn, par = quad(j, u)
                at_least(dve, "t_h", KD * q + k + 1)
                V.tensor_tensor(t_lo[par][:, k, :], psum[:, 2 + k, :], f32(t_hi[par][:, k, :]), ALU.subtract) \
                 .then_inc(s["t_l"], 1)

            def weigh(j, u):
                q, slot, turn, par = quad(j, u)
                up = psum[:, 0:2, :].rearrange("p a (b i) -> p (a b) i", i=2 * I)
                experts = tile_experts(q)
                at_least(dve, "g_silu", q + 1)
                at_least(dve, "at_mm", q)
                for i, e in enumerate(experts):
                    V.scalar_tensor_tensor(e_act[:, i, :], g_act[:, i, :], tiles_in[:, slot, i, bass.ds(D + e, 1)],
                                           up[:, i, I:2 * I], ALU.mult, ALU.mult).then_inc(s["e_mul"], 1)
                return experts

            def result_rows(j, u, experts):
                q, slot, turn, par = quad(j, u)
                at_least(dve, f"y_sent{par}", 16 * SUB * (RING // 2 * (turn - 1) + slot // 2 + 1))
                for i, e in enumerate(experts):
                    V.tensor_copy(y_id[slot][:, i:i + 1], tiles_in[:, slot, i, bass.ds(D + E + e, 1)]) \
                     .then_inc(s["y_id_done"], 1)

            def act_low(j, u):
                q, slot, turn, par = quad(j, u)
                at_least(dve, "a_h", q + 1)
                V.tensor_tensor(a_lo[:, :], psum[:, 4, :], f32(a_hi[:, :]), ALU.subtract).then_inc(s["a_l"], 1)

            def result(j, u):
                q, slot, turn, par = quad(j, u)
                at_least(dve, f"y_sent{par}", 16 * SUB * ((RING // 2) * j + u // 2))
                at_least(dve, "y_mm", 2 * q + 2)
                V.tensor_copy(y_out[par][:, 2:4, :], psum[:, 7, :].rearrange("p (b d) -> p b d", d=D)) \
                 .then_inc(s["y_half1"], 1)

            def iteration(j, u):
                experts = weigh(j, u)
                if u + 2 < quads_left(j):
                    for k in range(KD):
                        x_low(j, u + 2, k)
                if not is_first(j, u):
                    result(j, u - 1)
                act_low(j, u)
                result_rows(j, u, experts)

            for u in range(2):
                for k in range(KD):
                    x_low(0, u, k)
            each_quad(dve, iteration)
            result(NQ // RING - 1, RING - 1)

            def sums(j, h):
                g = 2 * j + h
                x2 = [res[:, bass.ds(SUB * g + i, 1), :].squeeze(1) for i in range(SUB)]
                for i in range(SUB):
                    y = y_in[h * SUB + i]
                    at_least(dve, "y_paired", SUB * g + i + 1)
                    V.tensor_tensor(y[:, 0, :], y[:, 0, :], y[:, 1, :], ALU.add).then_inc(s["y_summed"], 1)
                for i in range(SUB):
                    at_least(dve, "y_summed", SUB * g + i + 1)
                    V.tensor_tensor(x2[i], x2[i], y_in[h * SUB + i][:, 0, :], ALU.add) \
                     .then_inc(s[f"y_used{h * SUB + i}"], 1)
                for i in range(SUB):
                    at_least_alone(dve, f"y_used{h * SUB + i}", j + 1)
                    V.bn_stats(o_stats[:, i, :], x2[i]).then_inc(s["o_bn"], 1)
                for i in range(SUB):
                    at_least_alone(dve, "o_bn", SUB * g + i + 1)
                    V.bn_aggr(o_mv[:, i, :], o_stats[:, i, :]).then_inc(s["o_agg"], 1)

            def norm(j, h):
                g = 2 * j + h
                n = NORM_STEPS * g
                at_least(dve, "o_agg", SUB * (g + 1))
                V.tensor_scalar(o_var[:, :], o_mv[:, :, 1], EPS, None, ALU.add).then_inc(s["o_norm"], 1)
                dve.wait_ge(s["o_norm"], n + 1)
                at_least(dve, "o_done", SUB * (g - 1))
                inverse_root(o_var[:, :], o_neg_half[:, :], o_half_bits[:, :], o_rstd[h][:, :], o_newton[:, :],
                             "o_norm", n + 1)
                V.scalar_tensor_tensor(o_shift[h][:, :], o_mv[:, :, 0], -1.0, o_rstd[h][:, :], ALU.mult, ALU.mult) \
                 .then_inc(s["o_ready"], 1)

            def body(j):
                for h in range(2):
                    sums(j, h)
                    norm(j, h)
            body(0)
            with dve.Fori(1, N // P // YR) as j:
                body(j)


_ORDER = ("x_tok x_T w_in_T conv_w conv_b w_x_T w_dt_T b_dt w_out_T gate_w_T gate_bias "
          "wg_T wu_T wd_T ws_g_T ws_u_T ws_d_T").split()


def kernel(L0_attn_x, L0_attn_W_in, L0_attn_conv_w, L0_attn_conv_b, L0_attn_W_x, L0_attn_W_dt, L0_attn_b_dt,
           L0_attn_W_out, L0_ffn_gate_w, L0_ffn_gate_bias, L0_ffn_Wg, L0_ffn_Wu, L0_ffn_Wd, L0_ffn_Ws_g,
           L0_ffn_Ws_u, L0_ffn_Ws_d):
    import numpy as np
    import concourse.bacc as bacc
    from concourse import mybir as mb
    from concourse.bass_utils import run_bass_kernel_spmd

    x = np.asarray(L0_attn_x)
    batch, seq, d = x.shape
    x = x.reshape(batch * seq, d)
    per_channel = lambda v: np.asarray(v).reshape(-1, 128).T
    laid = {
        "x_tok": x, "x_T": x.T,
        "w_in_T": np.asarray(L0_attn_W_in).T,
        "conv_w": np.asarray(L0_attn_conv_w).reshape(-1, 128, 4).transpose(1, 0, 2),
        "conv_b": per_channel(L0_attn_conv_b),
        "w_x_T": np.asarray(L0_attn_W_x).T,
        "w_dt_T": np.asarray(L0_attn_W_dt).T,
        "b_dt": per_channel(L0_attn_b_dt),
        "w_out_T": np.asarray(L0_attn_W_out).T,
        "gate_w_T": np.asarray(L0_ffn_gate_w).T,
        "gate_bias": np.asarray(L0_ffn_gate_bias).reshape(1, -1),
        "wg_T": np.asarray(L0_ffn_Wg).transpose(0, 2, 1),
        "wu_T": np.asarray(L0_ffn_Wu).transpose(0, 2, 1),
        "wd_T": np.asarray(L0_ffn_Wd).transpose(0, 2, 1),
        "ws_g_T": np.asarray(L0_ffn_Ws_g).T,
        "ws_u_T": np.asarray(L0_ffn_Ws_u).T,
        "ws_d_T": np.asarray(L0_ffn_Ws_d).T,
    }
    nc = bacc.Bacc("TRN2", target_bir_lowering=False, num_devices=1)
    arrays, args = {}, []
    for name in _ORDER:
        a = np.ascontiguousarray(laid[name])
        arrays[f"in_{name}"] = a
        args.append(nc.dram_tensor(f"in_{name}", a.shape, mb.dt.from_np(a.dtype), kind="ExternalInput").ap())
    out = nc.dram_tensor("out_dram", x.shape, mb.dt.from_np(x.dtype), kind="ExternalOutput").ap()
    mamba_moe(nc, *args, out, seq)
    got = run_bass_kernel_spmd(nc, [arrays], core_ids=[0]).results[0]["out_dram"]
    return got.reshape(batch, seq, d)
```

```python
import concourse.bass as bass
from concourse import mybir
from contextlib import ExitStack

P = 128
F32 = mybir.dt.float32
F32R = mybir.dt.float32r
BF16 = mybir.dt.bfloat16
I32 = mybir.dt.int32
ALU = mybir.AluOpType
ACT = mybir.ActivationFunctionType
AX_X = mybir.AxisListType.X

EPS = 1e-5
SCALE = 2.5
TOP = 4
GROUPS_KEPT = 2
LOWEST = 3e38
RSQRT_MAGIC = float(0x5F3759DF)
NEWTON = 3
EXP_MAX = 2.0 ** 60


def mamba_moe(nc, x_tok, x_T, w_in_T, conv_w, conv_b, w_x_T, w_dt_T, b_dt, w_out_T,
              gate_w_T, gate_bias, wg_T, wu_T, wd_T, ws_g_T, ws_u_T, ws_d_T, out, seq_len):
    N, D = x_tok.shape
    DI = w_in_T.shape[1] // 2
    R = w_dt_T.shape[0]
    TAPS = conv_w.shape[2]
    E, _, I = wg_T.shape
    SH = ws_d_T.shape[0]
    T = 512
    NT = N // T
    SUB = T // P
    KD, KI, KS = D // P, DI // P, SH // P
    NG = 4
    EG = E // NG
    ROW = D + 2 * E
    HALVES = 2
    HT = NT // HALVES
    CAP = N // HALVES + P
    IDLE = E * CAP
    HALF = IDLE + P
    RING = 4
    HTILES = -(-(N // HALVES * TOP // P + E) // (SUB * RING)) * SUB * RING
    NTILES = HALVES * HTILES
    HALO = TAPS - 1

    x_buf = nc.dram_tensor("x_buf", (HALVES * HALF, ROW), F32).ap()
    y_buf = nc.dram_tensor("y_buf", (TOP * N, D), F32).ap()

    with ExitStack() as ctx:
        def sb(name, shape, dt=F32, scope=ctx):
            return scope.enter_context(nc.sbuf_tensor(name, shape, dt))

        def sem(name):
            return ctx.enter_context(nc.semaphore(name))

        psum = ctx.enter_context(nc.psum_tensor("psum", [P, 8, T], F32))

        res = sb("res", [P, N // P, D])
        ident = sb("ident", [P, P])
        counts = sb("counts", [P, NT + HALVES, E])
        pad_row = sb("pad_row", [P, ROW])
        region = sb("region", [P, E])
        ntile_i = sb("ntile_i", [P, E], I32)
        row_step = sb("row_step", [P, E])
        ends = [sb(f"ends{i}", [P, 8 + E]) for i in range(3)]
        tile_no = sb("tile_no", [P, 1])
        ntile, is_past, past_step = (ends[i][:, 8:8 + E] for i in (2, 0, 1))
        tile_ef, tile_row = sb("tile_ef", [P, 1]), sb("tile_row", [P, 1])
        tile_e = sb("tile_e", [1, NTILES], I32)
        tile_at = sb("tile_at", [1, NTILES], I32)
        pad_at = sb("pad_at", [1, HALVES * E], I32)

        row, row_end = sb("row", [P, SUB, ROW]), sb("row_end", [P, SUB, ROW])
        xtok = row_end[:, :, 0:D]
        row_id, row_id_end = (sb(n, [P, SUB, TOP], I32) for n in ("row_id", "row_id_end"))
        NORMED = N // HALVES // P
        o_stats = row[:, 0, 0:6 * NORMED].rearrange("p (b s) -> p b s", s=6)
        o_mv = row[:, 0, 6 * NORMED:8 * NORMED].rearrange("p (b s) -> p b s", s=2)
        o_var, o_neg_half, o_newton, o_half_bits = (row[:, 0, i * NORMED:(i + 1) * NORMED] for i in range(8, 12))
        o_half_bits = o_half_bits.bitcast(I32)
        o_rstd, o_shift = ([row[:, 1, i * NORMED:(i + 1) * NORMED] for i in v] for v in ((0, 1), (2, 3)))
        assert 12 * NORMED <= ROW

        p0 = ExitStack()
        raw_gu = sb("raw_gu", [P, E, KD, 2 * I], F32, p0)
        raw_d = sb("raw_d", [P, E, D], F32, p0)
        p1sb = lambda name, shape, dt=F32: sb(name, shape, dt, p0)
        win_hi, win_lo = (p1sb(n, [P, KD, 2 * DI], F32R) for n in ("win_hi", "win_lo"))
        xT = p1sb("xT", [P, KD, T])
        x_hi, x_lo = (p1sb(n, [P, KD, T], F32R) for n in ("x_hi", "x_lo"))
        xs = p1sb("xs", [P, KI, HALO + T])
        xc = p1sb("xc", [P, KI, T])
        zs = p1sb("zs", [P, KI, T])
        m = p1sb("m", [P, KI, T])
        sp = p1sb("sp", [P, KI, T])
        wx = p1sb("wx", [P, KI, 2 * R])
        wdt_hi = p1sb("wdt_hi", [2 * R, DI], F32R)
        wdt_lo = p1sb("wdt_lo", [R, DI], F32R)
        wout = p1sb("wout", [P, KI, D])
        dt = p1sb("dt", [2 * R, T], F32R)
        x1 = p1sb("x1", [P, SUB, D])
        x1T_hi, x1T_lo = (p1sb(n, [P, KD, T], F32R) for n in ("x1T_hi", "x1T_lo"))
        gw = p1sb("gw", [P, KD, E])
        gw_split = p1sb("gw_split", [P, KD, 2 * E], F32R)
        gw_hi, gw_lo = (gw_split[:, :, i * E:(i + 1) * E] for i in range(2))
        wsgu_hi, wsgu_lo = (p1sb(n, [P, KD, 2 * SH], F32R) for n in ("wsgu_hi", "wsgu_lo"))
        wsd = p1sb("wsd", [P, KS, D])
        cw_taps = p1sb("cw_taps", [P, KI, TAPS])
        cbias = p1sb("cbias", [P, KI])
        dtbias = p1sb("dtbias", [P, KI])
        gbias = p1sb("gbias", [P, E])
        keep = p1sb("keep", [P, NT])
        tri = p1sb("tri", [P, P], BF16)
        ones = p1sb("ones", [P, P], BF16)
        before = p1sb("before", [P, NG, NG])
        tok_row = p1sb("tok_row", [P, SUB])

        sg = p1sb("sg", [P, KS, T])
        sh = p1sb("sh", [P, KS, T])
        stats = p1sb("stats", [P, SUB, 6])
        mv = p1sb("mv", [P, SUB, 2])
        var, neg_half, rstd, newton = (p1sb(n, [P, SUB]) for n in ("var", "neg_half", "rstd", "newton"))
        half_bits = p1sb("half_bits", [P, SUB], I32)
        S3 = [P, SUB, E]
        score, sfc, picked = p1sb("score", S3), p1sb("sfc", S3), p1sb("picked", S3)
        above, equal, sel, posn = (p1sb(n, S3) for n in ("above", "equal", "sel", "posn"))
        wsel, slots = equal, picked
        sel16 = p1sb("sel16", S3, BF16)
        pmx, pmn = p1sb("pmx", [P, SUB, NG, 2]), p1sb("pmn", [P, SUB, NG, 2])
        g1, g2, g3, gsc = (p1sb(n, [P, SUB * NG]) for n in ("g1", "g2", "g3", "gsc"))
        cmp_a, cmp_b = (v[:, :, :].rearrange("p b (g k) -> p b g k", k=NG) for v in (above, posn))
        assert E == NG * NG
        gkeep, gpen = p1sb("gkeep", [P, SUB * NG]), p1sb("gpen", [P, SUB * NG])
        top8 = p1sb("top8", [P, SUB, 8])
        pos8 = top8
        nabove, wsum = p1sb("nabove", [P, SUB]), p1sb("wsum", [P, SUB])
        ones_f = p1sb("ones_f", S3)
        block_start = p1sb("block_start", S3)

        p0.close()

        p2 = ctx.enter_context(ExitStack())
        p2sb = lambda name, shape, dt=F32: sb(name, shape, dt, p2)
        t_hi, t_lo = ([p2sb(f"{n}{i}", [P, KD, T], F32R) for i in range(2)] for n in ("t_hi", "t_lo"))
        g_act = p2sb("g_act", [P, SUB, I])
        e_act = p2sb("e_act", [P, SUB, I])
        a_hi, a_lo = p2sb("a_hi", [P, T], F32R), p2sb("a_lo", [P, T], F32R)
        y_out = [p2sb(f"y_out{i}", [P, SUB, D]) for i in range(2)]
        assert 4 * KD * T + 2 * SUB * I + 2 * T + 2 * SUB * D == E * KD * 2 * I
        ew_d_lo = p2sb("ew_d_lo", [P, E, D], F32R)
        ew_gu_hi, ew_gu_lo = (p2sb(n, [P, E, KD, 2 * I], F32R) for n in ("ew_gu_hi", "ew_gu_lo"))
        y_id = [p2sb(f"y_id{i}", [P, SUB], I32) for i in range(RING)]
        tiles_in = p2sb("tiles_in", [P, RING, SUB, ROW])
        ew_d_hi = p2sb("ew_d_hi", [P, E, D], F32R)
        y_in = [p2sb(f"y_in{i}", [P, TOP, D]) for i in range(SUB)]
        p2.close()
        p3 = ctx.enter_context(ExitStack())
        y_in += [sb(f"y_in{i}", [P, TOP, D], F32, p3) for i in range(SUB, 2 * SUB)]

        win_f = sp[:, :, :].rearrange("p a b -> p (a b)").rearrange("p (k n) -> p k n", k=KD)
        wsgu_f = sh[:, :, :]
        wdt_f = sg[0:2 * R, 0, :]

        names = """w_in_in w_x_in w_dt_in w_out_in gate_in w_sgu_in w_sd_in consts_in
            win_h win_l wdt_h wdt_l gw_h gw_l wsgu_h wsgu_l
            ones_ready keep_one keep_ready pre_zero id_zero id_ready tri_one tri_ready before_one before_ready const_ready
            xT_in xtok_in x_hi_done x_lo_done s1_mm s1_evac halo_done conv_step tap_done conv_step_pool xc_done m_done
            wx_mm dt_hi dt_lo wdt_mm exp_done exp_clamped ln_done sp_done y_done
            wout_mm ln_in bn bn_mv norm_step x1_done x1_twice xt_mm x1T_h x1T_l
            gate_mm gate_sum gate_exp route_step sel_done rank_mm routed row_x sent
            sgu_mm ssilu h_done sd_mm res_done
            raw_in table_step table_mm table_done pad_at_done pad_ready pads_out ew_hi ew_gu_low ew_d_low
            tile_in0 tile_in1 tile_in2 tile_in3 t_mm t_h t_l gu_mm g_silu e_mul at_mm a_h a_l y_mm
            y_evac y_id_done y_sent0_0 y_sent0_1 y_sent1_0 y_sent1_1
            y_in0 y_in1 y_in2 y_in3 y_in4 y_in5 y_in6 y_in7 y_paired
            y_used0 y_used1 y_used2 y_used3 y_used4 y_used5 y_used6 y_used7 y_paired_dve y_summed
            o_bn o_agg o_norm o_ready o_done stored""".split()
        s = {n: sem(n) for n in names}

        def at_least_alone(eng, name, n):
            if isinstance(n, int):
                return at_least(eng, name, n)
            n = eng.to_reg(n)
            eng.wait_ge(s["ones_ready"], 1)
            eng.wait_ge(s[name], n)

        def at_least(eng, name, n):
            if isinstance(n, int) and n <= 0:
                return
            eng.wait_ge(s[name], n)

        TABLE_STEPS = 16

        def table_bank(h, i):
            at = (3 * SUB + 1) * E + i * HTILES
            return psum[0:1, (3, 5)[h], at:at + HTILES]

        NORM_STEPS = 4 + 3 * NEWTON
        NQ = NTILES // SUB

        def quad(j, u):
            return RING * j + u, u % RING, j + u // RING, u % 2

        def table_values(eng, table, q, most):
            return nc.values_load_multi_w_load_instructions(
                table[0:1, bass.ds(SUB * q, SUB)], engines=(eng.engine,), min_val=0, max_val=most,
                skip_runtime_bounds_check_because="the table is clamped to these bounds")[1]

        def quads_left(j):
            return RING if isinstance(j, int) and j == NB - 1 else 2 * RING

        def is_first(j, u):
            return isinstance(j, int) and j == 0 and u == 0

        HQ, HB = HTILES // SUB, HTILES // SUB // RING
        NB = HALVES * HB
        HG = HT
        assert HB > HG

        def half_of(j, u):
            return ((j if isinstance(j, int) else j.min_val) * RING + u) // HQ

        def group_of(j):
            return j - (NB - HG)

        def each_quad(eng, iteration):
            def body(j):
                for u in range(RING):
                    iteration(j, u)
            body(0)
            with eng.Fori(1, HB) as j:
                body(j)
            for j in range(HB, NB - HG + 1):
                body(j)
            with eng.Fori(NB - HG + 1, NB - 1) as j:
                body(j)
            body(NB - 1)

        def sums_beside(j):
            return (j if isinstance(j, int) else j.min_val) >= NB - HG

        LAG = 2

        def block_beside(j, u):
            first = isinstance(j, int) and j == NB - HG
            if not sums_beside(j) or first and u < LAG:
                return []
            return [(group_of(j) - (u < LAG), (u - LAG) % SUB)]
        blocks_behind = [(HG - 1, i) for i in range(SUB - LAG, SUB)]

        def y_left(eng, j, u):
            q, slot, turn, par = quad(j, u)
            if isinstance(q, int) and q < 0:
                return
            h = half_of(j, u)
            at_least(eng, f"y_sent{par}_{h}", 16 * SUB * (RING // 2 * (turn - h * HB) + slot // 2 + 1))

        def results_sent(eng, h):
            for par in range(2):
                at_least(eng, f"y_sent{par}_{h}", 16 * SUB * HQ // 2)

        def norm_blocks(k):
            return (0, SUB * HG) if k == 0 else (SUB * (HG + k - 1), SUB)

        def slots_of(g):
            n = g - HG
            return [((i + SUB) if n % 2 == 0 else i, n // 2 + 1 if n % 2 == 0 else HG + n // 2 + 1) for i in range(SUB)]

        def sum_of(g, i):
            return psum[:, 2 * (g - HG) + i // 2, (i % 2) * D:(i % 2 + 1) * D]

        PART = E // 4
        gu_parts = [slice(i * PART, (i + 1) * PART) for i in range(4)]
        d_parts = [slice(0, E // 2), slice(E // 2, E)]
        CONV_DVE = KI // 2
        STEPS_DVE, STEPS_POOL = HALO * CONV_DVE, HALO * (KI - CONV_DVE)
        tap_out = [sg[:, 0, :], sg[:, 1, :], sh[:, 0, :], sh[:, 1, :], zs[:, 2, :], zs[:, 3, :]]
        assert len(tap_out) == STEPS_POOL

        def tap_added(eng, t, n):
            if isinstance(t, int) and not 0 < t < NT:
                return
            at_least(eng, "conv_step_pool", STEPS_POOL * t + n)

        block = ctx.enter_context(nc.Block())
        taps = cw_taps

        @block.sync
        def _(sp_):
            sp_.dma_start(win_f, w_in_T.rearrange("(k p) n -> p k n", p=P)).then_inc(s["w_in_in"], 16)

            def load_x(t):
                at_least(sp_, "x_hi_done", t)
                at_least(sp_, "x_lo_done", t)
                sp_.dma_start(xT[:, :, :], x_T.rearrange("(k p) n -> p k n", p=P)[:, :, bass.ds(t * T, T)]) \
                   .then_inc(s["xT_in"], 16)

            def load_tok(t):
                at_least(sp_, "ln_in", 2 * t)
                sp_.dma_start(xtok, x_tok.rearrange("(n p) d -> p n d", p=P)[:, bass.ds(t * SUB, SUB), :]) \
                   .then_inc(s["xtok_in"], 16)

            load_x(0)
            sp_.dma_start(cw_taps[:, :, :], conv_w).then_inc(s["consts_in"], 16)
            sp_.dma_start(cbias[:, :], conv_b).then_inc(s["consts_in"], 16)
            sp_.dma_start(dtbias[:, :], b_dt).then_inc(s["consts_in"], 16)
            sp_.dma_start(gbias[:, :], gate_bias.to_broadcast([P, E])).then_inc(s["consts_in"], 16)
            for i in range(2):
                sp_.dma_start(wx[:, :, i * R:(i + 1) * R],
                              w_x_T.rearrange("(k p) n -> p k n", p=P)[:, :, 0:R]).then_inc(s["w_x_in"], 16)
                sp_.dma_start(wdt_f[i * R:(i + 1) * R, :], w_dt_T).then_inc(s["w_dt_in"], 16)
            sp_.dma_start(wout[:, :, :], w_out_T.rearrange("(k p) n -> p k n", p=P)).then_inc(s["w_out_in"], 16)
            load_tok(0)
            sp_.dma_start(gw[:, :, :], gate_w_T.rearrange("(k p) n -> p k n", p=P)).then_inc(s["gate_in"], 16)
            for i, w in enumerate((ws_g_T, ws_u_T)):
                sp_.dma_start(wsgu_f[:, :, i * SH:(i + 1) * SH],
                              w.rearrange("(k p) n -> p k n", p=P)).then_inc(s["w_sgu_in"], 16)
            sp_.dma_start(wsd[:, :, :], ws_d_T.rearrange("(k p) n -> p k n", p=P)).then_inc(s["w_sd_in"], 16)
            load_x(1)
            for e in range(E):
                for i, w in enumerate((wg_T, wu_T)):
                    sp_.dma_start(raw_gu[:, e, :, i * I:(i + 1) * I],
                                  w[e, :, :].rearrange("(k p) i -> p k i", p=P)).then_inc(s["raw_in"], 16)
                sp_.dma_start(raw_d[:, e, :], wd_T[e, :, :]).then_inc(s["raw_in"], 16)
            with sp_.Fori(1, NT - 1) as t:
                load_x(t + 1)
                load_tok(t)
            load_tok(NT - 1)

            at_least(sp_, "pad_ready", 1)
            for h in range(HALVES):
                r = h * HALF + IDLE
                sp_.dma_start(x_buf[r:r + P, :], pad_row[:, :]).then_inc(s["pads_out"], 16)

            def pads(g):
                for first in table_values(sp_, pad_at, g, HALVES * HALF - P):
                    sp_.dma_start(x_buf[bass.ds(first, P), :], pad_row[:, :]).then_inc(s["pads_out"], 16)
            EQ = E // SUB
            assert HB - 1 >= EQ

            def rows_sent(h):
                at_least(sp_, "pads_out", 16 * (HALVES + (h + 1) * E))
                at_least(sp_, "sent", 16 * SUB * TOP * HT * (h + 1))
            at_least(sp_, "pad_at_done", 1)
            for g in range(EQ):
                pads(g)
            rows_sent(0)
            at_least(sp_, "table_done", 2)
            at_least(sp_, "wout_mm", 2 * NT)
            at_least(sp_, "xt_mm", NT)
            at_least(sp_, "row_x", NT)
            at_least(sp_, "x1_twice", NT)

            def load_results(g, i, u, n):
                at_least(sp_, f"y_used{u}", n - 1)
                sp_.dma_start(y_in[u][:, :, :], y_buf.rearrange("(k n p) d -> p n k d", k=TOP, p=P)
                              [:, bass.ds(SUB * g + i, 1), :, :].squeeze(1)).then_inc(s[f"y_in{u}"], 16)

            def load_tiles(j, u):
                q, slot, turn, _ = quad(j, u)
                if isinstance(j, int) and j == HB and u == 0:
                    rows_sent(1)
                    at_least(sp_, "table_done", 4)
                at_least(sp_, "y_id_done", SUB * (q - RING + 1))
                for i, first in enumerate(table_values(sp_, tile_at, q, HALVES * HALF - P)):
                    sp_.dma_start(tiles_in[:, slot, i, :], x_buf[bass.ds(first, P), :]) \
                       .then_inc(s[f"tile_in{slot}"], 16)
                for g, i in block_beside(j, u):
                    if isinstance(g, int) and g == 0 and i == 0:
                        results_sent(sp_, 0)
                    load_results(g, i, i, g + 1)
                if not isinstance(j, int) and j.min_val == 1 and u == RING - 1:
                    at_least(sp_, "pad_at_done", 2)
                    pads(EQ - 1 + j)
            each_quad(sp_, load_tiles)

            for g, i in blocks_behind:
                load_results(g, i, i, g + 1)
            results_sent(sp_, 1)
            for g in range(HG, HALVES * HG):
                for i, (u, n) in enumerate(slots_of(g)):
                    load_results(g, i, u, n)
            at_least(sp_, "stored", 16 * HALVES * HG)

        @block.gpsimd
        def _(pool):
            nc.gpsimd.memset(ident[:, :], 0.0).then_inc(s["id_zero"], 1)
            pool.wait_ge(s["id_zero"], 1)
            nc.gpsimd.affine_select(out=ident[:, :], in_=ident[:, :], compare_op=ALU.not_equal, fill=1.0,
                                    base=0, pattern=[[-1, P]], channel_multiplier=1).then_inc(s["id_ready"], 1)
            nc.gpsimd.memset(tri[:, :], 1.0).then_inc(s["tri_one"], 1)
            pool.wait_ge(s["tri_one"], 1)
            nc.gpsimd.affine_select(out=tri[:, :], in_=tri[:, :], compare_op=ALU.is_gt, fill=0.0,
                                    base=0, pattern=[[1, P]], channel_multiplier=-1).then_inc(s["tri_ready"], 1)
            nc.gpsimd.memset(ones[:, :], 1.0).then_inc(s["ones_ready"], 1)
            nc.gpsimd.memset(before[:, :, :], 1.0).then_inc(s["before_one"], 1)
            pool.wait_ge(s["before_one"], 1)
            nc.gpsimd.affine_select(out=before[:, :, :], in_=before[:, :, :], compare_op=ALU.is_gt, fill=0.0,
                                    base=0, pattern=[[1, NG], [-1, NG]], channel_multiplier=0) \
                     .then_inc(s["before_ready"], 1)
            nc.gpsimd.iota(tok_row[:, :], pattern=[[P - TOP * N, SUB]], base=-N, channel_multiplier=1,
                           allow_small_or_imprecise_dtypes=True).then_inc(s["const_ready"], 1)
            for v, first in ((counts[:, 0, :], 0), (counts[:, HT + 1, :], HALF), (region[:, :], 0)):
                nc.gpsimd.iota(v, pattern=[[CAP, E]], base=first, channel_multiplier=0,
                               allow_small_or_imprecise_dtypes=True).then_inc(s["const_ready"], 1)
            nc.gpsimd.iota(tile_no[:, :], pattern=[[0, 1]], base=0, channel_multiplier=1,
                           allow_small_or_imprecise_dtypes=True).then_inc(s["const_ready"], 1)
            nc.gpsimd.memset(pad_row[:, 0:D + E], 0.0)
            nc.gpsimd.memset(pad_row[:, D + E:ROW], float(TOP * N)).then_inc(s["pad_ready"], 1)

            def conv(t):
                for n in range(STEPS_POOL):
                    c = CONV_DVE + n // HALO
                    at_least(pool, "tap_done", STEPS_POOL * (t - 1) + n + 1)
                    if n % HALO:
                        tap_added(pool, t, n)
                    nc.gpsimd.tensor_tensor(xc[:, c, :], xc[:, c, :], tap_out[n], ALU.add) \
                             .then_inc(s["conv_step_pool"], 1)

            def gate_product(t):
                for c in range(KI):
                    at_least(pool, "xc_done", KI * t + c + 1)
                    at_least(pool, "s1_evac", 2 * KI * t + KI + c + 1)
                    if c == 0:
                        at_least(pool, "wout_mm", 2 * t)
                    nc.gpsimd.tensor_tensor(m[:, c, :], xc[:, c, :], zs[:, c, :], ALU.mult).then_inc(s["m_done"], 1)

            def x_low(t):
                at_least(pool, "x_hi_done", t + 1)
                at_least(pool, "s1_mm", 2 * KI * t)
                nc.gpsimd.tensor_tensor(x_lo[:, :, :], xT[:, :, :], x_hi[:, :, :].bitcast(F32), ALU.subtract) \
                         .then_inc(s["x_lo_done"], 1)

            def send(t, row=row, row_id=row_id):
                at_least_alone(pool, "routed", t + 1)
                at_least_alone(pool, "row_x", t + 1)
                for b in range(SUB):
                    for k in range(TOP):
                        nc.gpsimd.indirect_dma_start(
                            out=x_buf, out_offset=bass.IndirectOffsetOnAxis(ap=row_id[:, b, k:k + 1], axis=0),
                            in_=row[:, b, :], in_offset=None).then_inc(s["sent"], 16)

            x_low(0)
            x_low(1)
            gate_product(0)

            def tile(t, first=False, more=True):
                conv(t + 1)
                gate_product(t + 1)
                if more:
                    x_low(t + 2)
                if not first:
                    send(t - 1)
            tile(0, first=True)
            with pool.Fori(1, NT - 2) as t:
                tile(t)
            tile(NT - 2, more=False)
            for i in range(len(gu_parts)):
                r = gu_parts[i]
                if i >= len(gu_parts) // 2:
                    at_least(pool, "wout_mm", 2 * NT)
                at_least(pool, "ew_hi", i + 1)
                nc.gpsimd.tensor_tensor(ew_gu_lo[:, r, :, :], raw_gu[:, r, :, :], ew_gu_hi[:, r, :, :].bitcast(F32),
                                        ALU.subtract).then_inc(s["ew_gu_low"], 1)
            send(NT - 2)
            send(NT - 1, row_end, row_id_end)

            def pair(g, i, u, n):
                at_least(pool, f"y_in{u}", 16 * n)
                nc.gpsimd.tensor_tensor(y_in[u][:, 0:2, :], y_in[u][:, 0:2, :], y_in[u][:, 2:4, :], ALU.add) \
                         .then_inc(s["y_paired"], 1)

            def send_results(j, u):
                q, slot, turn, par = quad(j, u)
                if sums_beside(j) and not (isinstance(j, int) and (group_of(j), u) in blocks_behind):
                    pair(group_of(j), u, u, group_of(j) + 1)
                at_least_alone(pool, "y_evac", q + 1)
                at_least_alone(pool, "y_id_done", SUB * (q + 1))
                for i in range(SUB):
                    nc.gpsimd.indirect_dma_start(
                        out=y_buf, out_offset=bass.IndirectOffsetOnAxis(ap=y_id[slot][:, i:i + 1], axis=0),
                        in_=y_out[par][:, i, :], in_offset=None, bounds_check=TOP * N - 1, oob_is_err=False) \
                      .then_inc(s[f"y_sent{par}_{half_of(j, u)}"], 16)
            each_quad(pool, send_results)
            for g in range(HG, HALVES * HG):
                for i, (u, n) in enumerate(slots_of(g)):
                    pair(g, i, u, n)

        def split_mm(pe, o, w_hi, w_lo, v_hi, v_lo, start, stop):
            pe.matmul(o, w_hi, v_hi, start=start, stop=False)
            pe.matmul(o, w_hi, v_lo, start=False, stop=False)
            return pe.matmul(o, w_lo, v_hi, start=False, stop=stop)

        @block.tensor
        def _(pe):
            def in_proj(t, chunks):
                for j in chunks:
                    if j == 0:
                        at_least(pe, "x_hi_done", t + 1)
                        at_least(pe, "x_lo_done", t + 1)
                    at_least(pe, "s1_evac", 2 * KI * t + j - 1)
                    for k in range(KD):
                        mm = split_mm(pe, psum[:, j % 2, :], win_hi[:, k, j * P:(j + 1) * P],
                                      win_lo[:, k, j * P:(j + 1) * P], x_hi[:, k, :], x_lo[:, k, :],
                                      k == 0, k == KD - 1)
                    mm.then_inc(s["s1_mm"], 1)

            def dt_in(t):
                at_least(pe, "dt_lo", t)
                for c in range(KI):
                    at_least(pe, "xc_done", KI * t + c + 1)
                    mm = pe.matmul(psum[0:2 * R, 2, :], wx[:, c, :], xc[:, c, :], start=c == 0, stop=c == KI - 1)
                mm.then_inc(s["wx_mm"], 1)

            def dt_out(t, chunks):
                at_least(pe, "dt_lo", t + 1)
                at_least(pe, "x1T_h", t)
                at_least(pe, "x1T_l", t)
                for c in chunks:
                    if c >= 2:
                        at_least(pe, "sp_done", KI * t + c - 1)
                    pe.matmul(psum[:, 4 + c % 2, :], wdt_hi[:, c * P:(c + 1) * P], dt[:, :], start=True, stop=False)
                    pe.matmul(psum[:, 4 + c % 2, :], wdt_lo[:, c * P:(c + 1) * P], dt[0:R, :],
                              start=False, stop=True).then_inc(s["wdt_mm"], 1)

            def out_proj(t):
                at_least(pe, "y_done", KI * (t + 1))
                for b in range(SUB):
                    o = psum[:, 4 + b // 2, (b % 2) * D:(b % 2 + 1) * D]
                    for c in range(KI):
                        mm = pe.matmul(o, m[:, c, b * P:(b + 1) * P], wout[:, c, :], start=c == 0, stop=c == KI - 1)
                    if b % 2:
                        mm.then_inc(s["wout_mm"], 1)

            def transposes(t):
                for b in range(SUB):
                    at_least(pe, "x1_done", SUB * t + b + 1)
                    for k in range(KD):
                        mm = pe.transpose(psum[:, 4 + k, b * P:(b + 1) * P], x1[:, b, k * P:(k + 1) * P], ident[:, :])
                mm.then_inc(s["xt_mm"], 1)

            def gate(t):
                at_least(pe, "x1T_h", t + 1)
                at_least(pe, "x1T_l", t + 1)
                at_least(pe, "gate_sum", t)
                for b in range(SUB):
                    r = slice(b * P, (b + 1) * P)
                    for k in range(KD):
                        o = psum[:, 3, b * 2 * E:(b + 1) * 2 * E]
                        pe.matmul(o, x1T_hi[:, k, r], gw_split[:, k, :], start=k == 0, stop=False)
                        mm = pe.matmul(o, x1T_lo[:, k, r], gw_split[:, k, :], start=False, stop=k == KD - 1)
                mm.then_inc(s["gate_mm"], 1)

            def shared_up(t, i):
                at_least(pe, "res_done", 2 * t)
                at_least(pe, "h_done", KS * t + i)
                for j in range(2):
                    c = slice(j * SH + i * P, j * SH + (i + 1) * P)
                    for k in range(KD):
                        mm = split_mm(pe, psum[:, 6 + j, :], wsgu_hi[:, k, c], wsgu_lo[:, k, c],
                                      x1T_hi[:, k, :], x1T_lo[:, k, :], k == 0, k == KD - 1)
                mm.then_inc(s["sgu_mm"], 1)

            def ranks(t):
                at_least(pe, "sel_done", t + 1)
                at_least(pe, "routed", t)
                for b in range(SUB):
                    o = psum[:, 3, (2 * SUB + b) * E:(2 * SUB + b + 1) * E]
                    pe.matmul(o, tri[:, :], sel16[:, b, :], start=True, stop=b == 0)
                    for q in range(b):
                        pe.matmul(o, ones[:, :], sel16[:, q, :], start=False, stop=q == b - 1)
                for b in range(SUB):
                    mm = pe.matmul(psum[:, 3, 3 * SUB * E:(3 * SUB + 1) * E], ones[:, :], sel16[:, b, :],
                                   start=b == 0, stop=b == SUB - 1)
                mm.then_inc(s["rank_mm"], 1)

            def shared_down(t):
                at_least(pe, "h_done", KS * (t + 1))
                for b in range(SUB):
                    o = psum[:, 6 + b // 2, (b % 2) * D:(b % 2 + 1) * D]
                    for c in range(KS):
                        mm = pe.matmul(o, sh[:, c, b * P:(b + 1) * P], wsd[:, c, :], start=c == 0, stop=c == KS - 1)
                    if b % 2:
                        mm.then_inc(s["sd_mm"], 1)

            def table_mm(h):
                at_least(pe, "table_step", TABLE_STEPS * (h + 1))
                for i, v in enumerate((tile_ef, tile_row)):
                    mm = pe.matmul(table_bank(h, i), v[:, :], ident[:, 0:HTILES], start=True, stop=True)
                mm.then_inc(s["table_mm"], 1)

            def tile(t, first=False, last=False):
                dt_out(t, range(0, 2))
                if not last:
                    in_proj(t + 1, range(0, KI))
                dt_out(t, range(2, KI))
                if not first:
                    shared_up(t - 1, 0)
                if not last:
                    in_proj(t + 1, range(KI, KI + 2))
                out_proj(t)
                if not last:
                    in_proj(t + 1, range(KI + 2, 2 * KI))
                if not first:
                    shared_up(t - 1, 1)
                if last:
                    table_mm(0)
                if not first and not last:
                    ranks(t - 1)
                if not last:
                    dt_in(t + 1)
                transposes(t)
                if last:
                    ranks(t - 1)
                if not first:
                    shared_down(t - 1)
                gate(t)

            pe.wait_ge(s["win_h"], 1)
            pe.wait_ge(s["win_l"], 1)
            in_proj(0, range(2 * KI))
            pe.wait_ge(s["w_x_in"], 32)
            dt_in(0)
            pe.wait_ge(s["wdt_h"], 1)
            pe.wait_ge(s["wdt_l"], 1)
            pe.wait_ge(s["w_out_in"], 16)
            pe.wait_ge(s["id_ready"], 1)
            pe.wait_ge(s["gw_h"], 1)
            pe.wait_ge(s["gw_l"], 1)
            tile(0, first=True)
            pe.wait_ge(s["tri_ready"], 1)
            pe.wait_ge(s["ones_ready"], 1)
            pe.wait_ge(s["wsgu_h"], 1)
            pe.wait_ge(s["wsgu_l"], 1)
            pe.wait_ge(s["w_sd_in"], 16)
            tile(1)
            with pe.Fori(2, NT - 1) as t:
                tile(t)
            tile(NT - 1, last=True)
            shared_up(NT - 1, 0)
            shared_up(NT - 1, 1)
            ranks(NT - 1)

            def tile_experts(q):
                return table_values(pe, tile_e, q, E - 1)

            def turn_x(j, u):
                q, slot, turn, par = quad(j, u)
                at_least(pe, f"tile_in{slot}", 16 * SUB * (turn + 1))
                for k in range(KD):
                    at_least(pe, "t_l", KD * (q - 1) + k + 1)
                    for i in range(SUB):
                        mm = pe.transpose(psum[:, 2 + k, i * P:(i + 1) * P],
                                          tiles_in[:, slot, i, k * P:(k + 1) * P], ident[:, :])
                    mm.then_inc(s["t_mm"], 1)

            def gate_up(j, u, experts):
                q, slot, turn, par = quad(j, u)
                at_least(pe, "t_l", KD * (q + 1))
                at_least(pe, "e_mul", SUB * q)
                for i, e in enumerate(experts):
                    o = psum[:, i // 2, (i % 2) * 2 * I:(i % 2 + 1) * 2 * I]
                    r = slice(i * P, (i + 1) * P)
                    for k in range(KD):
                        w_hi, w_lo = (w[:, bass.ds(e, 1), k, :].squeeze(1) for w in (ew_gu_hi, ew_gu_lo))
                        pe.matmul(o, t_hi[par][:, k, r], w_hi, start=k == 0, stop=False)
                        pe.matmul(o, t_hi[par][:, k, r], w_lo, start=False, stop=False)
                        mm = pe.matmul(o, t_lo[par][:, k, r], w_hi, start=False, stop=k == KD - 1)
                mm.then_inc(s["gu_mm"], 1)

            def turn_act(j, u):
                q, slot, turn, par = quad(j, u)
                at_least(pe, "e_mul", SUB * (q + 1))
                at_least(pe, "a_l", q)
                for i in range(SUB):
                    mm = pe.transpose(psum[:, 4, i * P:(i + 1) * P], e_act[:, i, :], ident[:, :])
                mm.then_inc(s["at_mm"], 1)

            def down(j, u, experts):
                q, slot, turn, par = quad(j, u)
                if isinstance(q, int):
                    at_least(pe, "ew_d_low", len(d_parts))
                    at_least(pe, "res_done", 2 * NT)
                at_least(pe, "a_l", q + 1)
                at_least(pe, "y_evac", q)
                for i, e in enumerate(experts):
                    o = psum[:, 6 + i // 2, (i % 2) * D:(i % 2 + 1) * D]
                    r = slice(i * P, (i + 1) * P)
                    w_hi, w_lo = (w[:, bass.ds(e, 1), :].squeeze(1) for w in (ew_d_hi, ew_d_lo))
                    pe.matmul(o, a_hi[:, r], w_hi, start=True, stop=False)
                    pe.matmul(o, a_hi[:, r], w_lo, start=False, stop=False)
                    mm = pe.matmul(o, a_lo[:, r], w_hi, start=False, stop=True)
                mm.then_inc(s["y_mm"], 1)

            def iteration(j, u):
                q, left = RING * j + u, quads_left(j)
                if u + 2 < left:
                    turn_x(j, u + 2)
                if not is_first(j, u):
                    down(j, u - 1, tile_experts(q - 1))
                if u + 1 < left:
                    experts = tile_experts(q + 1)
                turn_act(j, u)
                if u + 1 < left:
                    gate_up(j, u + 1, experts)
                if isinstance(j, int) and j == 0:
                    if u == 2:
                        table_mm(1)
                    if u == RING - 1:
                        at_least(pe, "table_done", 4)

            at_least(pe, "table_done", 2)
            at_least(pe, "routed", NT)
            turn_x(0, 0)
            turn_x(0, 1)
            at_least(pe, "ew_gu_low", len(gu_parts))
            gate_up(0, 0, tile_experts(0))
            shared_down(NT - 1)
            each_quad(pe, iteration)
            down(NB - 1, RING - 1, tile_experts(NQ - 1))

            at_least(pe, "y_evac", NQ)
            for g in range(HG, HALVES * HG):
                for i, (u, n) in enumerate(slots_of(g)):
                    at_least(pe, "y_paired", SUB * g + i + 1 - len(blocks_behind))
                    terms = (res[:, SUB * g + i, :], y_in[u][:, 0, :], y_in[u][:, 1, :])
                    for k, v in enumerate(terms):
                        mm = pe.matmul(sum_of(g, i), ident[:, :], v, start=k == 0, stop=k == len(terms) - 1)
                    mm.then_inc(s[f"y_used{u}"], 1)

        @block.scalar
        def _(act):
            A = nc.scalar.activation

            def split_x(t):
                at_least(act, "xT_in", 16 * (t + 1))
                at_least(act, "s1_mm", 2 * KI * t)
                A(x_hi[:, :, :], xT[:, :, :], ACT.Copy).then_inc(s["x_hi_done"], 1)

            def conv_in(t, chunks):
                for c in chunks:
                    at_least(act, "s1_mm", 2 * KI * t + c + 1)
                    at_least(act, "halo_done", t + 1)
                    at_least(act, "m_done", KI * t)
                    at_least(act, "wx_mm", t)
                    A(xs[:, c, HALO:HALO + T], psum[:, c % 2, :], ACT.Copy)
                    A(xc[:, c, :], psum[:, c % 2, :], ACT.Identity, bias=cbias[:, c:c + 1],
                      scale=taps[:, c, HALO:HALO + 1]).then_inc(s["s1_evac"], 1)

            def taps_out(t, steps):
                for n in steps:
                    c, k = CONV_DVE + n // HALO, n % HALO
                    at_least(act, "s1_evac", 2 * KI * t + c + 1)
                    at_least(act, "m_done", KI * t)
                    at_least(act, "h_done", KS * (t - 2))
                    at_least(act, "sd_mm", 2 * (t - 2))
                    A(tap_out[n], xs[:, c, k:k + T], ACT.Copy, scale=taps[:, c, k:k + 1]).then_inc(s["tap_done"], 1)

            def silu_z(t, chunks):
                for c in chunks:
                    if c >= 2:
                        tap_added(act, t, len(tap_out) - KI + c + 1)
                    at_least(act, "s1_mm", 2 * KI * t + KI + c + 1)
                    at_least(act, "m_done", KI * t)
                    A(zs[:, c, :], psum[:, c % 2, :], ACT.Silu).then_inc(s["s1_evac"], 1)

            def silu_xc(t):
                for c in range(KI):
                    if c < CONV_DVE:
                        at_least(act, "conv_step", STEPS_DVE * t + HALO * (c + 1))
                    else:
                        at_least(act, "conv_step_pool", STEPS_POOL * t + HALO * (c - CONV_DVE + 1))
                    A(xc[:, c, :], xc[:, c, :], ACT.Silu).then_inc(s["xc_done"], 1)

            def dt_high(t):
                at_least(act, "wx_mm", t + 1)
                at_least(act, "wdt_mm", KI * t)
                A(dt[:, :], psum[0:2 * R, 2, :], ACT.Copy).then_inc(s["dt_hi"], 1)

            def exps(t, chunks):
                for c in chunks:
                    at_least(act, "wdt_mm", KI * t + c + 1)
                    at_least(act, "y_done", KI * t)
                    A(sp[:, c, :], psum[:, 4 + c % 2, :], ACT.Exp, bias=dtbias[:, c:c + 1]).then_inc(s["exp_done"], 1)

            def logs(t, chunks):
                for c in chunks:
                    at_least(act, "exp_clamped", KI * t + c + 1)
                    A(sp[:, c, :], sp[:, c, :], ACT.Ln, bias=1.0).then_inc(s["ln_done"], 1)

            def x1T_high(t):
                at_least(act, "xt_mm", t + 1)
                at_least(act, "sgu_mm", KS * t)
                A(x1T_hi[:, :, :], psum[:, 4:4 + KD, :], ACT.Copy).then_inc(s["x1T_h"], 1)

            def gate_exp(t):
                at_least(act, "gate_sum", t + 1)
                A(score[:, :, :], score[:, :, :], ACT.Exp, scale=-1.0).then_inc(s["gate_exp"], 1)

            def shared_silu(t, i):
                at_least(act, "sgu_mm", KS * t + i + 1)
                tap_added(act, t + 2, i + 1)
                A(sg[:, i, :], psum[:, 6, :], ACT.Silu).then_inc(s["ssilu"], 1)

            def copy_row(t, row=row):
                at_least(act, "x1_done", SUB * (t + 1))
                if row is not row_end:
                    at_least(act, "sent", 16 * SUB * TOP * t)
                A(row[:, :, 0:D], x1[:, :, :], ACT.Copy).then_inc(s["row_x"], 1)
                A(res[:, bass.ds(t * SUB, SUB), :], x1[:, :, :], ACT.Copy, scale=2.0).then_inc(s["x1_twice"], 1)

            def weights_high(i):
                at_least(act, "raw_in", 16 * 3 * E)
                at_least(act, "s1_mm", 2 * KI * NT)
                at_least(act, "m_done", KI * NT)
                at_least(act, "wx_mm", NT)
                A(ew_gu_hi[:, gu_parts[i], :, :], raw_gu[:, gu_parts[i], :, :], ACT.Copy).then_inc(s["ew_hi"], 1)

            def tile(t, first=False, last=False, more=True):
                exps(t, range(0, 2))
                if not last:
                    conv_in(t + 1, range(0, 1))
                logs(t, range(0, 2))
                if not last:
                    conv_in(t + 1, range(1, KI))
                exps(t, range(2, KI))
                if not last:
                    taps_out(t + 1, range(0, 1))
                logs(t, range(2, KI))
                if not last:
                    taps_out(t + 1, range(1, STEPS_POOL))
                if last:
                    weights_high(0)
                if not first:
                    shared_silu(t - 1, 0)
                if last:
                    weights_high(1)
                if not last:
                    silu_z(t + 1, range(0, 2))
                if not first:
                    copy_row(t - 1)
                if last:
                    weights_high(2)
                if not last:
                    silu_xc(t + 1)
                    silu_z(t + 1, range(2, KI))
                if not first:
                    shared_silu(t - 1, 1)
                if last:
                    weights_high(3)
                if more:
                    split_x(t + 2)
                if not last:
                    dt_high(t + 1)
                nc.scalar.preload_act_table_set("natural_log_exp_and_others")
                x1T_high(t)
                if last:
                    copy_row(t, row_end)
                gate_exp(t)

            act.wait_ge(s["w_in_in"], 16)
            A(win_hi[:, :, :], win_f, ACT.Copy).then_inc(s["win_h"], 1)
            split_x(0)
            act.wait_ge(s["consts_in"], 64)
            conv_in(0, range(KI))
            silu_z(0, range(KI))
            split_x(1)
            silu_xc(0)
            act.wait_ge(s["w_dt_in"], 32)
            A(wdt_hi[:, :], wdt_f, ACT.Copy).then_inc(s["wdt_h"], 1)
            dt_high(0)
            act.wait_ge(s["gate_in"], 16)
            A(gw_hi, gw[:, :, :], ACT.Copy).then_inc(s["gw_h"], 1)
            act.wait_ge(s["w_sgu_in"], 32)
            A(wsgu_hi[:, :, :], wsgu_f, ACT.Copy).then_inc(s["wsgu_h"], 1)
            act.wait_ge(s["win_l"], 1)
            act.wait_ge(s["wdt_l"], 1)
            act.wait_ge(s["wsgu_l"], 1)
            nc.scalar.preload_act_table_set("natural_log_exp_and_others")
            tile(0, first=True)
            tile(1)
            with act.Fori(2, NT - 2) as t:
                tile(t)
            tile(NT - 2, more=False)
            tile(NT - 1, last=True, more=False)
            shared_silu(NT - 1, 0)
            shared_silu(NT - 1, 1)
            at_least(act, "row_x", NT)
            at_least(act, "x1_twice", NT)
            for r in d_parts:
                A(ew_d_hi[:, r, :], raw_d[:, r, :], ACT.Copy).then_inc(s["ew_hi"], 1)


            def x_high(j, u, k):
                q, slot, turn, par = quad(j, u)
                at_least(act, "t_mm", KD * q + k + 1)
                at_least(act, "gu_mm", q - 1)
                A(t_hi[par][:, k, :], psum[:, 2 + k, :], ACT.Copy).then_inc(s["t_h"], 1)

            def gate_silu(j, u):
                q, slot, turn, par = quad(j, u)
                at_least(act, "gu_mm", q + 1)
                at_least(act, "e_mul", SUB * q)
                A(g_act[:, :, :], psum[:, 0:2, :].rearrange("p a (b i) -> p (a b) i", i=2 * I)[:, :, 0:I],
                  ACT.Silu).then_inc(s["g_silu"], 1)

            def act_high(j, u):
                q, slot, turn, par = quad(j, u)
                at_least(act, "at_mm", q + 1)
                at_least(act, "y_mm", q)
                A(a_hi[:, :], psum[:, 4, :], ACT.Copy).then_inc(s["a_h"], 1)

            def result(j, u):
                q, slot, turn, par = quad(j, u)
                at_least(act, "y_mm", q + 1)
                y_left(act, j, u - 2)
                A(y_out[par][:, :, :], psum[:, 6:8, :].rearrange("p a (b d) -> p (a b) d", d=D), ACT.Copy) \
                    .then_inc(s["y_evac"], 1)

            def out_norm(k):
                first, n = norm_blocks(k)
                at_least(act, "o_ready", k + 1)
                for b in range(first, first + n):
                    g, i = b // SUB, b % SUB
                    A(res[:, b, :], sum_of(g, i) if g >= HG else res[:, b, :], ACT.Identity,
                      bias=o_shift[k % 2][:, b - first:b - first + 1],
                      scale=o_rstd[k % 2][:, b - first:b - first + 1]).then_inc(s["o_done"], 1)
                    if i == SUB - 1:
                        at_least(act, "o_done", b + 1)
                        act.dma_start(out.rearrange("(n p) d -> p n d", p=P)[:, b + 1 - SUB:b + 1, :],
                                      res[:, b + 1 - SUB:b + 1, :]).then_inc(s["stored"], 16)

            def iteration(j, u):
                gate_silu(j, u)
                if u + 2 < quads_left(j):
                    for k in range(KD):
                        x_high(j, u + 2, k)
                if not is_first(j, u):
                    result(j, u - 1)
                act_high(j, u)

            at_least(act, "ew_gu_low", len(gu_parts))
            for u in range(2):
                for k in range(KD):
                    x_high(0, u, k)
            each_quad(act, iteration)
            result(NB - 1, RING - 1)
            for k in range(1 + HG):
                out_norm(k)

        @block.vector
        def _(dve):
            V = nc.vector

            def f32(ap):
                return ap.bitcast(F32)

            def inverse_root(v, neg_half, half_bits, y, h, name, n):
                def then(ins):
                    nonlocal n
                    n = n + 1
                    ins.then_inc(s[name], 1)
                    dve.wait_ge(s[name], n)
                V.tensor_scalar(neg_half, v, -0.5, None, ALU.mult).then_inc(s[name], 1)
                n = n + 1
                then(V.tensor_scalar(half_bits, v.bitcast(I32), 1, None, ALU.arith_shift_right))
                then(V.tensor_scalar(y.bitcast(I32), half_bits, -1.0, RSQRT_MAGIC, ALU.mult, ALU.add))
                for i in range(NEWTON):
                    then(V.tensor_tensor(h, y, y, ALU.mult))
                    then(V.tensor_tensor(h, h, neg_half, ALU.mult))
                    then(V.scalar_tensor_tensor(y, h, 1.5, y, ALU.add, ALU.mult))
                return n

            def halo(t):
                at_least(dve, "conv_step", STEPS_DVE * t)
                at_least(dve, "conv_step_pool", STEPS_POOL * t)
                at_least(dve, "s1_evac", 2 * KI * (t - 1) + KI)
                V.tensor_scalar(xs[:, :, 0:HALO], xs[:, :, T:T + HALO], keep[:, bass.ds(t, 1)], None, ALU.mult) \
                 .then_inc(s["halo_done"], 1)

            def conv(t, chunks):
                for c in chunks:
                    for k in range(HALO):
                        n = STEPS_DVE * t + HALO * c + k
                        if k == 0:
                            at_least(dve, "s1_evac", 2 * KI * t + c + 1)
                            at_least(dve, "halo_done", t + 1)
                        elif c < CONV_DVE:
                            at_least(dve, "conv_step", n)
                        else:
                            at_least(dve, "conv_step_pool", n - STEPS_DVE)
                        V.scalar_tensor_tensor(xc[:, c, :], xs[:, c, k:k + T], taps[:, c, k:k + 1], xc[:, c, :],
                                               ALU.mult, ALU.add).then_inc(s["conv_step"] if c < CONV_DVE else s["conv_step_pool"], 1)

            def dt_low(t):
                at_least(dve, "dt_hi", t + 1)
                V.tensor_tensor(dt[R:2 * R, :], psum[R:2 * R, 2, :], f32(dt[R:2 * R, :]), ALU.subtract) \
                 .then_inc(s["dt_lo"], 1)

            def clamp(t, chunks):
                for c in chunks:
                    at_least(dve, "exp_done", KI * t + c + 1)
                    V.tensor_scalar(sp[:, c, :], sp[:, c, :], EXP_MAX, None, ALU.min).then_inc(s["exp_clamped"], 1)

            def softplus(t, chunks):
                for c in chunks:
                    at_least(dve, "ln_done", KI * t + c + 1)
                    V.scalar_tensor_tensor(sp[:, c, :], psum[:, 4 + c % 2, :], dtbias[:, c:c + 1], sp[:, c, :],
                                           ALU.add, ALU.max).then_inc(s["sp_done"], 1)
                for c in chunks:
                    at_least(dve, "sp_done", KI * t + c + 1)
                    at_least(dve, "m_done", KI * t + c + 1)
                    V.tensor_tensor(m[:, c, :], m[:, c, :], sp[:, c, :], ALU.mult).then_inc(s["y_done"], 1)

            def layer_norm(t):
                at_least(dve, "xtok_in", 16 * (t + 1))
                at_least(dve, "row_x", t)
                at_least(dve, "x1_twice", t)
                for h in range(2):
                    at_least(dve, "wout_mm", 2 * t + h + 1)
                    V.scalar_tensor_tensor(x1[:, 2 * h:2 * h + 2, :], xtok[:, 2 * h:2 * h + 2, :], 2.0,
                                           psum[:, 4 + h, :].rearrange("p (b d) -> p b d", d=D),
                                           ALU.mult, ALU.add).then_inc(s["ln_in"], 1)
                for b in range(SUB):
                    at_least(dve, "ln_in", 2 * t + b // 2 + 1)
                    V.bn_stats(stats[:, b, :], x1[:, b, :]).then_inc(s["bn"], 1)
                for b in range(SUB):
                    at_least_alone(dve, "bn", SUB * t + b + 1)
                    V.bn_aggr(mv[:, b, :], stats[:, b, :]).then_inc(s["bn_mv"], 1)
                dve.wait_ge(s["bn_mv"], SUB * (t + 1))
                n = NORM_STEPS * t
                V.tensor_scalar(var[:, :], mv[:, :, 1], EPS, None, ALU.add).then_inc(s["norm_step"], 1)
                dve.wait_ge(s["norm_step"], n + 1)
                inverse_root(var[:, :], neg_half[:, :], half_bits[:, :], rstd[:, :], newton[:, :], "norm_step", n + 1)
                for b in range(SUB):
                    V.tensor_scalar(x1[:, b, :], x1[:, b, :], mv[:, b, 0:1], rstd[:, b:b + 1],
                                    ALU.subtract, ALU.mult).then_inc(s["x1_done"], 1)

            def x1T_low(t):
                at_least(dve, "x1T_h", t + 1)
                V.tensor_tensor(x1T_lo[:, :, :], psum[:, 4:4 + KD, :], f32(x1T_hi[:, :, :]), ALU.subtract) \
                 .then_inc(s["x1T_l"], 1)

            def shared_act(t, i):
                at_least(dve, "ssilu", KS * t + i + 1)
                tap_added(dve, t + 2, KS + i + 1)
                at_least(dve, "sd_mm", 2 * t)
                V.tensor_tensor(sh[:, i, :], sg[:, i, :], psum[:, 7, :], ALU.mult).then_inc(s["h_done"], 1)

            def residual(t):
                for h in range(2):
                    at_least(dve, "sd_mm", 2 * t + h + 1)
                    at_least(dve, "x1_twice", t + 1)
                    r = res[:, bass.ds(t * SUB + 2 * h, 2), :]
                    V.tensor_tensor(r, r, psum[:, 6 + h, :].rearrange("p (b d) -> p b d", d=D), ALU.add) \
                     .then_inc(s["res_done"], 1)

            done = [0]
            STEPS = 45

            def step(ins, t, wait=True, alone=False):
                done[0] += 1
                ins.then_inc(s["route_step"], 1)
                if wait:
                    (at_least_alone if alone else at_least)(dve, "route_step", STEPS * t + done[0])

            def flat(ap):
                return ap.rearrange("p b e -> p (b e)")

            def route(t):
                done[0] = 0
                dve.wait_ge(s["gate_mm"], t + 1)
                V.tensor_reduce(score[:, :, :], psum[:, 3, 0:2 * SUB * E].rearrange("p (b i e) -> p b e i", i=2, e=E),
                                axis=AX_X, op=ALU.add).then_inc(s["gate_sum"], 1)
                dve.wait_ge(s["gate_exp"], t + 1)
                step(V.tensor_scalar(flat(sfc[:, :, :]), flat(score[:, :, :]), 1.0, None, ALU.add), t)
                step(V.reciprocal(flat(score[:, :, :]), flat(sfc[:, :, :])), t)
                step(V.tensor_tensor(sfc[:, :, :], score[:, :, :],
                                     gbias[:, :].unsqueeze(1).to_broadcast([P, SUB, E]), ALU.add), t)
                grp = flat(sfc[:, :, :]).rearrange("p (g j k) -> p g j k", j=2, k=2)
                mx, mn = (v[:, :, :, :].rearrange("p b g k -> p (b g) k") for v in (pmx, pmn))
                step(V.tensor_tensor(mx, grp[:, :, 0, :], grp[:, :, 1, :], ALU.max), t, False)
                step(V.tensor_tensor(mn, grp[:, :, 0, :], grp[:, :, 1, :], ALU.min), t)
                step(V.tensor_tensor(g1[:, :], mx[:, :, 0], mx[:, :, 1], ALU.max), t, False)
                step(V.tensor_tensor(g2[:, :], mx[:, :, 0], mx[:, :, 1], ALU.min), t, False)
                step(V.tensor_tensor(g3[:, :], mn[:, :, 0], mn[:, :, 1], ALU.max), t)
                step(V.tensor_tensor(g2[:, :], g2[:, :], g3[:, :], ALU.max), t)
                step(V.tensor_tensor(gsc[:, :], g1[:, :], g2[:, :], ALU.add), t)

            def pick(t):
                gs = gsc[:, :].rearrange("p (b g) -> p b g", g=NG)
                one, other = (gs.unsqueeze(a).to_broadcast([P, SUB, NG, NG]) for a in (3, 2))
                ca, cb = (v[:, :, :, :] for v in (cmp_a, cmp_b))
                step(V.tensor_tensor(ca, other, one, ALU.is_gt), t, False)
                step(V.tensor_tensor(cb, other, one, ALU.is_equal), t)
                step(V.tensor_tensor(cb, cb, before[:, :, :].unsqueeze(1).to_broadcast([P, SUB, NG, NG]), ALU.mult), t)
                step(V.tensor_tensor(ca, ca, cb, ALU.add), t)
                step(V.tensor_reduce(g1[:, :], ca.rearrange("p b g k -> p (b g) k"), axis=AX_X, op=ALU.add), t)
                step(V.tensor_scalar(gkeep[:, :], g1[:, :], float(GROUPS_KEPT), None, ALU.is_lt), t)
                step(V.tensor_scalar(gpen[:, :], gkeep[:, :], 1.0, LOWEST, ALU.subtract, ALU.mult), t, False)
                pk = picked[:, :, :].rearrange("p b (g j) -> p (b g) j", j=EG)
                sf = sfc[:, :, :].rearrange("p b (g j) -> p (b g) j", j=EG)
                step(V.tensor_tensor(pk, sf, gkeep[:, :].unsqueeze(2).to_broadcast([P, SUB * NG, EG]), ALU.mult), t)
                step(V.tensor_tensor(pk, pk, gpen[:, :].unsqueeze(2).to_broadcast([P, SUB * NG, EG]), ALU.add),
                     t, alone=True)
                for b in range(SUB):
                    step(V.max(top8[:, b, :], picked[:, b, :]), t, b == SUB - 1)

            def choose(t, row=row):
                fourth = top8[:, :, TOP - 1:TOP].to_broadcast([P, SUB, E])
                step(V.tensor_tensor(above[:, :, :], picked[:, :, :], fourth, ALU.is_gt), t, False)
                step(V.tensor_tensor(equal[:, :, :], picked[:, :, :], fourth, ALU.is_equal), t)
                step(V.tensor_reduce(nabove[:, :], above[:, :, :], axis=AX_X, op=ALU.add), t, False)
                step(V.tensor_tensor_scan(flat(posn[:, :, :]), flat(block_start[:, :, :]), flat(equal[:, :, :]), 0.0,
                                          ALU.mult, ALU.add), t)
                step(V.tensor_tensor(posn[:, :, :], posn[:, :, :],
                                     nabove[:, :].unsqueeze(2).to_broadcast([P, SUB, E]), ALU.add), t)
                step(V.scalar_tensor_tensor(posn[:, :, :], posn[:, :, :], float(TOP), equal[:, :, :],
                                            ALU.is_le, ALU.mult), t)
                step(V.tensor_tensor(sel[:, :, :], posn[:, :, :], above[:, :, :], ALU.add), t)
                V.tensor_copy(sel16[:, :, :], sel[:, :, :]).then_inc(s["sel_done"], 1)
                step(V.tensor_tensor(wsel[:, :, :], score[:, :, :], sel[:, :, :], ALU.mult), t, False)
                step(V.tensor_tensor_scan(flat(slots[:, :, :]), flat(ones_f[:, :, :]), flat(sel[:, :, :]), 0.0,
                                          ALU.mult, ALU.add), t)
                step(V.tensor_reduce(wsum[:, :], wsel[:, :, :], axis=AX_X, op=ALU.add), t)
                step(V.tensor_scalar(wsum[:, :], wsum[:, :], 1e-20, None, ALU.add), t)
                step(V.reciprocal(nabove[:, :], wsum[:, :]), t)
                if row is not row_end:
                    at_least(dve, "sent", 16 * SUB * TOP * t)
                step(V.scalar_tensor_tensor(row[:, :, D:D + E], wsel[:, :, :], SCALE,
                                            nabove[:, :].unsqueeze(2).to_broadcast([P, SUB, E]),
                                            ALU.mult, ALU.mult), t, False)
                step(V.scalar_tensor_tensor(row[:, :, D + E:ROW], slots[:, :, :], float(N),
                                            tok_row[:, :].unsqueeze(2).to_broadcast([P, SUB, E]),
                                            ALU.mult, ALU.add), t)
                step(V.tensor_scalar(tok_row[:, :], tok_row[:, :], float(T), None, ALU.add), t)

            def place(t, row_id=row_id):
                dve.wait_ge(s["rank_mm"], t + 1)
                rank = psum[:, 3, 2 * SUB * E:3 * SUB * E].rearrange("p (b e) -> p b e", e=E)
                c = t + t // HT
                before_t, behind_t = (counts[:, bass.ds(c + i, 1), :] for i in range(2))
                step(V.tensor_tensor(posn[:, :, :], rank, before_t.to_broadcast([P, SUB, E]), ALU.add), t)
                step(V.tensor_tensor(behind_t.squeeze(1), before_t.squeeze(1),
                                     psum[:, 3, 3 * SUB * E:(3 * SUB + 1) * E], ALU.add), t)
                step(V.scalar_tensor_tensor(posn[:, :, :], posn[:, :, :], 1.0, sel[:, :, :],
                                            ALU.add, ALU.mult), t, alone=True)
                for b in range(SUB):
                    step(V.max(pos8[:, b, :], posn[:, b, :]), t, b == SUB - 1)
                V.tensor_scalar(row_id[:, :, :], pos8[:, :, 0:TOP], 1.0, None, ALU.subtract).then_inc(s["routed"], 1)
                assert done[0] == STEPS, done[0]

            def table(h):
                n = [h * TABLE_STEPS]

                def then(ins):
                    n[0] += 1
                    ins.then_inc(s["table_step"], 1)
                    dve.wait_ge(s["table_step"], n[0])
                c = counts[:, h * (HT + 1) + HT, :]
                V.tensor_copy(pad_at[:, h * E:(h + 1) * E], c[0:1, :]).then_inc(s["pad_at_done"], 1)
                at_least(dve, "table_mm", h)
                then(V.scalar_tensor_tensor(ntile, c, -float(h * HALF), region[:, :], ALU.add, ALU.subtract))
                then(V.tensor_scalar(ntile_i[:, :], ntile, float(P - 1), None, ALU.add))
                then(V.tensor_scalar(ntile_i[:, :], ntile_i[:, :], P.bit_length() - 1, None, ALU.arith_shift_right))
                then(V.tensor_copy(ends[0][:, 8:8 + E], ntile_i[:, :]))
                then(V.tensor_scalar(row_step[:, :], ends[0][:, 8:8 + E], -float(P), float(CAP), ALU.mult, ALU.add))
                for i, d in enumerate((1, 2, 4, 8)):
                    a, b = ends[(0, 1, 2, 1)[i]], ends[(1, 2, 1, 2)[i]]
                    then(V.tensor_tensor(b[:, 8:8 + E], a[:, 8:8 + E], a[:, 8 - d:8 - d + E], ALU.add))
                then(V.tensor_tensor(is_past, tile_no[:, :].to_broadcast([P, E]), ends[2][:, 8:8 + E], ALU.is_ge))
                then(V.tensor_tensor(past_step, is_past, row_step[:, :], ALU.mult))
                then(V.tensor_reduce(tile_ef[:, :], is_past, axis=AX_X, op=ALU.add))
                then(V.tensor_scalar(tile_ef[:, :], tile_ef[:, :], float(E - 1), None, ALU.min))
                then(V.tensor_reduce(tile_row[:, :], past_step, axis=AX_X, op=ALU.add))
                then(V.scalar_tensor_tensor(tile_row[:, :], tile_no[:, :], float(P), tile_row[:, :], ALU.mult, ALU.add))
                then(V.tensor_scalar(tile_row[:, :], tile_row[:, :], float(IDLE), float(h * HALF), ALU.min, ALU.add))
                assert n[0] == TABLE_STEPS * (h + 1), n[0]

            def table_out(h):
                at_least(dve, "table_mm", h + 1)
                for i, v in enumerate((tile_e, tile_at)):
                    V.tensor_copy(v[:, h * HTILES:(h + 1) * HTILES], table_bank(h, i)).then_inc(s["table_done"], 1)

            def tile(t, first=False, last=False, more=True):
                if not last:
                    halo(t + 1)
                if not first:
                    route(t - 1)
                clamp(t, range(0, 2))
                if not first:
                    pick(t - 1)
                softplus(t, range(0, 2))
                if not last:
                    conv(t + 1, range(0, 1))
                clamp(t, range(2, KI))
                softplus(t, range(2, KI))
                if not last:
                    conv(t + 1, range(1, 2))
                if not first:
                    shared_act(t - 1, 0)
                    if last:
                        table(0)
                    if not last:
                        choose(t - 1)
                layer_norm(t)
                if not first:
                    shared_act(t - 1, 1)
                    if last:
                        table_out(0)
                        choose(t - 1)
                    place(t - 1)
                if not last:
                    dt_low(t + 1)
                x1T_low(t)
                if not first:
                    residual(t - 1)

            dve.wait_ge(s["win_h"], 1)
            V.tensor_tensor(win_lo[:, :, :], win_f, f32(win_hi[:, :, :]), ALU.subtract).then_inc(s["win_l"], 1)
            V.memset(keep[:, :], 1.0).then_inc(s["keep_one"], 1)
            V.memset(xs[:, :, T:T + HALO], 0.0).then_inc(s["keep_one"], 1)
            dve.wait_ge(s["keep_one"], 2)
            for t in range(0, NT, seq_len // T):
                V.memset(keep[:, t:t + 1], 0.0).then_inc(s["keep_ready"], 1)
            V.memset(ones_f[:, :, :], 1.0).then_inc(s["pre_zero"], 1)
            V.memset(block_start[:, :, 1:E], 1.0).then_inc(s["pre_zero"], 1)
            V.memset(block_start[:, :, 0:1], 0.0).then_inc(s["pre_zero"], 1)
            for v in ends:
                V.memset(v[:, 0:8], 0.0).then_inc(s["pre_zero"], 1)
            dve.wait_ge(s["keep_ready"], N // seq_len)
            dve.wait_ge(s["consts_in"], 64)
            halo(0)
            conv(0, range(KI))
            dve.wait_ge(s["wdt_h"], 1)
            V.tensor_tensor(wdt_lo[:, :], wdt_f[0:R, :], f32(wdt_hi[0:R, :]), ALU.subtract).then_inc(s["wdt_l"], 1)
            dt_low(0)
            dve.wait_ge(s["gw_h"], 1)
            V.tensor_tensor(gw_lo, gw[:, :, :], f32(gw_hi), ALU.subtract).then_inc(s["gw_l"], 1)
            dve.wait_ge(s["wsgu_h"], 1)
            V.tensor_tensor(wsgu_lo[:, :, :], wsgu_f, f32(wsgu_hi[:, :, :]), ALU.subtract).then_inc(s["wsgu_l"], 1)
            dve.wait_ge(s["before_ready"], 1)
            dve.wait_ge(s["const_ready"], 5)
            dve.wait_ge(s["pre_zero"], 3 + len(ends))
            tile(0, first=True)
            tile(1)
            with dve.Fori(2, NT - 2) as t:
                tile(t)
            tile(NT - 2, more=False)
            tile(NT - 1, last=True, more=False)
            route(NT - 1)
            shared_act(NT - 1, 0)
            pick(NT - 1)
            choose(NT - 1, row_end)
            shared_act(NT - 1, 1)
            place(NT - 1, row_id_end)

            def tile_experts(q):
                return table_values(dve, tile_e, q, E - 1)

            def x_low(j, u, k):
                q, slot, turn, par = quad(j, u)
                at_least(dve, "t_h", KD * q + k + 1)
                V.tensor_tensor(t_lo[par][:, k, :], psum[:, 2 + k, :], f32(t_hi[par][:, k, :]), ALU.subtract) \
                 .then_inc(s["t_l"], 1)

            def weigh(j, u):
                q, slot, turn, par = quad(j, u)
                up = psum[:, 0:2, :].rearrange("p a (b i) -> p (a b) i", i=2 * I)
                experts = tile_experts(q)
                at_least(dve, "g_silu", q + 1)
                at_least(dve, "at_mm", q)
                for i, e in enumerate(experts):
                    V.scalar_tensor_tensor(e_act[:, i, :], g_act[:, i, :], tiles_in[:, slot, i, bass.ds(D + e, 1)],
                                           up[:, i, I:2 * I], ALU.mult, ALU.mult).then_inc(s["e_mul"], 1)
                return experts

            def result_rows(j, u, experts):
                q, slot, turn, par = quad(j, u)
                y_left(dve, j, u - RING)
                for i, e in enumerate(experts):
                    V.tensor_copy(y_id[slot][:, i:i + 1], tiles_in[:, slot, i, bass.ds(D + E + e, 1)]) \
                     .then_inc(s["y_id_done"], 1)

            def act_low(j, u):
                q, slot, turn, par = quad(j, u)
                at_least(dve, "a_h", q + 1)
                V.tensor_tensor(a_lo[:, :], psum[:, 4, :], f32(a_hi[:, :]), ALU.subtract).then_inc(s["a_l"], 1)

            def block_sum(g, i, u, n):
                x2 = res[:, bass.ds(SUB * g + i, 1), :].squeeze(1)
                y = y_in[u]
                if isinstance(g, int) and (g, i) in blocks_behind:
                    at_least(dve, f"y_in{u}", 16 * n)
                    V.tensor_tensor(y[:, 0:2, :], y[:, 0:2, :], y[:, 2:4, :], ALU.add).then_inc(s["y_paired_dve"], 1)
                    at_least(dve, "y_paired_dve", blocks_behind.index((g, i)) + 1)
                else:
                    at_least(dve, "y_paired", SUB * g + i + 1)
                V.tensor_tensor(y[:, 0, :], y[:, 0, :], y[:, 1, :], ALU.add).then_inc(s["y_summed"], 1)
                at_least(dve, "y_summed", SUB * g + i + 1)
                V.tensor_tensor(x2, x2, y[:, 0, :], ALU.add).then_inc(s[f"y_used{u}"], 1)
                at_least_alone(dve, f"y_used{u}", n)
                V.bn_stats(o_stats[:, bass.ds(SUB * g + i, 1), :].squeeze(1), x2).then_inc(s["o_bn"], 1)

            def norm(k):
                first, n = norm_blocks(k)
                steps = NORM_STEPS * k
                for i in range(n):
                    at_least(dve, "o_bn", first + i + 1)
                    V.bn_aggr(o_mv[:, i, :], o_stats[:, i, :]).then_inc(s["o_agg"], 1)
                at_least(dve, "o_agg", first + n)
                V.tensor_scalar(o_var[:, 0:n], o_mv[:, 0:n, 1], EPS, None, ALU.add).then_inc(s["o_norm"], 1)
                dve.wait_ge(s["o_norm"], steps + 1)
                if k >= 2:
                    at_least(dve, "o_done", sum(norm_blocks(k - 2)))
                rstd, shift = o_rstd[k % 2][:, 0:n], o_shift[k % 2][:, 0:n]
                inverse_root(o_var[:, 0:n], o_neg_half[:, 0:n], o_half_bits[:, 0:n], rstd, o_newton[:, 0:n],
                             "o_norm", steps + 1)
                V.scalar_tensor_tensor(shift, o_mv[:, 0:n, 0], -1.0, rstd, ALU.mult, ALU.mult) \
                 .then_inc(s["o_ready"], 1)

            def iteration(j, u):
                experts = weigh(j, u)
                if is_first(j, u):
                    table(1)
                if u + 2 < quads_left(j):
                    for k in range(KD):
                        x_low(j, u + 2, k)
                if is_first(j, u):
                    residual(NT - 1)
                act_low(j, u)
                result_rows(j, u, experts)
                if isinstance(j, int) and j == 0:
                    if u == RING - 1:
                        table_out(1)
                for g, i in block_beside(j, u):
                    block_sum(g, i, i, g + 1)

            def down_low(i):
                at_least(dve, "ew_hi", len(gu_parts) + i + 1)
                r = d_parts[i]
                V.tensor_tensor(ew_d_lo[:, r, :], raw_d[:, r, :], f32(ew_d_hi[:, r, :]), ALU.subtract) \
                 .then_inc(s["ew_d_low"], 1)

            down_low(0)
            for u in range(2):
                for k in range(KD):
                    x_low(0, u, k)
            down_low(1)
            each_quad(dve, iteration)

            for g, i in blocks_behind:
                block_sum(g, i, i, g + 1)
            norm(0)
            for g in range(HG, HALVES * HG):
                for i, (u, n) in enumerate(slots_of(g)):
                    at_least(dve, "o_ready", g - HG + 1)
                    if i % 2 == 0:
                        at_least(dve, f"y_used{u + 1}", n)
                    V.bn_stats(o_stats[:, i, :], sum_of(g, i)).then_inc(s["o_bn"], 1)
                norm(g - HG + 1)


_ORDER = ("x_tok x_T w_in_T conv_w conv_b w_x_T w_dt_T b_dt w_out_T gate_w_T gate_bias "
          "wg_T wu_T wd_T ws_g_T ws_u_T ws_d_T").split()


def kernel(L0_attn_x, L0_attn_W_in, L0_attn_conv_w, L0_attn_conv_b, L0_attn_W_x, L0_attn_W_dt, L0_attn_b_dt,
           L0_attn_W_out, L0_ffn_gate_w, L0_ffn_gate_bias, L0_ffn_Wg, L0_ffn_Wu, L0_ffn_Wd, L0_ffn_Ws_g,
           L0_ffn_Ws_u, L0_ffn_Ws_d):
    import numpy as np
    import concourse.bacc as bacc
    from concourse import mybir as mb
    from concourse.bass_utils import run_bass_kernel_spmd

    x = np.asarray(L0_attn_x)
    batch, seq, d = x.shape
    x = x.reshape(batch * seq, d)
    per_channel = lambda v: np.asarray(v).reshape(-1, 128).T
    laid = {
        "x_tok": x, "x_T": x.T,
        "w_in_T": np.asarray(L0_attn_W_in).T,
        "conv_w": np.asarray(L0_attn_conv_w).reshape(-1, 128, 4).transpose(1, 0, 2),
        "conv_b": per_channel(L0_attn_conv_b),
        "w_x_T": np.asarray(L0_attn_W_x).T,
        "w_dt_T": np.asarray(L0_attn_W_dt).T,
        "b_dt": per_channel(L0_attn_b_dt),
        "w_out_T": np.asarray(L0_attn_W_out).T,
        "gate_w_T": np.asarray(L0_ffn_gate_w).T,
        "gate_bias": np.asarray(L0_ffn_gate_bias).reshape(1, -1),
        "wg_T": np.asarray(L0_ffn_Wg).transpose(0, 2, 1),
        "wu_T": np.asarray(L0_ffn_Wu).transpose(0, 2, 1),
        "wd_T": np.asarray(L0_ffn_Wd).transpose(0, 2, 1),
        "ws_g_T": np.asarray(L0_ffn_Ws_g).T,
        "ws_u_T": np.asarray(L0_ffn_Ws_u).T,
        "ws_d_T": np.asarray(L0_ffn_Ws_d).T,
    }
    nc = bacc.Bacc("TRN2", target_bir_lowering=False, num_devices=1)
    arrays, args = {}, []
    for name in _ORDER:
        a = np.ascontiguousarray(laid[name])
        arrays[f"in_{name}"] = a
        args.append(nc.dram_tensor(f"in_{name}", a.shape, mb.dt.from_np(a.dtype), kind="ExternalInput").ap())
    out = nc.dram_tensor("out_dram", x.shape, mb.dt.from_np(x.dtype), kind="ExternalOutput").ap()
    mamba_moe(nc, *args, out, seq)
    got = run_bass_kernel_spmd(nc, [arrays], core_ids=[0]).results[0]["out_dram"]
    return got.reshape(batch, seq, d)
```
